# Optimizing a Trainium2 kernel written in Bass

```python
import numpy as np
import jax
import jax.numpy as jnp

def _softmax(x, axis=-1):
    return jax.nn.softmax(x, axis=axis)

def _gelu(x):
    return jax.nn.gelu(x, approximate=True)

def _silu(x):
    return jax.nn.silu(x)

def _sigmoid(x):
    return jax.nn.sigmoid(x)

def _layernorm(x, axis=-1, eps=1e-05):
    m = jnp.mean(x, axis=axis, keepdims=True)
    v = jnp.var(x, axis=axis, keepdims=True)
    return (x - m) / jnp.sqrt(v + eps)

def _scatter_add(tgt, idx, src, axis=0):
    return tgt.at[idx].add(src)

def _segment_sum(src, seg, n):
    return jax.ops.segment_sum(src, seg, n)
kernel_name = 'mk_cond_seq_d4_seqx_r8_c204e1'

def setup_inputs(seed: int=0):
    np.random.seed(seed)
    _w = jnp.asarray

    def _rec_inputs():
        import jax
        import jax.numpy as jnp
        _rk = jax.random.key(seed)
        x = -0.0002928 + 1 * jax.random.normal(jax.random.fold_in(_rk, 1), (128, 32, 128), jnp.float32)
        _lenS = 32 - jax.random.randint(jax.random.fold_in(_rk, 7), (128,), 0, max(1, 32 // 4) + 1, jnp.int32)
        _lenS2 = 32 - jax.random.randint(jax.random.fold_in(_rk, 8), (128,), 0, max(1, 32 // 4) + 1, jnp.int32)
        itok_B_6_14 = jax.random.randint(jax.random.fold_in(_rk, 11), (128,), 6, 15, jnp.int32)
        condB_theta = jax.random.uniform(jax.random.fold_in(_rk, 12), (128,), jnp.float32, 0.0, 0.983423)
        condB_phi = jax.random.uniform(jax.random.fold_in(_rk, 13), (128,), jnp.float32, 0.0, 0.961312)
        itok_B_34_63 = jax.random.randint(jax.random.fold_in(_rk, 15), (128,), 34, 64, jnp.int32)
        fside_Bx16xSxS_0 = -1.47943e-05 + 1.00017 * jax.random.normal(jax.random.fold_in(_rk, 16), (128, 16, 32, 32), jnp.float32)
        itok_B_0_15 = jax.random.randint(jax.random.fold_in(_rk, 17), (128,), 0, 16, jnp.int32)
        _validS = jnp.arange(32)[None, :] < _lenS[:, None]
        _validS2 = jnp.arange(32)[None, :] < _lenS2[:, None]
        _causal = jnp.tril(jnp.ones((32, 32), dtype=bool))
        mask_Bx1xSxS_bk0 = jnp.logical_not(jnp.broadcast_to(_validS[:, None, None, :], (128, 1, 32, 32)))
        return (x, itok_B_6_14, condB_theta, condB_phi, itok_B_34_63, fside_Bx16xSxS_0, itok_B_0_15, mask_Bx1xSxS_bk0)
    x, itok_B_6_14, condB_theta, condB_phi, itok_B_34_63, fside_Bx16xSxS_0, itok_B_0_15, mask_Bx1xSxS_bk0 = _rec_inputs()

    def _L0_cond_setup():
        import jax, jax.numpy as jnp
        import numpy as np
        D = 128
        E = 8
        FF = 512
        TOPK = 2
        S = 32
        SE = 64
        SH = 128
        B, T = (2, 256)

        def _forward(x, subject_ids, ln_g, ln_b, subj_emb, hyp_w1, hyp_b1, hyp_w2, hyp_b2, sty_w1, sty_b1, sty_w2, sty_b2, router_w, exp_w1, exp_b1, exp_w2, exp_b2):
            mu = x.mean(-1, keepdims=True)
            var = x.var(-1, keepdims=True)
            h = (x - mu) * jax.lax.rsqrt(var + 1e-05) * ln_g + ln_b
            m_t = h.mean(1, keepdims=True)
            v_t = h.var(1, keepdims=True)
            h_norm = (h - m_t) * jax.lax.rsqrt(v_t + 1e-08)
            se = subj_emb[subject_ids]
            hyp = jax.nn.relu(se @ hyp_w1 + hyp_b1) @ hyp_w2 + hyp_b2
            sty = jax.nn.relu(hyp @ sty_w1 + sty_b1) @ sty_w2 + sty_b2
            gamma, beta = jnp.split(sty, 2, axis=-1)
            gamma = jax.nn.softplus(gamma) + 1e-08
            h = h_norm * gamma[:, None, :] + beta[:, None, :]
            h_flat = h.reshape(-1, D)
            probs = jax.nn.softmax(h_flat @ router_w, axis=-1)
            gates, idx = jax.lax.top_k(probs, TOPK)
            gates = gates / gates.sum(-1, keepdims=True)
            N = h_flat.shape[0]
            combine = jnp.zeros((N, E), h_flat.dtype).at[jnp.arange(N)[:, None], idx].add(gates)
            hid = jax.nn.relu(jnp.einsum('nd,edf->nef', h_flat, exp_w1) + exp_b1)
            eout = jnp.einsum('nef,efd->ned', hid, exp_w2) + exp_b2
            y = jnp.einsum('ned,ne->nd', eout, combine)
            return x + y.reshape(x.shape)
        key = jax.random.key(seed)
        ks = jax.random.split(key, 16)
        n = lambda k, sh, s=0.02: jax.random.normal(k, sh, dtype=jnp.float32) * s
        return {'x': jax.random.normal(ks[0], (B, T, D), dtype=jnp.float32), 'subject_ids': jax.random.randint(ks[1], (B,), 0, S), 'ln_g': jnp.ones((D,), jnp.float32), 'ln_b': jnp.zeros((D,), jnp.float32), 'subj_emb': n(ks[2], (S, SE)), 'hyp_w1': n(ks[3], (SE, SH), 1.0 / np.sqrt(SE)), 'hyp_b1': jnp.zeros((SH,), jnp.float32), 'hyp_w2': n(ks[4], (SH, SH), 1.0 / np.sqrt(SH)), 'hyp_b2': jnp.zeros((SH,), jnp.float32), 'sty_w1': n(ks[5], (SH, SH // 2), 1.0 / np.sqrt(SH)), 'sty_b1': jnp.zeros((SH // 2,), jnp.float32), 'sty_w2': n(ks[6], (SH // 2, 2 * D), 1.0 / np.sqrt(SH // 2)), 'sty_b2': jnp.zeros((2 * D,), jnp.float32), 'router_w': n(ks[7], (D, E), 1.0 / np.sqrt(D)), 'exp_w1': n(ks[8], (E, D, FF), 1.0 / np.sqrt(D)), 'exp_b1': jnp.zeros((E, FF), jnp.float32), 'exp_w2': n(ks[9], (E, FF, D), 1.0 / np.sqrt(FF)), 'exp_b2': jnp.zeros((E, D), jnp.float32)}
    _L0_cond_all = _L0_cond_setup()
    _L0_cond_in = {k: v for k, v in _L0_cond_all.items() if k in ('ln_g', 'ln_b', 'subj_emb', 'hyp_w1', 'hyp_b1', 'hyp_w2', 'hyp_b2', 'sty_w1', 'sty_b1', 'sty_w2', 'sty_b2', 'router_w', 'exp_w1', 'exp_b1', 'exp_w2', 'exp_b2')}
    del _L0_cond_all

    def _L1_cond_setup():
        import jax, jax.numpy as jnp
        import numpy as np
        key = jax.random.key(seed)
        k1, k2, k3 = jax.random.split(key, 3)
        B, N, D = (16, 512, 128)
        embeddings = jax.random.normal(k1, (B, N, D), dtype=jnp.float32)
        theta = jax.random.uniform(k2, (B,), dtype=jnp.float32)
        phi = jax.random.uniform(k3, (B,), dtype=jnp.float32)
        return {'embeddings': embeddings, 'theta': theta, 'phi': phi}
    _L1_cond_all = _L1_cond_setup()
    _L1_cond_in = {k: v for k, v in _L1_cond_all.items() if k in ()}
    del _L1_cond_all

    def _L2_cond_setup():
        import jax, jax.numpy as jnp
        import numpy as np
        import math
        D_MODEL = 128
        N_HEAD = 16
        HEAD_DIM = D_MODEL // N_HEAD
        D_FF = 512
        NUM_STEPS = 100.0
        RESCALE = 4000.0
        EPS = 1e-05

        def _sin_emb(t):
            half = D_MODEL // 2
            x = t.astype(jnp.float32) / NUM_STEPS * RESCALE
            freqs = jnp.exp(jnp.arange(half, dtype=jnp.float32) * (-math.log(10000.0) / (half - 1)))
            e = x[:, None] * freqs[None, :]
            return jnp.concatenate([jnp.sin(e), jnp.cos(e)], axis=-1)

        def _ln(x):
            m = jnp.mean(x, axis=-1, keepdims=True)
            v = jnp.var(x, axis=-1, keepdims=True)
            return (x - m) / jnp.sqrt(v + EPS)

        def _gelu2(x):
            return x * jax.nn.sigmoid(1.702 * x)
        key = jax.random.key(seed)
        ks = jax.random.split(key, 24)
        B, S, D, F = (4, 64, D_MODEL, D_FF)
        std = 0.02
        inp = {'src': jax.random.normal(ks[0], (B, S, D), dtype=jnp.float32), 'src_mask': jax.random.randint(ks[1], (B, 1, S, S), 0, 2).astype(bool), 'timestep': jax.random.randint(ks[2], (B,), 0, 100, dtype=jnp.int32), 'attention_bias': jax.random.normal(ks[3], (B, N_HEAD, S, S), dtype=jnp.float32), 'W_ada': jax.random.normal(ks[4], (D, 2 * D), dtype=jnp.float32) * std, 'b_ada': jnp.zeros((2 * D,), dtype=jnp.float32), 'Wq': jax.random.normal(ks[5], (D, D), dtype=jnp.float32) * std, 'bq': jnp.zeros((D,), dtype=jnp.float32), 'Wk': jax.random.normal(ks[6], (D, D), dtype=jnp.float32) * std, 'bk': jnp.zeros((D,), dtype=jnp.float32), 'Wv': jax.random.normal(ks[7], (D, D), dtype=jnp.float32) * std, 'bv': jnp.zeros((D,), dtype=jnp.float32), 'Wo': jax.random.normal(ks[8], (D, D), dtype=jnp.float32) * std, 'bo': jnp.zeros((D,), dtype=jnp.float32), 'W1': jax.random.normal(ks[9], (D, F), dtype=jnp.float32) * std, 'b1': jnp.zeros((F,), dtype=jnp.float32), 'W2': jax.random.normal(ks[10], (F, D), dtype=jnp.float32) * std, 'b2': jnp.zeros((D,), dtype=jnp.float32), 'g2': jnp.ones((D,), dtype=jnp.float32), 'beta2': jnp.zeros((D,), dtype=jnp.float32)}
        return inp
    _L2_cond_all = _L2_cond_setup()
    _L2_cond_in = {k: v for k, v in _L2_cond_all.items() if k in ('W_ada', 'b_ada', 'Wq', 'bq', 'Wk', 'bk', 'Wv', 'bv', 'Wo', 'bo', 'W1', 'b1', 'W2', 'b2', 'g2', 'beta2')}
    del _L2_cond_all

    def _L3_cond_setup():
        import jax, jax.numpy as jnp
        import numpy as np
        B, S, D = (32, 128, 128)
        A = 32
        E = 16
        LN_EPS = 1e-05
        key = jax.random.key(seed)
        ks = jax.random.split(key, 10)
        s = lambda fan_in: 1.0 / np.sqrt(fan_in)
        return {'hidden_states': jax.random.normal(ks[0], (B, S, D), dtype=jnp.float32), 'domain_id': jax.random.randint(ks[1], (B,), 0, E, dtype=jnp.int64), 'down_W': jax.random.uniform(ks[2], (A, D), jnp.float32, -s(D), s(D)), 'down_b': jax.random.uniform(ks[3], (A,), jnp.float32, -s(D), s(D)), 'up_W': jax.random.uniform(ks[4], (D, A), jnp.float32, -s(A), s(A)), 'up_b': jax.random.uniform(ks[5], (D,), jnp.float32, -s(A), s(A)), 'expert_W': jax.random.uniform(ks[6], (E, A, A), jnp.float32, -s(A), s(A)), 'expert_b': jax.random.uniform(ks[7], (E, A), jnp.float32, -s(A), s(A)), 'domain_emb': jax.random.normal(ks[8], (E, A), dtype=jnp.float32), 'ln_gamma': jnp.ones((D,), jnp.float32), 'ln_beta': jnp.zeros((D,), jnp.float32)}
    _L3_cond_all = _L3_cond_setup()
    _L3_cond_in = {k: v for k, v in _L3_cond_all.items() if k in ('down_W', 'down_b', 'up_W', 'up_b', 'expert_W', 'expert_b', 'domain_emb', 'ln_gamma', 'ln_beta')}
    del _L3_cond_all
    return {'x': x, 'itok_B_6_14': itok_B_6_14, 'condB_theta': condB_theta, 'condB_phi': condB_phi, 'itok_B_34_63': itok_B_34_63, 'fside_Bx16xSxS_0': fside_Bx16xSxS_0, 'itok_B_0_15': itok_B_0_15, 'mask_Bx1xSxS_bk0': mask_Bx1xSxS_bk0, 'L0_cond_ln_g': _L0_cond_in['ln_g'], 'L0_cond_ln_b': _L0_cond_in['ln_b'], 'L0_cond_subj_emb': _L0_cond_in['subj_emb'], 'L0_cond_hyp_w1': _L0_cond_in['hyp_w1'], 'L0_cond_hyp_b1': _L0_cond_in['hyp_b1'], 'L0_cond_hyp_w2': _L0_cond_in['hyp_w2'], 'L0_cond_hyp_b2': _L0_cond_in['hyp_b2'], 'L0_cond_sty_w1': _L0_cond_in['sty_w1'], 'L0_cond_sty_b1': _L0_cond_in['sty_b1'], 'L0_cond_sty_w2': _L0_cond_in['sty_w2'], 'L0_cond_sty_b2': _L0_cond_in['sty_b2'], 'L0_cond_router_w': _L0_cond_in['router_w'], 'L0_cond_exp_w1': _L0_cond_in['exp_w1'], 'L0_cond_exp_b1': _L0_cond_in['exp_b1'], 'L0_cond_exp_w2': _L0_cond_in['exp_w2'], 'L0_cond_exp_b2': _L0_cond_in['exp_b2'], 'L2_cond_W_ada': _L2_cond_in['W_ada'], 'L2_cond_b_ada': _L2_cond_in['b_ada'], 'L2_cond_Wq': _L2_cond_in['Wq'], 'L2_cond_bq': _L2_cond_in['bq'], 'L2_cond_Wk': _L2_cond_in['Wk'], 'L2_cond_bk': _L2_cond_in['bk'], 'L2_cond_Wv': _L2_cond_in['Wv'], 'L2_cond_bv': _L2_cond_in['bv'], 'L2_cond_Wo': _L2_cond_in['Wo'], 'L2_cond_bo': _L2_cond_in['bo'], 'L2_cond_W1': _L2_cond_in['W1'], 'L2_cond_b1': _L2_cond_in['b1'], 'L2_cond_W2': _L2_cond_in['W2'], 'L2_cond_b2': _L2_cond_in['b2'], 'L2_cond_g2': _L2_cond_in['g2'], 'L2_cond_beta2': _L2_cond_in['beta2'], 'L3_cond_down_W': _L3_cond_in['down_W'], 'L3_cond_down_b': _L3_cond_in['down_b'], 'L3_cond_up_W': _L3_cond_in['up_W'], 'L3_cond_up_b': _L3_cond_in['up_b'], 'L3_cond_expert_W': _L3_cond_in['expert_W'], 'L3_cond_expert_b': _L3_cond_in['expert_b'], 'L3_cond_domain_emb': _L3_cond_in['domain_emb'], 'L3_cond_ln_gamma': _L3_cond_in['ln_gamma'], 'L3_cond_ln_beta': _L3_cond_in['ln_beta']}

def reference(x, itok_B_6_14, condB_theta, condB_phi, itok_B_34_63, fside_Bx16xSxS_0, itok_B_0_15, mask_Bx1xSxS_bk0, L0_cond_ln_g, L0_cond_ln_b, L0_cond_subj_emb, L0_cond_hyp_w1, L0_cond_hyp_b1, L0_cond_hyp_w2, L0_cond_hyp_b2, L0_cond_sty_w1, L0_cond_sty_b1, L0_cond_sty_w2, L0_cond_sty_b2, L0_cond_router_w, L0_cond_exp_w1, L0_cond_exp_b1, L0_cond_exp_w2, L0_cond_exp_b2, L2_cond_W_ada, L2_cond_b_ada, L2_cond_Wq, L2_cond_bq, L2_cond_Wk, L2_cond_bk, L2_cond_Wv, L2_cond_bv, L2_cond_Wo, L2_cond_bo, L2_cond_W1, L2_cond_b1, L2_cond_W2, L2_cond_b2, L2_cond_g2, L2_cond_beta2, L3_cond_down_W, L3_cond_down_b, L3_cond_up_W, L3_cond_up_b, L3_cond_expert_W, L3_cond_expert_b, L3_cond_domain_emb, L3_cond_ln_gamma, L3_cond_ln_beta):
    import jax
    import jax.numpy as jnp

    def _L0_cond_ref(x, subject_ids, ln_g, ln_b, subj_emb, hyp_w1, hyp_b1, hyp_w2, hyp_b2, sty_w1, sty_b1, sty_w2, sty_b2, router_w, exp_w1, exp_b1, exp_w2, exp_b2):
        import jax, jax.numpy as jnp
        import numpy as np
        D = 128
        E = 8
        FF = 512
        TOPK = 2
        S = 32
        SE = 64
        SH = 128
        B, T = (2, 256)

        def _forward(x, subject_ids, ln_g, ln_b, subj_emb, hyp_w1, hyp_b1, hyp_w2, hyp_b2, sty_w1, sty_b1, sty_w2, sty_b2, router_w, exp_w1, exp_b1, exp_w2, exp_b2):
            mu = x.mean(-1, keepdims=True)
            var = x.var(-1, keepdims=True)
            h = (x - mu) * jax.lax.rsqrt(var + 1e-05) * ln_g + ln_b
            m_t = h.mean(1, keepdims=True)
            v_t = h.var(1, keepdims=True)
            h_norm = (h - m_t) * jax.lax.rsqrt(v_t + 1e-08)
            se = subj_emb[subject_ids]
            hyp = jax.nn.relu(se @ hyp_w1 + hyp_b1) @ hyp_w2 + hyp_b2
            sty = jax.nn.relu(hyp @ sty_w1 + sty_b1) @ sty_w2 + sty_b2
            gamma, beta = jnp.split(sty, 2, axis=-1)
            gamma = jax.nn.softplus(gamma) + 1e-08
            h = h_norm * gamma[:, None, :] + beta[:, None, :]
            h_flat = h.reshape(-1, D)
            probs = jax.nn.softmax(h_flat @ router_w, axis=-1)
            gates, idx = jax.lax.top_k(probs, TOPK)
            gates = gates / gates.sum(-1, keepdims=True)
            N = h_flat.shape[0]
            combine = jnp.zeros((N, E), h_flat.dtype).at[jnp.arange(N)[:, None], idx].add(gates)
            hid = jax.nn.relu(jnp.einsum('nd,edf->nef', h_flat, exp_w1) + exp_b1)
            eout = jnp.einsum('nef,efd->ned', hid, exp_w2) + exp_b2
            y = jnp.einsum('ned,ne->nd', eout, combine)
            return x + y.reshape(x.shape)
        return _forward(x, subject_ids, ln_g, ln_b, subj_emb, hyp_w1, hyp_b1, hyp_w2, hyp_b2, sty_w1, sty_b1, sty_w2, sty_b2, router_w, exp_w1, exp_b1, exp_w2, exp_b2)

    def _L1_cond_ref(embeddings, theta, phi):
        import jax, jax.numpy as jnp
        import numpy as np
        B, N, D = embeddings.shape
        e = embeddings.reshape(B, N, D // 4, 4)
        ct = jnp.cos(theta)[:, None, None]
        st = jnp.sin(theta)[:, None, None]
        cp = jnp.cos(phi)[:, None, None]
        sp = jnp.sin(phi)[:, None, None]
        x0, x1, x2, x3 = (e[..., 0], e[..., 1], e[..., 2], e[..., 3])
        out = jnp.stack([x0 * ct + x1 * st, -x0 * st + x1 * ct, x2 * cp + x3 * sp, -x2 * sp + x3 * cp], axis=-1)
        return out.reshape(B, N, D)

    def _L2_cond_ref(src, src_mask, timestep, attention_bias, W_ada, b_ada, Wq, bq, Wk, bk, Wv, bv, Wo, bo, W1, b1, W2, b2, g2, beta2):
        import jax, jax.numpy as jnp
        import numpy as np
        import math
        D_MODEL = 128
        N_HEAD = 16
        HEAD_DIM = D_MODEL // N_HEAD
        D_FF = 512
        NUM_STEPS = 100.0
        RESCALE = 4000.0
        EPS = 1e-05

        def _sin_emb(t):
            half = D_MODEL // 2
            x = t.astype(jnp.float32) / NUM_STEPS * RESCALE
            freqs = jnp.exp(jnp.arange(half, dtype=jnp.float32) * (-math.log(10000.0) / (half - 1)))
            e = x[:, None] * freqs[None, :]
            return jnp.concatenate([jnp.sin(e), jnp.cos(e)], axis=-1)

        def _ln(x):
            m = jnp.mean(x, axis=-1, keepdims=True)
            v = jnp.var(x, axis=-1, keepdims=True)
            return (x - m) / jnp.sqrt(v + EPS)

        def _gelu2(x):
            return x * jax.nn.sigmoid(1.702 * x)
        B, S, D = src.shape
        emb = jax.nn.silu(_sin_emb(timestep)) @ W_ada + b_ada
        scale, shift = jnp.split(emb[:, None, :], 2, axis=-1)
        x = _ln(src) * (1.0 + scale) + shift
        q = (x @ Wq + bq).reshape(B, S, N_HEAD, HEAD_DIM).transpose(0, 2, 1, 3)
        k = (x @ Wk + bk).reshape(B, S, N_HEAD, HEAD_DIM).transpose(0, 2, 1, 3)
        v = (x @ Wv + bv).reshape(B, S, N_HEAD, HEAD_DIM).transpose(0, 2, 1, 3)
        scores = jnp.einsum('bhqd,bhkd->bhqk', q / math.sqrt(HEAD_DIM), k)
        scores = scores + attention_bias
        scores = jnp.where(src_mask, -jnp.inf, scores.astype(jnp.float32))
        probs = jax.nn.softmax(scores, axis=-1).astype(v.dtype)
        ctx = jnp.einsum('bhqk,bhkd->bhqd', probs, v)
        ctx = ctx.transpose(0, 2, 1, 3).reshape(B, S, D)
        x = x + (ctx @ Wo + bo)
        h = _ln(x) * g2 + beta2
        ff = _gelu2(h @ W1 + b1) @ W2 + b2
        return x + ff

    def _L3_cond_ref(hidden_states, domain_id, down_W, down_b, up_W, up_b, expert_W, expert_b, domain_emb, ln_gamma, ln_beta):
        import jax, jax.numpy as jnp
        import numpy as np
        B, S, D = (32, 128, 128)
        A = 32
        E = 16
        LN_EPS = 1e-05
        residual = hidden_states
        hidden = jnp.einsum('bsd,ad->bsa', hidden_states, down_W) + down_b
        hidden = jax.nn.gelu(hidden, approximate=False)
        valid = (domain_id >= 0) & (domain_id < E)
        idx = jnp.clip(domain_id, 0, E - 1)
        Wsel = expert_W[idx]
        bsel = expert_b[idx]
        expert_out = jnp.einsum('bsa,boa->bso', hidden, Wsel) + bsel[:, None, :]
        domain_output = jnp.where(valid[:, None, None], expert_out, hidden)
        hidden = domain_output + domain_emb[idx][:, None, :]
        hidden = jnp.einsum('bsa,da->bsd', hidden, up_W) + up_b
        x = hidden + residual
        mu = jnp.mean(x, axis=-1, keepdims=True)
        var = jnp.mean(jnp.square(x - mu), axis=-1, keepdims=True)
        return (x - mu) * jax.lax.rsqrt(var + LN_EPS) * ln_gamma + ln_beta
    x = _L0_cond_ref(x, itok_B_6_14, L0_cond_ln_g, L0_cond_ln_b, L0_cond_subj_emb, L0_cond_hyp_w1, L0_cond_hyp_b1, L0_cond_hyp_w2, L0_cond_hyp_b2, L0_cond_sty_w1, L0_cond_sty_b1, L0_cond_sty_w2, L0_cond_sty_b2, L0_cond_router_w, L0_cond_exp_w1, L0_cond_exp_b1, L0_cond_exp_w2, L0_cond_exp_b2)
    x = _L1_cond_ref(x, condB_theta, condB_phi)
    x = _L2_cond_ref(x, mask_Bx1xSxS_bk0, itok_B_34_63, fside_Bx16xSxS_0, L2_cond_W_ada, L2_cond_b_ada, L2_cond_Wq, L2_cond_bq, L2_cond_Wk, L2_cond_bk, L2_cond_Wv, L2_cond_bv, L2_cond_Wo, L2_cond_bo, L2_cond_W1, L2_cond_b1, L2_cond_W2, L2_cond_b2, L2_cond_g2, L2_cond_beta2)
    x = _L3_cond_ref(x, itok_B_0_15, L3_cond_down_W, L3_cond_down_b, L3_cond_up_W, L3_cond_up_b, L3_cond_expert_W, L3_cond_expert_b, L3_cond_domain_emb, L3_cond_ln_gamma, L3_cond_ln_beta)
    return x

_drawn_inputs = setup_inputs


def setup_inputs(seed=0):
    import zlib

    import numpy as np

    out = dict(_drawn_inputs(seed))
    spreads = {'L0_cond_ln_g': (1.0, 0.6),
     'L0_cond_ln_b': (0.0, 0.8),
     'L0_cond_hyp_b1': (0.0, 0.1),
     'L0_cond_hyp_b2': (0.0, 0.1),
     'L0_cond_sty_b1': (0.0, 0.1),
     'L0_cond_sty_b2': (0.0, 0.1),
     'L0_cond_exp_b1': (0.0, 0.1),
     'L0_cond_exp_b2': (0.0, 0.1),
     'L2_cond_b_ada': (0.0, 0.1),
     'L2_cond_bq': (0.0, 0.8),
     'L2_cond_bk': (0.0, 0.8),
     'L2_cond_bv': (0.0, 0.492),
     'L2_cond_bo': (0.0, 0.1),
     'L2_cond_b1': (0.0, 0.372),
     'L2_cond_b2': (0.0, 0.1),
     'L2_cond_g2': (1.0, 0.6),
     'L2_cond_beta2': (0.0, 0.8),
     'L3_cond_ln_gamma': (1.0, 0.2),
     'L3_cond_ln_beta': (0.0, 0.1)}
    factors = {'fside_Bx16xSxS_0': 6.116,
     'L2_cond_Wq': 8.0,
     'L2_cond_Wk': 8.0,
     'L2_cond_Wv': 3.966,
     'L3_cond_down_b': 5.956}
    for name, (base, spread) in spreads.items():
        noise = np.random.default_rng([zlib.crc32(name.encode()), seed]).standard_normal(out[name].shape)
        drawn = base * np.exp(spread * noise) if base else spread * noise
        out[name] = jnp.asarray(drawn.astype(out[name].dtype))
    for name, factor in factors.items():
        out[name] = (out[name] * factor).astype(out[name].dtype)
    return out
```

```python
from contextlib import ExitStack

import concourse.bass as bass
from concourse import mybir

F32 = mybir.dt.float32
I32 = mybir.dt.int32
U32 = mybir.dt.uint32
U8 = mybir.dt.uint8
ALU = mybir.AluOpType
ACT = mybir.ActivationFunctionType
AX = mybir.AxisListType

P = 128
PI = 3.14159265358979
TWO_PI_HI = 6.28125
TWO_PI_LO = 2 * PI - TWO_PI_HI
ROUND = 12582912.0
MASKED = -1.0e30


class Signal:

    def __init__(self, sem, per, lead):
        self.sem, self.per, self.lead = sem, per, lead

    def open(self, eng):
        eng.sem_inc(self.sem, self.lead)

    def upto(self, g, k=None):
        return g * self.per + (self.per if k is None else k) + self.lead


def build(nc, a, out):
    B, S, D = a["x"].shape
    NT = B * S // P
    BT = P // S
    GT = 4
    NG = NT // GT
    GB = GT * BT
    GN = GT * P
    H = 16
    HD = D // H
    NE, _, FF = a["L0_cond_exp_w1"].shape
    FC = FF // P
    HJ = 4
    HP = H // HJ
    GV = HP * HD + HP
    NX, A, _ = a["L3_cond_expert_W"].shape
    SE = a["L0_cond_subj_emb"].shape[1]
    NS = a["L0_cond_subj_emb"].shape[0]
    SQ = a["L0_cond_sty_w1"].shape[1]

    wud = nc.dram_tensor("expert_up_rows", [(NX + 1) * A, D], F32, kind="Internal").ap()

    with ExitStack() as ctx:
        def sb(name, shape, dt=F32):
            return ctx.enter_context(nc.sbuf_tensor(name, shape, dt))

        def sem(name):
            return ctx.enter_context(nc.semaphore(name))

        def signal(name, per=1, lead=0):
            return Signal(sem(name), per, lead)

        X = sb("X", [P, NT, D])
        HT = sb("HT", [P, NT * P])
        BIAS = sb("BIAS", [P, NT, H, S])
        EXP = sb("EXP", [P, 2 * NE * FF])
        W1E = EXP[:, 0:NE * FF].rearrange("p (e f) -> p e f", e=NE)
        W2E = EXP[:, NE * FF:2 * NE * FF].rearrange("p (e c d) -> p e c d", e=NE, c=FC)
        hid = sb("hid", [P, 2, FC, GN])
        lent = [0]

        def setup(shape, dt=F32):
            n = 1
            for d in shape[1:]:
                n *= d
            lent[0] += n
            assert lent[0] <= FC * GN
            ap = hid[0:shape[0], 1, :, :].rearrange("p c n -> p (c n)")[:, lent[0] - n:lent[0]]
            return ap if dt is F32 else ap.bitcast(dt)

        used = [0]

        def part(n):
            lo = used[0] if used[0] + n <= 2 * NE * FF or used[0] >= 2 * NE * FF else 2 * NE * FF
            used[0] = lo + n
            if lo < 2 * NE * FF:
                return EXP[:, lo:lo + n]
            lo -= 2 * NE * FF
            assert lo + n <= NT * P
            return HT[:, lo:lo + n]

        B1E = sb("B1E", [P, NE, FC])
        ident = sb("ident", [P, P])
        ln_gb = sb("ln_gb", [P, 2])
        ids = setup([P, B], I32); ids2 = setup([P, B], I32); ids3 = setup([NX + 2, B], I32)
        idf = setup([P, B])
        embw = setup([NS, SE])
        hypw1 = setup([SE, P]); hypw2 = setup([P, P])
        styw1 = setup([P, SQ]); styw2 = setup([SQ, 2 * D])
        hb = sb("hb", [P, 5])
        wada = setup([P, 2 * D]); bada = sb("bada", [P, 2])
        rw = sb("rw", [P, NE])
        b2bd = sb("b2bd", [P, GT, D])
        fq = sb("fq", [P, 1]); ph = sb("ph", [P, 2])
        wq = sb("wq", [P, D]); wk = sb("wk", [P, D]); wv = sb("wv", [P, D]); wo = sb("wo", [P, D])
        w1 = sb("w1", [P, FF]); w2 = sb("w2", [P, FC, D]); b1 = sb("b1", [P, FC])
        cols = sb("cols", [P, 6])
        bqs = sb("bqs", [P, 1]); bkm = sb("bkm", [P, HP])
        rows = sb("rows", [P, 4, D])
        maskb = sb("maskb", [P, NT, S], U8); ot = sb("ot", [P, 2, GT, D])
        maskn = ot[:, :, :, :].rearrange("p a t d -> p (a t d)").rearrange("p (t k) -> p t k", k=S)
        hm16 = sb("hm16", [P, H]); hm4 = sb("hm4", [P, HP]); vm = sb("vm", [P, BT, HJ, HP])
        e4 = sb("e4", [BT, P]); ang = sb("ang", [BT, 2, NT]); tr = sb("tr", [BT, 4, NT]); trk = sb("trk", [BT, 4, NT])
        C4 = sb("C4", [P, NT, 4]); S4 = sb("S4", [P, NT, 4])
        iot = sb("iot", [P, 1], I32); iof = sb("iof", [P, 1]); acol = sb("acol", [P, 1], I32); acf = sb("acf", [P, 1])
        half = sb("half", [P, GB])
        desc = sb("desc", [P, NE], I32); dsf = sb("dsf", [P, NE])
        onehot = setup([NS, B])
        sA = setup([P, B]); sB = setup([P, B]); sC = setup([P, B]); sD = setup([P, B])
        gammaT = sb("gammaT", [P, B]); betaT = sb("betaT", [P, B])
        scaleT = sb("scaleT", [P, B]); shiftT = sb("shiftT", [P, B])
        doww = sb("doww", [A, D]); dwT = sb("dwT", [P, 4, A]); upw = sb("upw", [P, A]); upT = sb("upT", [A, D])
        exw = sb("exw", [A, NX, A]); wus = sb("wus", [P, NX // 4, D]); vecs = sb("vecs", [A, NX + 2]); emt = sb("emt", [A, NX])
        upb = sb("upb", [NX + 2, D]); CT = sb("CT", [NX + 2, D]); ohC = sb("ohC", [NX + 2, B])
        dom4 = sb("dom4", [BT, NT], I32); dom4f = sb("dom4f", [BT, NT]); domx = sb("domx", [P, NT]); domy = sb("domy", [P, NT])
        widx = sb("widx", [P, NT], U32)
        WSEL = sb("WSEL", [P, NT, D])
        hBD = sb("hBD", [P, 1, GT, P])
        comb = sb("comb", [P, NT, NE]); combT = sb("combT", [P, 2, P])
        g1 = sb("g1", [P, NT]); g2 = sb("g2", [P, NT]); m1 = sb("m1", [P, NT]); m2 = sb("m2", [P, NT]); mw = sb("mw", [P, NT])
        st = sb("st", [P, GT, 6]); mv = sb("mv", [P, GT, 2]); ve = sb("ve", [P, GT]); rstd = sb("rstd", [P, GT])
        xn = sb("xn", [P, GT, D]); xn2 = part(GT * D).rearrange("p (t d) -> p t d", d=D)
        st2, st3 = (sb(f"st{k}", [P, GT, 6]) for k in (2, 3))
        mv2, mv3 = (sb(f"mv{k}", [P, GT, 2]) for k in (2, 3))
        ve2, ve3, rstd2, rstd3 = (sb(f"{n}", [P, GT]) for n in ("ve2", "ve3", "rstd2", "rstd3"))
        big = sb("big", [P, 2, GN]); hTw = sb("hTw", [P, 1, GN])
        vs = sb("vs", [P, 4, GB])
        Lg, ta, tb, tc_ = (hid[:, 0, k, 0:NT * NE].rearrange("p (t e) -> p t e", e=NE) for k in range(4))
        xmT = part(2 * GN).rearrange("p (c n) -> p c n", c=2); QT = part(GN); KM = part(GB * HP * S).rearrange("p (b h k) -> p b h k", h=HP, k=S)
        Sc = part(2 * H * S).rearrange("p (c h k) -> p c h k", c=2, h=H)
        PT = part(HJ * P).rearrange("p (j q) -> p j q", j=HJ)
        VB = part(2 * BT * HJ * GV).rearrange("p (c b j v) -> p c b j v", c=2, b=BT, j=HJ)
        wv4 = sb("wv4", [P, HP, HJ, HP, HD])
        Cn = part(GT * D).rearrange("p (t d) -> p t d", d=D)
        mx = sb("mx", [P, 2, H]); rs = sb("rs", [P, HJ, HP])
        ctxT = part(GN)
        x2, x2b, X3, z = (part(GT * D).rearrange("p (t d) -> p t d", d=D) for _ in range(4))
        h2T = part(GN); X3T = part(GN)
        ohx = sb("ohx", [NX + 2, GT, P])

        PS = ctx.enter_context(nc.psum_tensor("PS", [P, 4, 512], F32))
        W = [ctx.enter_context(nc.psum_tensor(f"W{i}", [P, 512], F32)) for i in range(4)]

        ld_small = sem("ld_small"); ld_x = sem("ld_x"); ld_exp = sem("ld_exp"); ld_bias = sem("ld_bias"); ld_mask = sem("ld_mask")
        ld_b2 = sem("ld_b2"); st_wu = sem("st_wu"); ld_wsel = sem("ld_wsel"); out_done = [sem(f"out_done{i}") for i in range(2)]
        pool_set = sem("pool_set"); dve_set = sem("dve_set"); act_set = sem("act_set"); pe_set = sem("pe_set")
        b2_zero = sem("b2_zero")
        bias_masked = signal("bias_masked", GT)
        a_st = signal("a_st", 2 * GT + 1); a_rstd = signal("a_rstd"); a_xn = signal("a_xn", GT); a_T = signal("a_T", lead=1)
        a_h = signal("a_h", lead=1); a_dve = signal("a_dve", 7); a_sq = signal("a_sq"); a_rv = signal("a_rv"); a_fin = signal("a_fin")
        a_lg = signal("a_lg", lead=1)
        top = sem("top"); top_act = sem("top_act"); combined = sem("combined"); cT_ps = sem("cT_ps"); cT_sb = sem("cT_sb")
        bb_ps = sem("bb_ps"); bb_add = sem("bb_add")
        e_h = signal("e_h", NE * FC); e_relu = signal("e_relu", NE * FC, lead=1); e_y = signal("e_y", NE, lead=1); e_acc = signal("e_acc", NE, lead=1)
        r_mul = signal("r_mul", GT); r_swp = signal("r_swp", GT); r_x = signal("r_x", GT, lead=1)
        c_st = signal("c_st", 2 * GT + 1); c_rstd = signal("c_rstd"); c_xn = signal("c_xn", GT); c_xmul = signal("c_xmul")
        c_xm = signal("c_xm"); c_q = signal("c_q"); c_qk = signal("c_qk", GT); c_sc = signal("c_sc", GT, lead=1); c_mx = signal("c_mx", GT)
        c_sub = signal("c_sub", GT); c_exp = signal("c_exp", GT); c_rs = signal("c_rs", GT); c_cn = signal("c_cn", GT)
        c_pv = signal("c_pv", GT); c_v = signal("c_v", GT); c_pT = signal("c_pT", GT)
        d_cT = signal("d_cT"); d_o = signal("d_o"); d_x2 = signal("d_x2"); d_x2b = signal("d_x2b")
        d_st = signal("d_st", 2 * GT + 1); d_rstd = signal("d_rstd"); d_xn = signal("d_xn", GT); d_f = signal("d_f", FC)
        d_y = signal("d_y"); f_x3 = signal("f_x3"); f_oh = signal("f_oh"); f_u = signal("f_u", lead=1); f_z = signal("f_z")
        t1 = signal("t1"); t2 = signal("t2"); t3 = signal("t3"); qp = signal("qp"); kp = signal("kp"); dp = signal("dp")
        o_st = signal("o_st", 2 * GT + 1); o_rstd = signal("o_rstd"); o_zn = signal("o_zn", GT); o_g = signal("o_g")
        o_b = signal("o_b", lead=1)
        vb_ones = sem("vb_ones")

        bank_read = [sem(f"bank_read{b}") for b in range(4)]
        NEXT, PREV = ("T1", "Q", "K", "V0"), ("CT", "O", "T2", "F0", "F1", "F2", "F3", "Y", "T3", "D", "U")
        TURNS = ("CT", "P0", "O", "V1", "C0",
                 "P1", "V2", "T2", "C1", "F0", "F1", "F2",
                 "T1", "F3", "P2", "V3", "C2", "Q", "K", "Y",
                 "P3", "T3", "C3", "D", "V0", "U")
        BANK = {name: k % 4 for k, name in enumerate(TURNS)}

        def turns(name, g):
            mine = [t for t in TURNS if BANK[t] == BANK[name]]
            k = mine.index(name)
            start = sum(t in NEXT for t in mine)
            if isinstance(g, int) and g == -1:
                return sum(t in NEXT for t in mine[:k])
            if isinstance(g, int) and g == 0:
                return start + sum(t not in PREV for t in mine[:k])
            if isinstance(g, int) and g >= NG - 1:
                last = start + sum(t not in PREV for t in mine) + (NG - 2) * len(mine)
                if g == NG - 1:
                    return last + sum(t not in NEXT for t in mine[:k])
                return last + sum(t not in NEXT for t in mine) + sum(t in PREV for t in mine[:k])
            return (g - 1) * len(mine) + start + sum(t not in PREV for t in mine) + k

        def free(name, g):
            n = turns(name, g)
            if not (isinstance(n, int) and n == 0):
                nc.tensor.wait_ge(bank_read[BANK[name]], n)

        def was_read(eng, name, g):
            eng.wait_ge(bank_read[BANK[name]], turns(name, g) + 1)

        def read(ins, name):
            ins.then_inc(bank_read[BANK[name]], 1)

        def bank(name):
            return W[BANK[name]]

        def pipeline(eng, iteration):
            iteration(-1, 1, False, False, True)
            iteration(0, 0, False, True, True)
            with eng.Fori(0, (NG - 2) // 2) as i:
                for p in range(2):
                    iteration(i * 2 + p + 1, (p + 1) % 2, True, True, True)
            iteration(NG - 1, (NG - 1) % 2, True, True, False)
            iteration(NG, NG % 2, True, False, False)

        block = ctx.enter_context(nc.Block())

        passed = {e.engine.name: sem(f"passed_{e.engine.name}") for e in (nc.vector, nc.scalar, nc.tensor)}

        def hold(eng, sig, g, k=None):
            eng.wait_ge(sig.sem, sig.upto(g, k))

        def hold_apart(eng, sig, g, k=None):
            eng.wait_ge(sig.sem, sig.upto(g, k))
            eng.sem_inc(passed[eng.engine.name])

        def bc(ap, n):
            return ap.unsqueeze(len(ap.shape)).broadcast_to(list(ap.shape) + [n])

        def col(ap):
            return ap.rearrange("(p o) -> p o", o=1)

        def on_all(ap, n=P):
            return ap.rearrange("(o d) -> o d", o=1).broadcast_to([n, ap.shape[0]])

        x_view = a["x"].rearrange("(t b) s d -> (b s) t d", b=BT)
        out_view = out.rearrange("(t b) s d -> (b s) t d", b=BT)
        bias_view = a["fside_Bx16xSxS_0"].rearrange("b h q k -> b q h k")
        SMALL = 0

        @block.sync
        def _(sp):
            n = 0
            for dst, src in (
                (ids[0:NS, :], on_all(a["itok_B_6_14"], NS)), (ids2[:, :], on_all(a["itok_B_34_63"])),
                (ids3[:, :], on_all(a["itok_B_0_15"], NX + 2)), (embw[:, :], a["L0_cond_subj_emb"]),
                (hypw1[:, :], a["L0_cond_hyp_w1"]), (hypw2[:, :], a["L0_cond_hyp_w2"]),
                (styw1[:, :], a["L0_cond_sty_w1"]), (styw2[:, :], a["L0_cond_sty_w2"]),
                (hb[:, 0:1], col(a["L0_cond_hyp_b1"])), (hb[:, 1:2], col(a["L0_cond_hyp_b2"])),
                (hb[0:SQ, 2:3], col(a["L0_cond_sty_b1"])),
                (hb[:, 3:5], a["L0_cond_sty_b2"].rearrange("(c p) -> p c", p=P)),
                (ln_gb[:, 0:1], col(a["L0_cond_ln_g"])), (ln_gb[:, 1:2], col(a["L0_cond_ln_b"])),
                (rw[:, :], a["L0_cond_router_w"]),
                (wada[:, :], a["L2_cond_W_ada"]), (bada[:, :], a["L2_cond_b_ada"].rearrange("(c p) -> p c", p=P)),
                (fq[:, :], a["freqs"][:, 0:1]), (ph[:, :], a["freqs"][:, 1:3]),
                (ang[:, 0, :], a["condB_theta"].rearrange("(t b) -> b t", b=BT)),
                (ang[:, 1, :], a["condB_phi"].rearrange("(t b) -> b t", b=BT)),
                (dom4[:, :], a["itok_B_0_15"].rearrange("(t b) -> b t", b=BT)),
                (doww[:, :], a["L3_cond_down_W"]), (upw[:, :], a["L3_cond_up_W"]),
                (exw[:, :, :], a["L3_cond_expert_W"].rearrange("e o a -> o e a")),
                (vecs[:, 0:NX], a["L3_cond_expert_b"].rearrange("e o -> o e")),
                (emt[:, :], a["L3_cond_domain_emb"].rearrange("e o -> o e")),
                (upb[:, :], on_all(a["L3_cond_up_b"], NX + 2)),
                (wq[:, :], a["L2_cond_Wq"]), (wk[:, :], a["L2_cond_Wk"]), (wv[:, :], a["L2_cond_Wv"]), (wo[:, :], a["L2_cond_Wo"]),
                (w1[:, :], a["L2_cond_W1"]), (w2[:, :, :], a["L2_cond_W2"].rearrange("(c p) d -> p c d", p=P)),
                (b1[:, :], a["L2_cond_b1"].rearrange("(c p) -> p c", p=P)),
                (cols[:, 0:1], col(a["L2_cond_bq"])), (cols[:, 1:2], col(a["L2_cond_bk"])), (cols[:, 2:3], col(a["L2_cond_bv"])),
                (cols[:, 3:4], col(a["L2_cond_g2"])), (cols[:, 4:5], col(a["L2_cond_beta2"])),
                (rows[:, 0, :], on_all(a["L2_cond_bo"])), (rows[:, 1, :], on_all(a["L2_cond_b2"])),
                (rows[:, 2, :], on_all(a["L3_cond_ln_gamma"])), (rows[:, 3, :], on_all(a["L3_cond_ln_beta"])),
                (B1E[:, :, :], a["L0_cond_exp_b1"].rearrange("e (c p) -> p e c", p=P)),
            ):
                sp.dma_start(dst, src, allow_slow_non_contiguous=True).then_inc(ld_small, 16)
                n += 1
            for r in range(4):
                sp.dma_start(cols[A * r:A * r + A, 5:6], col(a["L3_cond_down_b"])).then_inc(ld_small, 16)
                n += 1
            assert n == N_SMALL, n
            sp.dma_start(X[:, :, :], x_view).then_inc(ld_x, 16)
            sp.dma_start(W1E[:, :, :], a["L0_cond_exp_w1"].rearrange("e d f -> d e f")).then_inc(ld_exp, 16)
            sp.dma_start(W2E[:, :, :, :], a["L0_cond_exp_w2"].rearrange("e (c p) d -> p e c d", p=P)).then_inc(ld_exp, 16)
            sp.dma_start(maskb[:, :, :], a["mask_Bx1xSxS_bk0"].rearrange("(t b) o q k -> (b o q) t k", b=BT)).then_inc(ld_mask, 16)
            sp.wait_ge(dve_set, D_WUS)
            sp.dma_start(wud[0:NX * A, :].rearrange("(c p) d -> p c d", p=P), wus[:, :, :]).then_inc(st_wu, 16)
            sp.dma_start(wud[NX * A:(NX + 1) * A, :], upT[:, :]).then_inc(st_wu, 16)
            sp.wait_ge(b2_zero, 1)
            for r in range(4):
                for t in range(GT):
                    lo = 32 * r + NE * t
                    sp.dma_start(b2bd[lo:lo + NE, t, :], a["L0_cond_exp_b2"]).then_inc(ld_b2, 16)
            with sp.Fori(0, NT) as t:
                for b in range(BT):
                    sp.dma_start(BIAS[S * b:S * b + S, bass.ds(t, 1), :, :].rearrange("p o h k -> p (o h) k"),
                                 bias_view[bass.ds(t * BT + b, 1), :, :, :].rearrange("o q h k -> (o q) h k")).then_inc(ld_bias, 16)
            with sp.Fori(0, NG // 2) as i:
                for p in range(2):
                    g = i * 2 + p
                    hold(sp, o_b, g)
                    sp.dma_start(out_view[:, bass.ds(g * GT, GT), :], ot[:, p, :, :]).then_inc(out_done[p], 16)
            for p in range(2):
                sp.wait_ge(out_done[p], 16 * (NG // 2) + 16)

        @block.gpsimd
        def _(pool):
            n = [0]

            def step(ins):
                n[0] += 1
                ins.then_inc(pool_set, 1)
                pool.wait_ge(pool_set, n[0])

            def band(ap, base, pattern, cm):
                step(pool.affine_select(out=ap, in_=ap, compare_op=ALU.is_ge, fill=0.0, base=base,
                                        pattern=pattern, channel_multiplier=cm))

            o_b.open(pool)
            for done in out_done:
                pool.sem_inc(done, 16)
            step(pool.memset(ident[:, :], 0.0))
            step(pool.affine_select(out=ident[:, :], in_=ident[:, :], compare_op=ALU.not_equal, fill=1.0,
                                    base=0, pattern=[[-1, P]], channel_multiplier=1))
            step(pool.iota(iot[:, :], [[0, 1]], base=0, channel_multiplier=1))
            for q in range(4):
                step(pool.iota(acol[A * q:A * q + A, :], [[0, 1]], base=0, channel_multiplier=1))
            step(pool.iota(desc[:, :], [[-1, NE]], base=NE, channel_multiplier=0))
            step(pool.memset(half[:, :], -0.5))
            step(pool.memset(hm16[:, :], 1.0))
            band(hm16[:, :], 0, [[-HD, H]], 1)
            band(hm16[:, :], HD - 1, [[HD, H]], -1)
            step(pool.memset(vm[:, :, :, :], 1.0))
            band(vm[:, :, :, :], 0, [[0, BT], [0, HJ], [-S, HP]], 1)
            band(vm[:, :, :, :], S - 1, [[0, BT], [0, HJ], [S, HP]], -1)
            step(pool.memset(e4[:, :], 1.0))
            band(e4[:, :], 0, [[1, P]], -S)
            band(e4[:, :], S - 1, [[-1, P]], S)
            assert n[0] == P_SET, n[0]
            pool.memset(b2bd[:, :, :], 0.0).then_inc(b2_zero, 1)
            step(pool.memset(hBD[:, :, :, :], 0.0))
            pool.wait_ge(ld_mask, 16)
            step(pool.tensor_copy(maskn[:, :, :], maskb[:, :, :]))
            step(pool.tensor_scalar(maskn[:, :, :], maskn[:, :, :], MASKED, 0.0, ALU.mult, ALU.add))
            pool.wait_ge(dve_set, D_WIDX)
            pool.wait_ge(st_wu, 32)
            for t in range(NT):
                pool.indirect_dma_start(out=WSEL[:, t, :], out_offset=None, in_=wud[:, :],
                                        in_offset=bass.IndirectOffsetOnAxis(ap=widx[:, t:t + 1], axis=0)).then_inc(ld_wsel, 16)
            with pool.Fori(0, NG) as g:
                hold(pool, a_st, g)
                pool.tensor_tensor(rstd[:, :], ve[:, :], half[:, 0:GT], ALU.pow).then_inc(a_rstd.sem, 1)
                hold(pool, a_dve, g, 4)
                pool.tensor_tensor(vs[:, 2, :], vs[:, 1, :], half[:, :], ALU.pow).then_inc(a_rv.sem, 1)
            pool.wait_ge(ld_bias, 16 * B)
            with pool.Fori(0, NG) as g:
                for s in range(GT):
                    bt = BIAS[:, bass.ds(g * GT + s, 1), :, :].rearrange("p o h k -> p (o h) k")
                    mk = maskn[:, bass.ds(g * GT + s, 1), :].broadcast_to([P, H, S])
                    pool.tensor_tensor(bt, bt, mk, ALU.add).then_inc(bias_masked.sem, 1)
            pool.wait_ge(e_acc.sem, e_acc.upto(NG - 1))
            for c in range(2):
                pool.tensor_copy(VB[:, c, :, :, HP * HD:GV], vm[:, :, :, :]).then_inc(vb_ones, 1)

            def iteration(g, p, prev, this, nxt):
                def subtract(g, s):
                    hold(pool, c_mx, g, s + 1)
                    c = s % 2
                    pool.tensor_tensor(Sc[:, c, :, :], Sc[:, c, :, :], bc(mx[:, c, :], S), ALU.subtract).then_inc(c_sub.sem, 1)

                if nxt:
                    for s in range(GT):
                        xt = X[:, bass.ds((g + 1) * GT + s, 1), :].rearrange("p o (w h e) -> p (o w) h e", h=2, e=2)
                        sw = big[:, 0, s * D:(s + 1) * D].rearrange("p (w h e) -> p w h e", h=2, e=2)
                        s4 = S4[:, bass.ds((g + 1) * GT + s, 1), :].broadcast_to([P, D // 4, 4]).rearrange("p w (h e) -> p w h e", h=2)
                        if s == 0:
                            hold(pool, r_x, g + 1, 0)
                        for e in range(2):
                            ins = pool.tensor_tensor(sw[:, :, :, e], xt[:, :, :, 1 - e], s4[:, :, :, e], ALU.mult)
                        ins.then_inc(r_swp.sem, 1)
                if prev:
                    hold(pool, d_st, g - 1)
                    pool.tensor_tensor(rstd2[:, :], ve2[:, :], half[:, 0:GT], ALU.pow).then_inc(d_rstd.sem, 1)
                if this:
                    subtract(g, 1)
                if prev:
                    pool.tensor_tensor(x2b[:, :, :], x2[:, :, :], rows[:, 1:2, :].broadcast_to([P, GT, D]), ALU.add).then_inc(d_x2b.sem, 1)
                if this:
                    subtract(g, 2)
                if nxt:
                    hold(pool, c_st, g + 1)
                    pool.tensor_tensor(rstd[:, :], ve[:, :], half[:, 0:GT], ALU.pow).then_inc(c_rstd.sem, 1)
                    hold(pool, c_xmul, g + 1)
                    pool.tensor_tensor(xmT[:, 1 - p, :].rearrange("d (b s) -> d b s", s=S), big[:, 1, :].rearrange("d (b s) -> d b s", s=S),
                                       bc(shiftT[:, bass.ds((g + 1) * GB, GB)], S), ALU.add).then_inc(c_xm.sem, 1)
                if this:
                    subtract(g, 3)
                if prev:
                    hold(pool, f_u, g - 1, 0)
                    pool.tensor_copy(ohx[:, :, :].rearrange("e t (b s) -> e (t b) s", s=S),
                                     bc(ohC[:, bass.ds((g - 1) * GB, GB)], S)).then_inc(f_oh.sem, 1)
                if nxt:
                    subtract(g + 1, 0)
                if prev:
                    hold(pool, o_st, g - 1)
                    pool.tensor_tensor(rstd3[:, :], ve3[:, :], half[:, 0:GT], ALU.pow).then_inc(o_rstd.sem, 1)
                    hold(pool, o_g, g - 1)
                    pool.wait_ge(out_done[1 - p], (g - 1 - (1 - p)) * 8 + 16)
                    pool.tensor_tensor(ot[:, 1 - p, :, :], z[:, :, :], rows[:, 3:4, :].broadcast_to([P, GT, D]), ALU.add).then_inc(o_b.sem, 1)

            pipeline(pool, iteration)

        @block.scalar
        def _(act):
            n = [0]

            def step(ins):
                n[0] += 1
                ins.then_inc(act_set, 1)

            for sig in (a_h, e_relu):
                sig.open(act)
            act.wait_ge(ld_small, 16 * N_SMALL)
            act.wait_ge(dve_set, D_ANG)
            step(act.activation(sB[:, :], sA[:, :], ACT.Sin))
            step(act.activation(trk[:, :, :], tr[:, :, :], ACT.Sin))
            act.wait_ge(act_set, 2)
            step(act.activation(sC[:, :], sB[:, :], ACT.Tanh, scale=0.5))
            act.wait_ge(pe_set, E_HYP1)
            step(act.activation(gammaT[:, :], W[0][:, 0:B], ACT.Relu, bias=hb[:, 0:1]))
            act.wait_ge(pe_set, E_HYP2)
            step(act.activation(betaT[:, :], W[1][:, 0:B], ACT.Identity, bias=hb[:, 1:2]))
            act.wait_ge(pe_set, E_STY1)
            step(act.activation(idf[0:SQ, :], W[0][0:SQ, 0:B], ACT.Relu, bias=hb[0:SQ, 2:3]))
            act.wait_ge(pe_set, E_STY2)
            step(act.activation(betaT[:, :], W[2][:, 0:B], ACT.Identity, bias=hb[:, 4:5]))
            step(act.activation(gammaT[:, :], W[1][:, 0:B], ACT.Identity, bias=hb[:, 3:4]))
            act.wait_ge(act_set, 8)
            step(act.activation(sD[:, :], gammaT[:, :], ACT.Abs))
            act.wait_ge(act_set, 9)
            step(act.activation(sD[:, :], sD[:, :], ACT.Exp, scale=-1.0))
            act.wait_ge(act_set, 10)
            step(act.activation(sD[:, :], sD[:, :], ACT.Ln, bias=1.0))
            assert n[0] == A_SET, n[0]
            with act.Fori(0, NG) as g:
                hold_apart(act, a_T, g)
                act.activation(HT[:, bass.ds(g * GN, GN)], W[3][:, :], ACT.Identity, bias=ln_gb[:, 1:2], scale=ln_gb[:, 0:1]).then_inc(a_h.sem, 1)
                hold_apart(act, a_dve, g, 2)
                act.activation(big[:, 0, :], HT[:, bass.ds(g * GN, GN)], ACT.Square).then_inc(a_sq.sem, 1)
            act.wait_ge(top, T_D)
            act.activation(g2[:, :], m2[:, :], ACT.Exp).then_inc(top_act, 1)
            for k in range(2):
                act.wait_ge(cT_ps, k + 1)
                act.activation(combT[:, k, :], W[k][:, 0:P], ACT.Copy).then_inc(cT_sb, 1)
            with act.Fori(0, NG) as g:
                for e in range(NE):
                    for c in range(FC):
                        if e >= 2:
                            hold(act, e_y, g, e - 1)
                        else:
                            hold(act, e_y, g, 0)
                        hold(act, e_h, g, e * FC + c + 1)
                        act.activation(hid[:, e % 2, c, :], W[c % 2][:, :], ACT.Relu, bias=B1E[:, e, c:c + 1]).then_inc(e_relu.sem, 1)
            hold(act, e_y, NG - 1)
            act.wait_ge(vb_ones, 2)

            def iteration(g, p, prev, this, nxt):
                def copy_pT(s):
                    hold(act, c_pT, g, s + 1)
                    read(act.activation(PT[:, :, :].rearrange("p j q -> p (j q)"), bank(f"P{s}")[:, :], ACT.Copy), f"P{s}")

                def copy_v(g, s):
                    hold(act, c_v, g, s + 1)
                    read(act.activation(VB[:, s % 2, :, :, 0:HP * HD], bank(f"V{s}")[:, :].rearrange("p (b j v) -> p b j v", b=BT, j=HJ), ACT.Copy), f"V{s}")

                def exps(g, s):
                    hold(act, c_sub, g, s + 1)
                    act.activation(Sc[:, s % 2, :, :], Sc[:, s % 2, :, :], ACT.Exp).then_inc(c_exp.sem, 1)

                def gelu(c):
                    hold(act, d_f, g - 1, c + 1)
                    read(act.activation(hid[:, 0, c, :], bank(f"F{c}")[:, :], ACT.Gelu_apprx_sigmoid, bias=b1[:, c:c + 1]), f"F{c}")

                if prev:
                    hold(act, d_cT, g - 1)
                    read(act.activation(ctxT[:, :], bank("CT")[:, :], ACT.Identity, bias=cols[:, 2:3]), "CT")
                if this:
                    copy_pT(0)
                    copy_v(g, 1)
                    exps(g, 1)
                    copy_pT(1)
                    copy_v(g, 2)
                if prev:
                    hold(act, t2, g - 1)
                    read(act.activation(h2T[:, :], bank("T2")[:, :], ACT.Identity, bias=cols[:, 4:5], scale=cols[:, 3:4]), "T2")
                if this:
                    exps(g, 2)
                if prev:
                    for c in range(FC):
                        gelu(c)
                if this:
                    copy_pT(2)
                    copy_v(g, 3)
                    exps(g, 3)
                if nxt:
                    hold(act, qp, g + 1)
                    read(act.activation(QT[:, :], bank("Q")[:, :], ACT.Identity, bias=bqs[:, :], scale=HD ** -0.5), "Q")
                    hold(act, kp, g + 1)
                    for h in range(HP):
                        ins = act.activation(KM[:, :, h, :], bank("K")[:, :].rearrange("d (b s) -> d b s", s=S), ACT.Identity,
                                             bias=bkm[:, h:h + 1], scale=hm4[:, h:h + 1])
                    read(ins, "K")
                if this:
                    copy_pT(3)
                if prev:
                    hold(act, t3, g - 1)
                    read(act.activation(X3T[:, :], bank("T3")[:, :], ACT.Copy), "T3")
                    hold(act, dp, g - 1)
                    for b in range(BT):
                        ins = act.activation(hBD[S * b:S * b + S, 0, :, S * b:S * b + S],
                                             bank("D")[S * b:S * b + S, :].rearrange("p (t q) -> p t q", q=P)[:, :, S * b:S * b + S],
                                             ACT.Gelu, bias=cols[S * b:S * b + S, 5:6])
                    read(ins, "D")
                if nxt:
                    copy_v(g + 1, 0)
                    exps(g + 1, 0)

            pipeline(act, iteration)

        @block.vector
        def _(dve):
            n = [0]

            def step(ins):
                n[0] += 1
                ins.then_inc(dve_set, 1)
                dve.wait_ge(dve_set, n[0])

            def wrap(ap, k, extra):
                step(dve.tensor_scalar(k, ap, 1 / (2 * PI), extra, ALU.mult, ALU.add))
                step(dve.tensor_scalar(k, k, ROUND, -ROUND, ALU.add, ALU.add))
                step(dve.scalar_tensor_tensor(out=ap, in0=k, scalar=-TWO_PI_HI, in1=ap, op0=ALU.mult, op1=ALU.add))
                step(dve.scalar_tensor_tensor(out=ap, in0=k, scalar=-TWO_PI_LO, in1=ap, op0=ALU.mult, op1=ALU.add))

            for sig in (e_acc, r_x, c_sc):
                sig.open(dve)
            dve.wait_ge(ld_small, 16 * N_SMALL)
            dve.wait_ge(pool_set, P_SET)
            step(dve.tensor_copy(iof[:, :], iot[:, :]))
            step(dve.tensor_copy(acf[:, :], acol[:, :]))
            step(dve.tensor_copy(dsf[:, :], desc[:, :]))
            step(dve.tensor_copy(idf[0:NS, :], ids[0:NS, :]))
            step(dve.tensor_scalar(onehot[:, :], idf[0:NS, :], iof[0:NS, :], None, ALU.is_equal))
            assert n[0] == D_ONEHOT, n[0]
            step(dve.tensor_copy(sB[:, :], ids2[:, :]))
            step(dve.tensor_scalar(sB[:, :], sB[:, :], 0.01, 4000.0, ALU.mult, ALU.mult))
            step(dve.tensor_scalar(sA[:, :], sB[:, :], fq[:, :], None, ALU.mult))
            wrap(sA[:, :], sB[:, :], ph[:, 0:1])
            step(dve.tensor_scalar(sA[:, :], sA[:, :], ph[:, 1:2], PI, ALU.add, ALU.min))
            step(dve.tensor_scalar(sA[:, :], sA[:, :], -PI, None, ALU.max))
            for k in range(4):
                step(dve.tensor_copy(tr[:, k, :], ang[:, k // 2, :]))
                wrap(tr[:, k, :], trk[:, k, :], 0.25 * (k % 2))
                step(dve.tensor_scalar(tr[:, k, :], tr[:, k, :], PI / 2 * (k % 2), PI, ALU.add, ALU.min))
                step(dve.tensor_scalar(tr[:, k, :], tr[:, k, :], -PI, None, ALU.max))
            assert n[0] == D_ANG, n[0]
            step(dve.tensor_reduce(out=hm4[:, :], in_=hm16[:, :].rearrange("p (j h) -> p h j", h=HP), axis=AX.X, op=ALU.add))
            step(dve.tensor_scalar(bkm[:, :], hm4[:, :], cols[:, 1:2], None, ALU.mult))
            step(dve.tensor_scalar(bqs[:, :], cols[:, 0:1], HD ** -0.5, None, ALU.mult))
            step(dve.tensor_tensor(vecs[:, 0:NX], vecs[:, 0:NX], emt[:, :], ALU.add))
            step(dve.tensor_copy(vecs[:, NX:NX + 1], emt[:, 0:1]))
            step(dve.tensor_copy(vecs[:, NX + 1:NX + 2], emt[:, NX - 1:NX]))
            step(dve.tensor_copy(dom4f[:, :], dom4[:, :]))
            step(dve.memset(wv4[:, :, :, :, :], 0.0))
            for h in range(HP):
                step(dve.tensor_copy(wv4[:, h, :, h, :], wv[:, :].rearrange("d (j h v) -> d j h v", j=HJ, h=HP)[:, :, h, :]))
            assert n[0] == D_TAB, n[0]
            dve.wait_ge(pe_set, E_SE)
            step(dve.tensor_copy(sD[0:SE, :], W[3][0:SE, 0:B]))
            dve.wait_ge(pe_set, E_DT)
            step(dve.tensor_copy(dwT[:, :, :], PS[:, 0:1, 0:A].broadcast_to([P, 4, A])))
            step(dve.tensor_copy(upT[:, :], PS[0:A, 1, 0:D]))
            assert n[0] == D_UPT, n[0]
            dve.wait_ge(act_set, 3)
            step(dve.scalar_tensor_tensor(out=sC[:, :], in0=sC[:, :], scalar=1.0, in1=sB[:, :], op0=ALU.add, op1=ALU.mult))
            step(dve.tensor_scalar(sC[:, :], sC[:, :], 0.5, None, ALU.mult))
            assert n[0] == D_SILU, n[0]
            dve.wait_ge(pe_set, E_ADA)
            step(dve.tensor_scalar(scaleT[:, :], PS[:, 2, 0:B], bada[:, 0:1], 1.0, ALU.add, ALU.add))
            step(dve.tensor_scalar(shiftT[:, :], PS[:, 3, 0:B], bada[:, 1:2], None, ALU.add))
            dve.wait_ge(pe_set, E_WU)
            step(dve.tensor_copy(wus[:, :, :].rearrange("p c d -> p (c d)"), PS[:, 0, :]))
            assert n[0] == D_WUS, n[0]
            dve.wait_ge(pe_set, E_CT)
            step(dve.tensor_tensor(CT[:, :], PS[0:NX + 2, 1, 0:D], upb[:, :], ALU.add))
            dve.wait_ge(pe_set, E_ROT)
            rot = PS[:, 2, 0:5 * NT].rearrange("p (k t) -> p k t", k=5)
            for k, (dst, src, sign) in enumerate(((S4, 0, 1), (S4, 0, -1), (S4, 2, 1), (S4, 2, -1), (C4, 1, 1), (C4, 1, 1), (C4, 3, 1), (C4, 3, 1))):
                step(dve.tensor_scalar(dst[:, :, k % 4], rot[:, src, :], float(sign), None, ALU.mult))
            step(dve.tensor_copy(domx[:, :], rot[:, 4, :]))
            step(dve.tensor_scalar(domy[:, :], domx[:, :], 0.0, None, ALU.is_ge))
            step(dve.scalar_tensor_tensor(out=domy[:, :], in0=domx[:, :], scalar=float(NX), in1=domy[:, :], op0=ALU.is_lt, op1=ALU.mult))
            step(dve.scalar_tensor_tensor(out=domx[:, :], in0=domx[:, :], scalar=-float(NX), in1=domy[:, :], op0=ALU.add, op1=ALU.mult))
            step(dve.tensor_scalar(domx[:, :], domx[:, :], float(NX), float(A), ALU.add, ALU.mult))
            step(dve.tensor_scalar(widx[:, :], domx[:, :], acf[:, :], None, ALU.add))
            assert n[0] == D_WIDX, n[0]
            step(dve.tensor_copy(sB[0:NX + 2, :], ids3[:, :]))
            step(dve.tensor_scalar(sA[0:NX + 2, :], sB[0:NX + 2, :], 0.0, float(NX + 1), ALU.is_lt, ALU.mult))
            step(dve.scalar_tensor_tensor(out=sA[0:NX + 2, :], in0=sB[0:NX + 2, :], scalar=float(NX) - 0.5, in1=sA[0:NX + 2, :], op0=ALU.is_gt, op1=ALU.add))
            step(dve.tensor_scalar(sB[0:NX + 2, :], sB[0:NX + 2, :], -1.0, float(NX), ALU.max, ALU.min))
            step(dve.tensor_tensor(sA[0:NX + 2, :], sA[0:NX + 2, :], sB[0:NX + 2, :], ALU.add))
            step(dve.tensor_scalar(ohC[:, :], sA[0:NX + 2, :], iof[0:NX + 2, :], None, ALU.is_equal))
            dve.wait_ge(act_set, A_SET)
            step(dve.scalar_tensor_tensor(out=gammaT[:, :], in0=gammaT[:, :], scalar=0.0, in1=sD[:, :], op0=ALU.max, op1=ALU.add))
            step(dve.tensor_scalar(gammaT[:, :], gammaT[:, :], 1e-8, None, ALU.add))
            assert n[0] == D_SET, n[0]

            def stats(src, sig, g, st=st, mv=mv, ve=ve):
                for s in range(GT):
                    dve.bn_stats(st[:, s, :], src(s)).then_inc(sig.sem, 1)
                hold_apart(dve, sig, g, GT)
                for s in range(GT):
                    dve.bn_aggr(mv[:, s, :], st[:, s, :]).then_inc(sig.sem, 1)
                hold_apart(dve, sig, g, 2 * GT)
                dve.tensor_scalar(ve[:, :], mv[:, :, 1], 1e-5, None, ALU.add).then_inc(sig.sem, 1)

            def normalise(dst, src, sig, g, mv=mv, rstd=rstd):
                for s in range(GT):
                    dve.tensor_scalar(dst(s), src(s), mv[:, s, 0:1], rstd[:, s:s + 1], ALU.subtract, ALU.mult).then_inc(sig.sem, 1)

            def tile_of(g, s):
                return X[:, bass.ds(g * GT + s, 1), :].rearrange("p o d -> p (o d)")

            dve.wait_ge(ld_x, 16)
            with dve.Fori(0, NG) as g:
                stats(lambda s: tile_of(g, s), a_st, g)
                hold(dve, a_rstd, g)
                hold(dve, a_T, g, 0)
                normalise(lambda s: xn[:, s, :], lambda s: tile_of(g, s), a_xn, g)
                ht = HT[:, bass.ds(g * GN, GN)].rearrange("d (b s) -> d b s", s=S)
                sq = big[:, 0, :].rearrange("d (b s) -> d b s", s=S)
                ctr = hTw[:, 0, :].rearrange("d (b s) -> d b s", s=S)
                hold(dve, a_h, g)
                dve.tensor_reduce(out=vs[:, 0, :], in_=ht, axis=AX.X, op=ALU.add).then_inc(a_dve.sem, 1)
                hold(dve, a_dve, g, 1)
                dve.scalar_tensor_tensor(out=ht, in0=bc(vs[:, 0, :], S), scalar=-1.0 / S, in1=ht, op0=ALU.mult, op1=ALU.add).then_inc(a_dve.sem, 1)
                hold(dve, a_sq, g)
                dve.tensor_reduce(out=vs[:, 1, :], in_=sq, axis=AX.X, op=ALU.add).then_inc(a_dve.sem, 1)
                hold(dve, a_dve, g, 3)
                dve.tensor_scalar(vs[:, 1, :], vs[:, 1, :], 1.0 / S, 1e-8, ALU.mult, ALU.add).then_inc(a_dve.sem, 1)
                hold(dve, a_rv, g)
                dve.tensor_tensor(vs[:, 3, :], vs[:, 2, :], gammaT[:, bass.ds(g * GB, GB)], ALU.mult).then_inc(a_dve.sem, 1)
                hold(dve, a_dve, g, 5)
                dve.tensor_tensor(ht, ht, bc(vs[:, 3, :], S), ALU.mult).then_inc(a_dve.sem, 1)
                hold(dve, a_dve, g, 6)
                hold(dve, a_lg, g, 0)
                dve.tensor_tensor(ctr, ht, bc(betaT[:, bass.ds(g * GB, GB)], S), ALU.add).then_inc(a_dve.sem, 1)
                hold_apart(dve, a_dve, g)
                dve.tensor_copy(HT[:, bass.ds(g * GN, GN)], hTw[:, 0, :]).then_inc(a_fin.sem, 1)

            k = [0]

            def pick(ins):
                k[0] += 1
                ins.then_inc(top, 1)
                dve.wait_ge(top, k[0])

            def best(lg, mval, w, sel):
                pick(dve.tensor_reduce(out=mval, in_=lg, axis=AX.X, op=ALU.max))
                pick(dve.tensor_tensor(w, lg, bc(mval, NE), ALU.is_equal))
                pick(dve.tensor_tensor(w, w, dsf[:, :].unsqueeze(1).broadcast_to([P, NT, NE]), ALU.mult))
                pick(dve.tensor_reduce(out=mw[:, :], in_=w, axis=AX.X, op=ALU.max))
                pick(dve.tensor_tensor(sel, w, bc(mw[:, :], NE), ALU.is_equal))

            hold(dve, a_lg, NG - 1)
            pick(dve.tensor_copy(Lg[:, :, :].rearrange("p t e -> p (t e)"), W[2][:, 0:NT * NE]))
            best(Lg[:, :, :], m1[:, :], ta[:, :, :], tb[:, :, :])
            pick(dve.scalar_tensor_tensor(out=Lg[:, :, :], in0=tb[:, :, :], scalar=MASKED, in1=Lg[:, :, :], op0=ALU.mult, op1=ALU.add))
            best(Lg[:, :, :], m2[:, :], ta[:, :, :], tc_[:, :, :])
            pick(dve.tensor_tensor(m2[:, :], m2[:, :], m1[:, :], ALU.subtract))
            assert k[0] == T_D, k[0]
            dve.wait_ge(top_act, 1)
            pick(dve.tensor_scalar(g1[:, :], g2[:, :], 1.0, None, ALU.add))
            pick(dve.reciprocal(g1[:, :], g1[:, :]))
            pick(dve.tensor_tensor(g2[:, :], g2[:, :], g1[:, :], ALU.mult))
            pick(dve.tensor_tensor(tb[:, :, :], tb[:, :, :], bc(g1[:, :], NE), ALU.mult))
            pick(dve.tensor_tensor(tc_[:, :, :], tc_[:, :, :], bc(g2[:, :], NE), ALU.mult))
            dve.tensor_tensor(comb[:, :, :], tb[:, :, :], tc_[:, :, :], ALU.add).then_inc(combined, 1)
            for g in range(NG):
                dve.wait_ge(bb_ps, g + 1)
                xg = X[:, g * GT:(g + 1) * GT, :].rearrange("p t d -> p (t d)")
                dve.tensor_tensor(xg, PS[:, g % 4, :], xg, ALU.add).then_inc(bb_add, 1)
            dve.wait_ge(bb_add, NG)
            dve.wait_ge(combined, 1)
            with dve.Fori(0, NG) as g:
                for e in range(NE):
                    hold(dve, e_y, g, e + 1)
                    if e:
                        hold(dve, e_acc, g, e)
                    for s in range(GT):
                        cb = comb[:, bass.ds(g * GT + s, 1), e]
                        ins = dve.scalar_tensor_tensor(out=tile_of(g, s), in0=W[2 + e % 2][:, s * D:(s + 1) * D], scalar=cb,
                                                       in1=tile_of(g, s), op0=ALU.mult, op1=ALU.add)
                    ins.then_inc(e_acc.sem, 1)
            hold(dve, e_acc, NG - 1)
            hold(dve, bias_masked, NG - 1)

            def iteration(g, p, prev, this, nxt):
                def scores(g, s):
                    hold(dve, c_qk, g, s + 1)
                    sc = Sc[:, s % 2, :, :]
                    dve.tensor_tensor(sc.rearrange("p (j h) k -> p j (h k)", j=HJ), PS[:, :, 0:P],
                                      BIAS[:, bass.ds(g * GT + s, 1), :, :].rearrange("p o (j h) k -> p (o j) (h k)", j=HJ), ALU.add).then_inc(c_sc.sem, 1)
                    hold(dve, c_sc, g, s + 1)
                    dve.tensor_reduce(out=mx[:, s % 2, :], in_=sc, axis=AX.X, op=ALU.max).then_inc(c_mx.sem, 1)

                def context(s):
                    hold(dve, c_pv, g, s + 1)
                    cv = bank(f"C{s}")[:, 0:HJ * GV].rearrange("p (j v) -> p j v", j=HJ)
                    dve.reciprocal(rs[:, :, :], cv[:, :, HP * HD:GV]).then_inc(c_rs.sem, 1)
                    hold(dve, c_rs, g, s + 1)
                    read(dve.tensor_tensor(Cn[:, s, :].rearrange("p (j h v) -> p j h v", j=HJ, h=HP),
                                           cv[:, :, 0:HP * HD].rearrange("p j (h v) -> p j h v", h=HP), bc(rs[:, :, :], HD), ALU.mult), f"C{s}")

                if prev:
                    hold(dve, d_o, g - 1)
                    read(dve.tensor_tensor(x2[:, :, :], bank("O")[:, :].rearrange("p (t d) -> p t d", d=D), rows[:, 0:1, :].broadcast_to([P, GT, D]), ALU.add), "O")
                    was_read(dve, "O", g)
                    stats(lambda s: x2[:, s, :], d_st, g - 1, st2, mv2, ve2)
                if this:
                    scores(g, 1)
                if prev:
                    hold(dve, d_rstd, g - 1)
                    normalise(lambda s: xn2[:, s, :], lambda s: x2[:, s, :], d_xn, g - 1, mv2, rstd2)
                if this:
                    context(0)
                if nxt:
                    for s in range(GT):
                        hold(dve, r_swp, g + 1, s + 1)
                        xt = X[:, bass.ds((g + 1) * GT + s, 1), :].rearrange("p o (w f) -> p (o w) f", f=4)
                        dve.tensor_tensor(xt, xt, C4[:, bass.ds((g + 1) * GT + s, 1), :].broadcast_to([P, D // 4, 4]), ALU.mult).then_inc(r_mul.sem, 1)
                    for s in range(GT):
                        hold(dve, r_mul, g + 1, s + 1)
                        dve.tensor_tensor(tile_of(g + 1, s), tile_of(g + 1, s), big[:, 0, s * D:(s + 1) * D], ALU.add).then_inc(r_x.sem, 1)
                if this:
                    scores(g, 2)
                if nxt:
                    hold_apart(dve, r_x, g + 1)
                    stats(lambda s: tile_of(g + 1, s), c_st, g + 1)
                if this:
                    context(1)
                if nxt:
                    hold(dve, c_rstd, g + 1)
                    normalise(lambda s: xn[:, s, :], lambda s: tile_of(g + 1, s), c_xn, g + 1)
                    hold(dve, t1, g + 1)
                    read(dve.tensor_tensor(big[:, 1, :].rearrange("d (b s) -> d b s", s=S), bank("T1")[:, :].rearrange("d (b s) -> d b s", s=S),
                                           bc(scaleT[:, bass.ds((g + 1) * GB, GB)], S), ALU.mult), "T1")
                    was_read(dve, "T1", g)
                    dve.sem_inc(c_xmul.sem)
                if this:
                    scores(g, 3)
                    context(2)
                if prev:
                    hold(dve, d_y, g - 1)
                    hold(dve, d_x2b, g - 1)
                    read(dve.tensor_tensor(X3[:, :, :].rearrange("p t d -> p (t d)"), bank("Y")[:, :], x2b[:, :, :].rearrange("p t d -> p (t d)"), ALU.add), "Y")
                if this:
                    context(3)
                if nxt:
                    scores(g + 1, 0)
                if prev:
                    hold(dve, f_u, g - 1)
                    was_read(dve, "Y", g)
                    hold(dve, o_b, g - 1, 0)
                    read(dve.tensor_tensor(z[:, :, :].rearrange("p t d -> p (t d)"), bank("U")[:, :], X3[:, :, :].rearrange("p t d -> p (t d)"), ALU.add), "U")
                    was_read(dve, "U", g)
                    stats(lambda s: z[:, s, :], o_st, g - 1, st3, mv3, ve3)
                    hold(dve, o_rstd, g - 1)
                    normalise(lambda s: z[:, s, :], lambda s: z[:, s, :], o_zn, g - 1, mv3, rstd3)
                    hold(dve, o_zn, g - 1)
                    dve.tensor_tensor(z[:, :, :], z[:, :, :], rows[:, 2:3, :].broadcast_to([P, GT, D]), ALU.mult).then_inc(o_g.sem, 1)

            pipeline(dve, iteration)

        @block.tensor
        def _(pe):
            n = [0]

            def mark(ins, at):
                n[0] += 1
                ins.then_inc(pe_set, 1)
                assert n[0] == at, (n[0], at)

            for sig in (a_T, a_lg, e_y, f_u):
                sig.open(pe)
            pe.wait_ge(ld_small, 16 * N_SMALL)
            pe.wait_ge(pool_set, P_SET)
            pe.wait_ge(dve_set, D_ONEHOT)
            mark(pe.matmul(W[3][0:SE, 0:B], embw[:, :], onehot[:, :], start=True, stop=True), E_SE)
            pe.transpose(PS[:, 0, 0:A], doww[:, :], ident[0:A, 0:A])
            mark(pe.transpose(PS[0:A, 1, 0:D], upw[:, :], ident[:, :]), E_DT)
            pe.wait_ge(dve_set, D_TAB + 1)
            mark(pe.matmul(W[0][:, 0:B], hypw1[:, :], sD[0:SE, :], start=True, stop=True), E_HYP1)
            pe.wait_ge(act_set, 4)
            mark(pe.matmul(W[1][:, 0:B], hypw2[:, :], gammaT[:, :], start=True, stop=True), E_HYP2)
            pe.wait_ge(act_set, 5)
            mark(pe.matmul(W[0][0:SQ, 0:B], styw1[:, :], betaT[:, :], start=True, stop=True), E_STY1)
            pe.wait_ge(act_set, 6)
            pe.matmul(W[1][:, 0:B], styw2[:, 0:D], idf[0:SQ, :], start=True, stop=True)
            mark(pe.matmul(W[2][:, 0:B], styw2[:, D:2 * D], idf[0:SQ, :], start=True, stop=True), E_STY2)
            pe.wait_ge(dve_set, D_SILU)
            pe.matmul(PS[:, 2, 0:B], wada[:, 0:D], sC[:, :], start=True, stop=True)
            mark(pe.matmul(PS[:, 3, 0:B], wada[:, D:2 * D], sC[:, :], start=True, stop=True), E_ADA)
            for c in range(NX // 4):
                ins = pe.matmul(PS[:, 0, c * D:(c + 1) * D], exw[:, 4 * c:4 * c + 4, :].rearrange("o e a -> o (e a)"), upT[:, :], start=True, stop=True)
            mark(ins, E_WU)
            mark(pe.matmul(PS[0:NX + 2, 1, 0:D], vecs[:, :], upT[:, :], start=True, stop=True), E_CT)
            pe.wait_ge(dve_set, D_WUS)
            pe.matmul(PS[:, 2, 0:4 * NT], e4[:, :], trk[:, :, :].rearrange("b k t -> b (k t)"), start=True, stop=True)
            mark(pe.matmul(PS[:, 2, 4 * NT:5 * NT], e4[:, :], dom4f[:, :], start=True, stop=True), E_ROT)
            pe.wait_ge(act_set, A_SET)
            with pe.Fori(0, NG) as g:
                hold(pe, a_h, g, 0)
                for s in range(GT):
                    hold(pe, a_xn, g, s + 1)
                    ins = pe.transpose(W[3][:, s * P:(s + 1) * P], xn[:, s, :], ident[:, :])
                ins.then_inc(a_T.sem, 1)
                hold(pe, a_dve, g)
                for s in range(GT):
                    ins = pe.matmul(W[2][:, bass.ds((g * GT + s) * NE, NE)], hTw[:, 0, s * P:(s + 1) * P], rw[:, :], start=True, stop=True)
                ins.then_inc(a_lg.sem, 1)
            pe.wait_ge(combined, 1)
            pe.wait_ge(ld_b2, 16 * 16)
            for k in range(2):
                pe.transpose(W[k][:, 0:P], comb[:, :, :].rearrange("p t e -> p (t e)")[:, k * P:(k + 1) * P], ident[:, :]).then_inc(cT_ps, 1)
            for g in range(NG):
                pe.wait_ge(cT_sb, g // 4 + 1)
                if g >= 4:
                    pe.wait_ge(bb_add, g - 3)
                r = 32 * (g % 4)
                pe.matmul(PS[:, g % 4, :], combT[r:r + 32, g // 4, :], b2bd[r:r + 32, :, :].rearrange("p t d -> p (t d)"), start=True, stop=True).then_inc(bb_ps, 1)
            pe.wait_ge(ld_exp, 32)
            hold(pe, a_fin, NG - 1)
            pe.wait_ge(cT_sb, 2)
            with pe.Fori(0, NG) as g:
                def up(e):
                    for c in range(FC):
                        if e * FC + c >= 2:
                            hold(pe, e_relu, g, e * FC + c - 1)
                        else:
                            hold(pe, e_relu, g, 0)
                        pe.matmul(W[c % 2][:, :], W1E[:, e, c * P:(c + 1) * P], HT[:, bass.ds(g * GN, GN)], start=True, stop=True).then_inc(e_h.sem, 1)

                def down(e):
                    if e >= 2:
                        hold(pe, e_acc, g, e - 1)
                    else:
                        hold(pe, e_acc, g, 0)
                    hold(pe, e_relu, g, (e + 1) * FC)
                    for s in range(GT):
                        for c in range(FC):
                            ins = pe.matmul(W[2 + e % 2][:, s * D:(s + 1) * D], hid[:, e % 2, c, s * P:(s + 1) * P], W2E[:, e, c, :], start=(c == 0), stop=(c == FC - 1))
                    ins.then_inc(e_y.sem, 1)

                up(0)
                for e in range(NE):
                    if e + 1 < NE:
                        up(e + 1)
                    down(e)
            hold(pe, e_acc, NG - 1)
            pe.wait_ge(ld_wsel, 16 * NT)
            pe.wait_ge(dve_set, D_SET)

            def iteration(g, p, prev, this, nxt):
                def transposed(name, src, ready, g_of, sig):
                    free(name, g)
                    for s in range(GT):
                        if ready is not None:
                            hold(pe, ready, g_of, s + 1)
                        ins = pe.transpose(bank(name)[:, s * P:(s + 1) * P], src[:, s, :], ident[:, :])
                    ins.then_inc(sig.sem, 1)

                def scores(g, s, par):
                    hold_apart(pe, c_sc, g, s)
                    for b in range(BT):
                        for j in range(HJ):
                            lo = s * P + b * S
                            ins = pe.matmul(PS[S * b:S * b + S, j, 0:P], QT[32 * j:32 * j + 32, lo:lo + S],
                                            KM[32 * j:32 * j + 32, s * BT + b, :, :].rearrange("d h k -> d (h k)"), start=True, stop=True)
                    ins.then_inc(c_qk.sem, 1)

                def values(it, g, s, par):
                    free(f"V{s}", it)
                    for b in range(BT):
                        lo = s * P + b * S
                        for h in range(HP):
                            ins = pe.matmul(bank(f"V{s}")[S * h:S * h + S, b * D:(b + 1) * D], xmT[:, par, lo:lo + S],
                                            wv4[:, h, :, :, :].rearrange("d j h v -> d (j h v)"), start=True, stop=True)
                    ins.then_inc(c_v.sem, 1)

                def transposed_probs(s):
                    hold(pe, c_exp, g, s + 1)
                    free(f"P{s}", g)
                    for j in range(HJ):
                        ins = pe.transpose(bank(f"P{s}")[:, j * P:(j + 1) * P], Sc[:, s % 2, j * HP:(j + 1) * HP, :].rearrange("p h k -> p (h k)"), ident[:, :])
                    ins.then_inc(c_pT.sem, 1)

                def context(s):
                    was_read(pe, f"P{s}", g)
                    free(f"C{s}", g)
                    for b in range(BT):
                        for j in range(HJ):
                            ins = pe.matmul(bank(f"C{s}")[S * b:S * b + S, j * GV:(j + 1) * GV], PT[:, j, b * S:b * S + S], VB[:, s % 2, b, j, :],
                                            start=True, stop=True)
                    ins.then_inc(c_pv.sem, 1)

                def up(c):
                    free(f"F{c}", g)
                    pe.matmul(bank(f"F{c}")[:, :], w1[:, c * P:(c + 1) * P], h2T[:, :], start=True, stop=True).then_inc(d_f.sem, 1)

                if prev:
                    was_read(pe, "C3", g - 1)
                    transposed("CT", Cn, None, None, d_cT)
                if this:
                    transposed_probs(0)
                if prev:
                    was_read(pe, "CT", g)
                    free("O", g)
                    for s in range(GT):
                        pe.matmul(bank("O")[:, s * D:(s + 1) * D], ctxT[:, s * P:(s + 1) * P], wo[:, :], start=True, stop=False)
                        ins = pe.matmul(bank("O")[:, s * D:(s + 1) * D], xmT[:, 1 - p, s * P:(s + 1) * P], ident[:, :], start=False, stop=True)
                    ins.then_inc(d_o.sem, 1)
                if this:
                    scores(g, 1, p)
                    values(g, g, 1, p)
                    context(0)
                    transposed_probs(1)
                    scores(g, 2, p)
                    values(g, g, 2, p)
                if prev:
                    transposed("T2", xn2, d_xn, g - 1, t2)
                if this:
                    context(1)
                if prev:
                    was_read(pe, "T2", g)
                    for c in range(FC - 1):
                        up(c)
                if nxt:
                    transposed("T1", xn, c_xn, g + 1, t1)
                if prev:
                    up(FC - 1)
                if this:
                    transposed_probs(2)
                    scores(g, 3, p)
                    values(g, g, 3, p)
                    context(2)
                if nxt:
                    hold(pe, c_xm, g + 1)
                    free("Q", g)
                    pe.matmul(bank("Q")[:, :], wq[:, :], xmT[:, 1 - p, :], start=True, stop=True).then_inc(qp.sem, 1)
                    free("K", g)
                    pe.matmul(bank("K")[:, :], wk[:, :], xmT[:, 1 - p, :], start=True, stop=True).then_inc(kp.sem, 1)
                if prev:
                    for c in range(FC):
                        was_read(pe, f"F{c}", g)
                    free("Y", g)
                    for s in range(GT):
                        for c in range(FC):
                            ins = pe.matmul(bank("Y")[:, s * D:(s + 1) * D], hid[:, 0, c, s * P:(s + 1) * P], w2[:, c, :], start=(c == 0), stop=(c == FC - 1))
                    ins.then_inc(d_y.sem, 1)
                if this:
                    transposed_probs(3)
                if prev:
                    was_read(pe, "Y", g)
                    transposed("T3", X3, None, None, t3)
                if this:
                    context(3)
                if prev:
                    was_read(pe, "T3", g)
                    free("D", g)
                    pe.matmul(bank("D")[:, :], dwT[:, :, :].rearrange("d r a -> d (r a)"), X3T[:, :], start=True, stop=True).then_inc(dp.sem, 1)
                if nxt:
                    was_read(pe, "Q", g)
                    was_read(pe, "K", g)
                    pe.sem_inc(passed["PE"])
                    scores(g + 1, 0, 1 - p)
                    values(g, g + 1, 0, 1 - p)
                if prev:
                    was_read(pe, "D", g)
                    hold(pe, f_oh, g - 1)
                    free("U", g)
                    for s in range(GT):
                        pe.matmul(bank("U")[:, s * D:(s + 1) * D], hBD[:, 0, s, :], WSEL[:, bass.ds((g - 1) * GT + s, 1), :].rearrange("p o d -> p (o d)"), start=True, stop=False)
                        ins = pe.matmul(bank("U")[:, s * D:(s + 1) * D], ohx[:, s, :], CT[:, :], start=False, stop=True)
                    ins.then_inc(f_u.sem, 1)

            pipeline(pe, iteration)


N_SMALL = 49
P_SET = 18
A_SET = 11
E_SE, E_DT, E_HYP1, E_HYP2, E_STY1, E_STY2, E_ADA, E_WU, E_CT, E_ROT = range(1, 11)
D_ONEHOT = 5
D_ANG = 42
D_TAB = 54
D_UPT = 57
D_SILU = 59
D_WUS = 62
D_WIDX = 77
D_SET = 85
T_D = 13


def kernel(**inputs):
    import numpy as np
    import concourse.bacc as bacc
    from concourse.bass_utils import run_bass_kernel_spmd

    nc = bacc.Bacc("TRN2", target_bir_lowering=False, num_devices=1)
    arrays = {name: np.ascontiguousarray(v) for name, v in inputs.items()}
    half = 64
    f = np.exp(np.arange(half, dtype=np.float32) * np.float32(-np.log(10000.0) / (half - 1))).astype(np.float32)
    freqs = np.zeros((128, 3), np.float32)
    freqs[:, 0] = np.concatenate([f, f])
    freqs[half:, 1] = 0.25
    freqs[half:, 2] = np.pi / 2
    arrays["freqs"] = freqs
    aps = {}
    for name, v in arrays.items():
        aps[name] = nc.dram_tensor(name + "_dram", v.shape, mybir.dt.from_np(v.dtype), kind="ExternalInput").ap()
    shape = inputs["x"].shape
    out = nc.dram_tensor("out_dram", shape, F32, kind="ExternalOutput").ap()
    build(nc, aps, out)
    r = run_bass_kernel_spmd(nc, [{k + "_dram": v for k, v in arrays.items()}], core_ids=[0])
    return r.results[0]["out_dram"]
```

```python
from contextlib import ExitStack

import concourse.bass as bass
from concourse import mybir

F32 = mybir.dt.float32
BF16 = mybir.dt.bfloat16
I32 = mybir.dt.int32
U32 = mybir.dt.uint32
U8 = mybir.dt.uint8
ALU = mybir.AluOpType
ACT = mybir.ActivationFunctionType
AX = mybir.AxisListType

P = 128
PI = 3.14159265358979
TWO_PI_HI = 6.28125
TWO_PI_LO = 2 * PI - TWO_PI_HI
ROUND = 12582912.0
MASKED = -1.0e30


class Signal:

    def __init__(self, sem, per, lead):
        self.sem, self.per, self.lead = sem, per, lead

    def open(self, eng):
        eng.sem_inc(self.sem, self.lead)

    def upto(self, g, k=None):
        return g * self.per + (self.per if k is None else k) + self.lead


def build(nc, a, out):
    B, S, D = a["x"].shape
    NT = B * S // P
    BT = P // S
    GT = 4
    NG = NT // GT
    GB = GT * BT
    GN = GT * P
    H = 16
    HD = D // H
    NE, _, FF = a["L0_cond_exp_w1"].shape
    FC = FF // P
    HJ = 4
    HP = H // HJ
    GV = HP * HD + HP
    NX, A, _ = a["L3_cond_expert_W"].shape
    SE = a["L0_cond_subj_emb"].shape[1]
    NS = a["L0_cond_subj_emb"].shape[0]
    SQ = a["L0_cond_sty_w1"].shape[1]

    LIST = 2 * NT + NE - 1
    REGION = B * S + P
    SPARE = 8
    assert (LIST - 3) % 4 == (LIST - 7) % 4 == 0 and LIST - 2 * NT < SPARE

    wud = nc.dram_tensor("expert_up_rows", [(NX + 1) * A, D], F32, kind="Internal").ap()
    hrows = nc.dram_tensor("expert_in_rows", [NE * REGION + SPARE * P, D], F32, kind="Internal").ap()
    yrows = nc.dram_tensor("expert_out_rows", [LIST * P, D], F32, kind="Internal").ap()

    with ExitStack() as ctx:
        def sb(name, shape, dt=F32):
            return ctx.enter_context(nc.sbuf_tensor(name, shape, dt))

        def sem(name):
            return ctx.enter_context(nc.semaphore(name))

        def signal(name, per=1, lead=0):
            return Signal(sem(name), per, lead)

        X = sb("X", [P, NT, D])
        ROOM = sb("ROOM", [P, NT * P])
        BIAS = sb("BIAS", [P, NT, H, S])
        EXP = sb("EXP", [P, 2 * NE * FF])
        W1E = EXP[:, 0:NE * FF].rearrange("p (e f) -> p e f", e=NE)
        W2E = EXP[:, NE * FF:2 * NE * FF].rearrange("p (e c d) -> p e c d", e=NE, c=FC)
        hid = sb("hid", [P, 2, FC, GN])
        lent = [0]

        def setup(shape, dt=F32):
            n = 1
            for d in shape[1:]:
                n *= d
            lent[0] += n
            assert lent[0] <= FC * GN
            ap = hid[0:shape[0], 1, :, :].rearrange("p c n -> p (c n)")[:, lent[0] - n:lent[0]]
            return ap if dt is F32 else ap.bitcast(dt)

        used = [0]

        def part(n):
            lo = used[0] if used[0] + n <= 2 * NE * FF or used[0] >= 2 * NE * FF else 2 * NE * FF
            used[0] = lo + n
            if lo < 2 * NE * FF:
                return EXP[:, lo:lo + n]
            lo -= 2 * NE * FF
            assert lo + n <= 3 * NT * P // 4
            return ROOM[:, lo:lo + n]

        hA = ROOM[:, 2 * GN:3 * GN]
        hrow = ROOM[:, 0:2 * GN].rearrange("p (c t d) -> p c t d", c=2, d=D)
        tile_in = ROOM[:, 0:GN].rearrange("p (c d) -> p c d", d=D)
        tile_out = ROOM[:, GN:2 * GN].rearrange("p (c d) -> p c d", d=D)
        tile_inT = ROOM[:, 3 * GN:3 * GN + 2 * P].rearrange("p (c n) -> p c n", c=2)
        Y = ROOM[:, 3 * NT * P // 4:NT * P].rearrange("p (k t d) -> p k t d", k=2, d=D)

        B1E = sb("B1E", [P, NE, FC])
        ident = sb("ident", [P, P])
        ln_gb = sb("ln_gb", [P, 2])
        ids = setup([P, B], I32); ids2 = setup([P, B], I32); ids3 = setup([NX + 2, B], I32)
        idf = setup([P, B])
        embw = setup([NS, SE])
        hypw1 = setup([SE, P]); hypw2 = setup([P, P])
        styw1 = setup([P, SQ]); styw2 = setup([SQ, 2 * D])
        hb = sb("hb", [P, 5])
        wada = setup([P, 2 * D]); bada = sb("bada", [P, 2])
        rw = sb("rw", [P, NE])
        B2E = sb("B2E", [P, NE, D])
        fq = sb("fq", [P, 1]); ph = sb("ph", [P, 2])
        wq = sb("wq", [P, D]); wk = sb("wk", [P, D]); wv = sb("wv", [P, D]); wo = sb("wo", [P, D])
        w1 = sb("w1", [P, FF]); w2 = sb("w2", [P, FC, D]); b1 = sb("b1", [P, FC])
        cols = sb("cols", [P, 6])
        bqs = sb("bqs", [P, 1]); bkm = sb("bkm", [P, HP])
        rows = sb("rows", [P, 4, D])
        maskb = sb("maskb", [P, NT, S], U8); ot = sb("ot", [P, 2, GT, D])
        maskn = ot[:, :, :, :].rearrange("p a t d -> p (a t d)").rearrange("p (t k) -> p t k", k=S)
        hm16 = sb("hm16", [P, H]); hm4 = sb("hm4", [P, HP]); vm = sb("vm", [P, BT, HJ, HP])
        e4 = sb("e4", [BT, P]); ang = sb("ang", [BT, 2, NT]); tr = sb("tr", [BT, 4, NT]); trk = sb("trk", [BT, 4, NT])
        C4 = sb("C4", [P, NT, 4]); S4 = sb("S4", [P, NT, 4])
        iot = sb("iot", [P, 1], I32); iof = sb("iof", [P, 1]); acol = sb("acol", [P, 1], I32); acf = sb("acf", [P, 1])
        half = sb("half", [P, GB])
        desc = sb("desc", [P, NE], I32); dsf = sb("dsf", [P, NE])
        onehot = setup([NS, B])
        sA = setup([P, B]); sB = setup([P, B]); sC = setup([P, B]); sD = setup([P, B])
        gammaT = sb("gammaT", [P, B]); betaT = sb("betaT", [P, B])
        scaleT = sb("scaleT", [P, B]); shiftT = sb("shiftT", [P, B])
        doww = sb("doww", [A, D]); dwT = sb("dwT", [P, 4, A]); upw = sb("upw", [P, A]); upT = sb("upT", [A, D])
        exw = ROOM[0:A, 4 * GN:5 * GN].rearrange("o (e a) -> o e a", e=NX); wus = ROOM[:, 5 * GN:6 * GN].rearrange("p (c d) -> p c d", d=D)
        vecs = sb("vecs", [A, NX + 2]); emt = sb("emt", [A, NX])
        upb = sb("upb", [NX + 2, D]); CT = sb("CT", [NX + 2, D]); ohC = sb("ohC", [NX + 2, B])
        dom4 = sb("dom4", [BT, NT], I32); dom4f = sb("dom4f", [BT, NT]); domx = sb("domx", [P, NT]); domy = sb("domy", [P, NT])
        widx = sb("widx", [P, NT], U32)
        WSEL = sb("WSEL", [P, NT, D])
        hBD = sb("hBD", [P, 1, GT, P])
        g1 = sb("g1", [P, NT]); g2 = sb("g2", [P, NT]); m1 = sb("m1", [P, NT]); m2 = sb("m2", [P, NT]); mw = sb("mw", [P, GT])
        upper = sb("upper", [P, P], BF16); ones = sb("ones", [P, P], BF16); both = sb("both", [P, GT + 1, NE], BF16)
        posf = sb("posf", [P, 2, NT]); moved = sb("moved", [P, 2, NT]); pos = sb("pos", [P, 2, NT], U32)
        pos_g = sb("pos_g", [P, 2, 2, GT], U32)
        base = sb("base", [P, NE]); regi = sb("regi", [P, NE], I32); regf = sb("regf", [P, NE])
        pads = sb("pads", [P, NE], I32); tiles = sb("tiles", [P, NE]); ends = sb("ends", [P, NE]); jump = sb("jump", [P, NE])
        seqi = sb("seqi", [P, LIST], I32); seq = sb("seq", [P, LIST])
        row_at = sb("row_at", [P, LIST], I32); expert_at = sb("expert_at", [P, LIST], I32); pair_at = sb("pair_at", [P, LIST + 3], I32); eight_at = sb("eight_at", [P, (LIST - 3) // 4], I32)
        st = sb("st", [P, GT, 6]); mv = sb("mv", [P, GT, 2]); ve = sb("ve", [P, GT]); rstd = sb("rstd", [P, GT])
        xn = sb("xn", [P, GT, D]); xn2 = part(GT * D).rearrange("p (t d) -> p t d", d=D)
        st2, st3 = (sb(f"st{k}", [P, GT, 6]) for k in (2, 3))
        mv2, mv3 = (sb(f"mv{k}", [P, GT, 2]) for k in (2, 3))
        ve2, ve3, rstd2, rstd3 = (sb(f"{n}", [P, GT]) for n in ("ve2", "ve3", "rstd2", "rstd3"))
        big = sb("big", [P, 2, GN]); hTw = sb("hTw", [P, 1, GN])
        vs = sb("vs", [P, 4, GB])
        sel = hid[:, 0, 0, 0:2 * NT * NE].rearrange("p (k t e) -> p k t e", k=2, e=NE)
        Lg, ta, pf = (hid[:, 0, 1, k * GT * NE:(k + 1) * GT * NE].rearrange("p (t e) -> p t e", e=NE) for k in range(3))
        picked = hid[:, 0, 2, 0:2 * GT * NE].rearrange("p (k t e) -> p k t e", k=2, e=NE)
        moves = hid[:, 0, 1, :].rearrange("p (k t e) -> p k t e", k=2, e=NE)
        passed_end = hid[:, 0, 2:4, :].rearrange("p c n -> p (c n)")[:, 0:LIST * NE].rearrange("p (i e) -> p i e", e=NE)
        pairf = hid[:, 0, 1, GN // 2 + P:GN // 2 + P + LIST + 3]
        listf = hid[:, 0, 1, GN // 2:GN // 2 + LIST]
        xmT = part(2 * GN).rearrange("p (c n) -> p c n", c=2); QT = part(GN); KM = part(GB * HP * S).rearrange("p (b h k) -> p b h k", h=HP, k=S)
        Sc = part(2 * H * S).rearrange("p (c h k) -> p c h k", c=2, h=H)
        PT = part(HJ * P).rearrange("p (j q) -> p j q", j=HJ)
        VB = part(2 * BT * HJ * GV).rearrange("p (c b j v) -> p c b j v", c=2, b=BT, j=HJ)
        wv4 = sb("wv4", [P, HP, HJ, HP, HD])
        Cn = part(GT * D).rearrange("p (t d) -> p t d", d=D)
        mx = sb("mx", [P, 2, H]); rs = sb("rs", [P, HJ, HP])
        ctxT = part(GN)
        x2, x2b, X3, z = (part(GT * D).rearrange("p (t d) -> p t d", d=D) for _ in range(4))
        h2T = part(GN); X3T = part(GN)
        ohx = sb("ohx", [NX + 2, GT, P])

        PS = ctx.enter_context(nc.psum_tensor("PS", [P, 4, 512], F32))
        W = [ctx.enter_context(nc.psum_tensor(f"W{i}", [P, 512], F32)) for i in range(4)]

        ld_small = sem("ld_small"); ld_x = sem("ld_x"); ld_exp = sem("ld_exp"); ld_bias = sem("ld_bias"); ld_mask = sem("ld_mask")
        ld_b2 = sem("ld_b2"); st_wu = sem("st_wu"); ld_wsel = sem("ld_wsel"); out_done = [sem(f"out_done{i}") for i in range(2)]
        pool_set = sem("pool_set"); dve_set = sem("dve_set"); act_set = sem("act_set"); pe_set = sem("pe_set")
        zeroed = sem("zeroed")
        bias_masked = signal("bias_masked", GT)
        a_st = signal("a_st", 2 * GT + 1); a_sqrt = signal("a_sqrt"); a_rstd = signal("a_rstd"); a_xn = signal("a_xn", GT)
        a_T = signal("a_T", lead=1); a_h = signal("a_h"); a_dve = signal("a_dve", 8); a_sq = signal("a_sq"); a_rv = signal("a_rv")
        a_lg = signal("a_lg", lead=1); a_rT = signal("a_rT", lead=1); a_row = signal("a_row", lead=2)
        best = signal("best", 13); a_pos = signal("a_pos"); placed = signal("placed", 4, lead=1)
        idx_ready = signal("idx_ready"); slot_free = signal("slot_free", lead=2); scattered = [sem(f"scattered{c}") for c in range(2)]
        listed = sem("listed"); pads_ready = sem("pads_ready"); pads_done = sem("pads_done"); spare_done = sem("spare_done")
        gate_act = sem("gate_act"); gate_dve = sem("gate_dve")
        tile_ld = [sem(f"tile_ld{c}") for c in range(4)]; tile_st = [sem(f"tile_st{c}") for c in range(4)]
        e_T, e_in, e_h, e_hc, e_hT, e_add, e_relu, e_y, e_yc = (
            signal(n, lead=2) for n in ("e_T", "e_in", "e_h", "e_hc", "e_hT", "e_add", "e_relu", "e_y", "e_yc"))
        y_idx = signal("y_idx"); y_ld = signal("y_ld", 16 * 2 * GT); y_add = signal("y_add", 2)
        r_mul = signal("r_mul", GT); r_swp = signal("r_swp", GT); r_x = signal("r_x", GT, lead=1)
        c_st = signal("c_st", 2 * GT + 1); c_rstd = signal("c_rstd"); c_xn = signal("c_xn", GT); c_xmul = signal("c_xmul")
        c_xm = signal("c_xm"); c_q = signal("c_q"); c_qk = signal("c_qk", GT); c_sc = signal("c_sc", GT, lead=1); c_mx = signal("c_mx", GT)
        c_sub = signal("c_sub", GT); c_exp = signal("c_exp", GT); c_rs = signal("c_rs", GT); c_cn = signal("c_cn", GT)
        c_pv = signal("c_pv", GT); c_v = signal("c_v", GT); c_pT = signal("c_pT", GT)
        d_cT = signal("d_cT"); d_o = signal("d_o"); d_x2 = signal("d_x2"); d_x2b = signal("d_x2b")
        d_st = signal("d_st", 2 * GT + 1); d_rstd = signal("d_rstd"); d_xn = signal("d_xn", GT); d_f = signal("d_f", FC)
        d_y = signal("d_y"); f_x3 = signal("f_x3"); f_oh = signal("f_oh"); f_u = signal("f_u", lead=1); f_z = signal("f_z")
        t1 = signal("t1"); t2 = signal("t2"); t3 = signal("t3"); qp = signal("qp"); kp = signal("kp"); dp = signal("dp")
        o_st = signal("o_st", 2 * GT + 1); o_rstd = signal("o_rstd"); o_zn = signal("o_zn", GT); o_g = signal("o_g")
        o_b = signal("o_b", lead=1)
        vb_ones = sem("vb_ones"); listed_dve = sem("listed_dve")

        bank_read = [sem(f"bank_read{b}") for b in range(4)]
        NEXT, PREV = ("T1", "Q", "K", "V0"), ("CT", "O", "T2", "F0", "F1", "F2", "F3", "Y", "T3", "D", "U")
        TURNS = ("CT", "P0", "O", "V1", "C0",
                 "P1", "V2", "T2", "C1", "F0", "F1", "F2",
                 "T1", "F3", "P2", "V3", "C2", "Q", "K", "Y",
                 "P3", "T3", "C3", "D", "V0", "U")
        BANK = {name: k % 4 for k, name in enumerate(TURNS)}

        def turns(name, g):
            mine = [t for t in TURNS if BANK[t] == BANK[name]]
            k = mine.index(name)
            start = sum(t in NEXT for t in mine)
            if isinstance(g, int) and g == -1:
                return sum(t in NEXT for t in mine[:k])
            if isinstance(g, int) and g == 0:
                return start + sum(t not in PREV for t in mine[:k])
            if isinstance(g, int) and g >= NG - 1:
                last = start + sum(t not in PREV for t in mine) + (NG - 2) * len(mine)
                if g == NG - 1:
                    return last + sum(t not in NEXT for t in mine[:k])
                return last + sum(t not in NEXT for t in mine) + sum(t in PREV for t in mine[:k])
            return (g - 1) * len(mine) + start + sum(t not in PREV for t in mine) + k

        def free(name, g):
            n = turns(name, g)
            if not (isinstance(n, int) and n == 0):
                nc.tensor.wait_ge(bank_read[BANK[name]], n)

        def was_read(eng, name, g):
            eng.wait_ge(bank_read[BANK[name]], turns(name, g) + 1)

        def read(ins, name):
            ins.then_inc(bank_read[BANK[name]], 1)

        def bank(name):
            return W[BANK[name]]

        class Place:

            def __init__(self, j, q):
                self.j, self.q = j, q

            def at(self, d):
                return self.j * 4 + (self.q + 2 + d)

            def slot(self, d):
                return (self.q + 2 + d) % 4

            def round(self, d):
                return self.j + (self.q + 2 + d) // 4

        def tile_pipeline(eng, step):
            step(Place(-1, 1), True, False, False, False)
            step(Place(-1, 2), True, True, False, False)
            step(Place(-1, 3), True, True, True, False)
            with eng.Fori(0, (LIST - 3) // 4) as j:
                for q in range(4):
                    step(Place(j, q), True, True, True, True)
            j = (LIST - 3) // 4
            step(Place(j, 0), False, True, True, True)
            step(Place(j, 1), False, False, True, True)
            step(Place(j, 2), False, False, False, True)

        def pipeline(eng, iteration):
            iteration(-1, 1, False, False, True, True)
            iteration(0, 0, False, True, True, True)
            with eng.Fori(0, (NG - 4) // 2) as i:
                for p in range(2):
                    iteration(i * 2 + p + 1, (p + 1) % 2, True, True, True, True)
            iteration(NG - 3, (NG - 3) % 2, True, True, True, True)
            iteration(NG - 2, (NG - 2) % 2, True, True, True, False)
            iteration(NG - 1, (NG - 1) % 2, True, True, False, False)
            iteration(NG, NG % 2, True, False, False, False)

        block = ctx.enter_context(nc.Block())

        passed = {e.engine.name: sem(f"passed_{e.engine.name}") for e in (nc.vector, nc.scalar, nc.tensor, nc.gpsimd)}

        def hold(eng, sig, g, k=None):
            eng.wait_ge(sig.sem, sig.upto(g, k))

        def hold_apart(eng, sig, g, k=None):
            eng.wait_ge(sig.sem, sig.upto(g, k))
            eng.sem_inc(passed[eng.engine.name])

        def bc(ap, n):
            return ap.unsqueeze(len(ap.shape)).broadcast_to(list(ap.shape) + [n])

        def col(ap):
            return ap.rearrange("(p o) -> p o", o=1)

        def on_all(ap, n=P):
            return ap.rearrange("(o d) -> o d", o=1).broadcast_to([n, ap.shape[0]])

        x_view = a["x"].rearrange("(t b) s d -> (b s) t d", b=BT)
        out_view = out.rearrange("(t b) s d -> (b s) t d", b=BT)
        bias_view = a["fside_Bx16xSxS_0"].rearrange("b h q k -> b q h k")
        SMALL = 0

        @block.sync
        def _(sp):
            n = 0
            for dst, src in (
                (ids[0:NS, :], on_all(a["itok_B_6_14"], NS)), (ids2[:, :], on_all(a["itok_B_34_63"])),
                (ids3[:, :], on_all(a["itok_B_0_15"], NX + 2)), (embw[:, :], a["L0_cond_subj_emb"]),
                (hypw1[:, :], a["L0_cond_hyp_w1"]), (hypw2[:, :], a["L0_cond_hyp_w2"]),
                (styw1[:, :], a["L0_cond_sty_w1"]), (styw2[:, :], a["L0_cond_sty_w2"]),
                (hb[:, 0:1], col(a["L0_cond_hyp_b1"])), (hb[:, 1:2], col(a["L0_cond_hyp_b2"])),
                (hb[0:SQ, 2:3], col(a["L0_cond_sty_b1"])),
                (hb[:, 3:5], a["L0_cond_sty_b2"].rearrange("(c p) -> p c", p=P)),
                (ln_gb[:, 0:1], col(a["L0_cond_ln_g"])), (ln_gb[:, 1:2], col(a["L0_cond_ln_b"])),
                (rw[:, :], a["L0_cond_router_w"]),
                (wada[:, :], a["L2_cond_W_ada"]), (bada[:, :], a["L2_cond_b_ada"].rearrange("(c p) -> p c", p=P)),
                (fq[:, :], a["freqs"][:, 0:1]), (ph[:, :], a["freqs"][:, 1:3]),
                (ang[:, 0, :], a["condB_theta"].rearrange("(t b) -> b t", b=BT)),
                (ang[:, 1, :], a["condB_phi"].rearrange("(t b) -> b t", b=BT)),
                (dom4[:, :], a["itok_B_0_15"].rearrange("(t b) -> b t", b=BT)),
                (doww[:, :], a["L3_cond_down_W"]), (upw[:, :], a["L3_cond_up_W"]),
                (exw[:, :, :], a["L3_cond_expert_W"].rearrange("e o a -> o e a")),
                (vecs[:, 0:NX], a["L3_cond_expert_b"].rearrange("e o -> o e")),
                (emt[:, :], a["L3_cond_domain_emb"].rearrange("e o -> o e")),
                (upb[:, :], on_all(a["L3_cond_up_b"], NX + 2)),
                (wq[:, :], a["L2_cond_Wq"]), (wk[:, :], a["L2_cond_Wk"]), (wv[:, :], a["L2_cond_Wv"]), (wo[:, :], a["L2_cond_Wo"]),
                (w1[:, :], a["L2_cond_W1"]), (w2[:, :, :], a["L2_cond_W2"].rearrange("(c p) d -> p c d", p=P)),
                (b1[:, :], a["L2_cond_b1"].rearrange("(c p) -> p c", p=P)),
                (cols[:, 0:1], col(a["L2_cond_bq"])), (cols[:, 1:2], col(a["L2_cond_bk"])), (cols[:, 2:3], col(a["L2_cond_bv"])),
                (cols[:, 3:4], col(a["L2_cond_g2"])), (cols[:, 4:5], col(a["L2_cond_beta2"])),
                (rows[:, 0, :], on_all(a["L2_cond_bo"])), (rows[:, 1, :], on_all(a["L2_cond_b2"])),
                (rows[:, 2, :], on_all(a["L3_cond_ln_gamma"])), (rows[:, 3, :], on_all(a["L3_cond_ln_beta"])),
                (B1E[:, :, :], a["L0_cond_exp_b1"].rearrange("e (c p) -> p e c", p=P)),
            ):
                sp.dma_start(dst, src, allow_slow_non_contiguous=True).then_inc(ld_small, 16)
                n += 1
            for r in range(4):
                sp.dma_start(cols[A * r:A * r + A, 5:6], col(a["L3_cond_down_b"])).then_inc(ld_small, 16)
                n += 1
            assert n == N_SMALL, n
            sp.dma_start(X[:, :, :], x_view).then_inc(ld_x, 16)
            sp.dma_start(W1E[:, :, :], a["L0_cond_exp_w1"].rearrange("e d f -> d e f")).then_inc(ld_exp, 16)
            sp.dma_start(W2E[:, :, :, :], a["L0_cond_exp_w2"].rearrange("e (c p) d -> p e c d", p=P)).then_inc(ld_exp, 16)
            sp.dma_start(maskb[:, :, :], a["mask_Bx1xSxS_bk0"].rearrange("(t b) o q k -> (b o q) t k", b=BT)).then_inc(ld_mask, 16)
            sp.wait_ge(dve_set, D_WUS)
            sp.dma_start(wud[0:NX * A, :].rearrange("(c p) d -> p c d", p=P), wus[:, :, :]).then_inc(st_wu, 16)
            sp.dma_start(wud[NX * A:(NX + 1) * A, :], upT[:, :]).then_inc(st_wu, 16)
            sp.dma_start(B2E[:, :, :].rearrange("p e d -> p (e d)"), on_all(a["L0_cond_exp_b2"].rearrange("e d -> (e d)"))).then_inc(ld_b2, 16)
            sp.wait_ge(zeroed, 1)
            for c in range(SPARE // GT):
                lo = NE * REGION + c * GN
                sp.dma_start(hrows[lo:lo + GN, :].rearrange("(t p) d -> p t d", p=P), hBD[:, 0, :, :]).then_inc(spare_done, 16)
            with sp.Fori(0, NT) as t:
                for b in range(BT):
                    sp.dma_start(BIAS[S * b:S * b + S, bass.ds(t, 1), :, :].rearrange("p o h k -> p (o h) k"),
                                 bias_view[bass.ds(t * BT + b, 1), :, :, :].rearrange("o q h k -> (o q) h k")).then_inc(ld_bias, 16)
            sp.wait_ge(pads_ready, 1)
            for e in range(NE):
                row = sp.value_load(pads[0:1, e:e + 1], min_val=0, max_val=NE * REGION)
                sp.dma_start(hrows[bass.ds(row, P), :], hBD[:, 0, 0, :]).then_inc(pads_done, 16)
            for c in range(2):
                sp.wait_ge(scattered[c], NG // 2 * 16 * 2 * GT)
            sp.wait_ge(listed, 1)
            sp.wait_ge(pads_done, 16 * NE)
            sp.wait_ge(spare_done, 16 * 2)

            def load(place, d):
                row = sp.value_load(row_at[0:1, bass.ds(place.at(d), 1)], min_val=0, max_val=NE * REGION + (SPARE - 1) * P)
                hold(sp, e_T, place.at(d - 4))
                sp.dma_start(tile_in[:, place.slot(d), :], hrows[bass.ds(row, P), :]).then_inc(tile_ld[place.slot(d)], 16)

            def store(place):
                hold(sp, e_yc, place.at(0))
                sp.dma_start(yrows[bass.ds(place.at(0) * P, P), :], tile_out[:, place.slot(0), :]).then_inc(tile_st[place.slot(0)], 16)

            for c in range(4):
                row = sp.value_load(row_at[0:1, c:c + 1], min_val=0, max_val=NE * REGION + (SPARE - 1) * P)
                sp.dma_start(tile_in[:, c, :], hrows[bass.ds(row, P), :]).then_inc(tile_ld[c], 16)
            for i in range(3):
                load(Place(0, i - 2), 4)
            with sp.Fori(0, (LIST - 7) // 4) as j:
                for q in range(4):
                    load(Place(j, q + 1), 4)
                    store(Place(j, q - 2))
            for i in range((LIST - 7) // 4 * 4, LIST):
                store(Place(i // 4, i % 4 - 2))
            with sp.Fori(0, NG // 2) as i:
                for p in range(2):
                    g = i * 2 + p
                    hold(sp, o_b, g)
                    sp.dma_start(out_view[:, bass.ds(g * GT, GT), :], ot[:, p, :, :]).then_inc(out_done[p], 16)
            for p in range(2):
                sp.wait_ge(out_done[p], 16 * (NG // 2) + 16)

        @block.gpsimd
        def _(pool):
            n = [0]

            def step(ins):
                n[0] += 1
                ins.then_inc(pool_set, 1)
                pool.wait_ge(pool_set, n[0])

            def band(ap, base, pattern, cm):
                step(pool.affine_select(out=ap, in_=ap, compare_op=ALU.is_ge, fill=0.0, base=base,
                                        pattern=pattern, channel_multiplier=cm))

            for sig in (slot_free, o_b):
                sig.open(pool)
            for done in out_done:
                pool.sem_inc(done, 16)
            step(pool.memset(ident[:, :], 0.0))
            step(pool.affine_select(out=ident[:, :], in_=ident[:, :], compare_op=ALU.not_equal, fill=1.0,
                                    base=0, pattern=[[-1, P]], channel_multiplier=1))
            step(pool.iota(iot[:, :], [[0, 1]], base=0, channel_multiplier=1))
            for q in range(4):
                step(pool.iota(acol[A * q:A * q + A, :], [[0, 1]], base=0, channel_multiplier=1))
            step(pool.iota(desc[:, :], [[-1, NE]], base=NE, channel_multiplier=0))
            step(pool.memset(half[:, :], -0.5))
            step(pool.memset(ones[:, :], 1.0))
            step(pool.memset(both[:, :, :], 0.0))
            step(pool.memset(upper[:, :], 1.0))
            band(upper[:, :], -1, [[1, P]], -1)
            step(pool.iota(seqi[:, :], [[1, LIST]], base=0, channel_multiplier=0))
            step(pool.iota(regi[:, :], [[REGION, NE]], base=0, channel_multiplier=0))
            step(pool.memset(hm16[:, :], 1.0))
            band(hm16[:, :], 0, [[-HD, H]], 1)
            band(hm16[:, :], HD - 1, [[HD, H]], -1)
            step(pool.memset(vm[:, :, :, :], 1.0))
            band(vm[:, :, :, :], 0, [[0, BT], [0, HJ], [-S, HP]], 1)
            band(vm[:, :, :, :], S - 1, [[0, BT], [0, HJ], [S, HP]], -1)
            step(pool.memset(e4[:, :], 1.0))
            band(e4[:, :], 0, [[1, P]], -S)
            band(e4[:, :], S - 1, [[-1, P]], S)
            assert n[0] == P_SET, n[0]
            pool.memset(hBD[:, :, :, :], 0.0).then_inc(zeroed, 1)

            def scatter(g, c):
                hold(pool, a_row, g)
                hold_apart(pool, idx_ready, g)
                for t in range(GT):
                    for k in range(2):
                        pool.indirect_dma_start(out=hrows[:, :], out_offset=bass.IndirectOffsetOnAxis(ap=pos_g[:, c, k, t:t + 1], axis=0),
                                                in_=hrow[:, c, t, :], in_offset=None).then_inc(scattered[c], 16)

            for c in range(2):
                scatter(c, c)
            with pool.Fori(0, (NG - 2) // 2) as i:
                for c in range(2):
                    pool.wait_ge(scattered[c], (i + 1) * (16 * 2 * GT))
                    pool.sem_inc(slot_free.sem)
                    scatter(i * 2 + c + 2, c)
            pool.wait_ge(ld_mask, 16)
            step(pool.tensor_copy(maskn[:, :, :], maskb[:, :, :]))
            step(pool.tensor_scalar(maskn[:, :, :], maskn[:, :, :], MASKED, 0.0, ALU.mult, ALU.add))
            pool.wait_ge(dve_set, D_WIDX)
            pool.wait_ge(st_wu, 32)
            for t in range(NT):
                pool.indirect_dma_start(out=WSEL[:, t, :], out_offset=None, in_=wud[:, :],
                                        in_offset=bass.IndirectOffsetOnAxis(ap=widx[:, t:t + 1], axis=0)).then_inc(ld_wsel, 16)
            pool.wait_ge(ld_bias, 16 * B)
            with pool.Fori(0, NG) as g:
                for s in range(GT):
                    bt = BIAS[:, bass.ds(g * GT + s, 1), :, :].rearrange("p o h k -> p (o h) k")
                    mk = maskn[:, bass.ds(g * GT + s, 1), :].broadcast_to([P, H, S])
                    pool.tensor_tensor(bt, bt, mk, ALU.add).then_inc(bias_masked.sem, 1)
            hold(pool, e_y, LIST - 1)
            for c in range(2):
                pool.tensor_copy(VB[:, c, :, :, HP * HD:GV], vm[:, :, :, :]).then_inc(vb_ones, 1)
            for c in range(4):
                pool.wait_ge(tile_st[c], 16 * ((LIST - 1 - c) // 4 + 1) + 16)

            def gather(g):
                hold_apart(pool, y_idx, g)
                for t in range(GT):
                    for k in range(2):
                        pool.indirect_dma_start(out=Y[:, k, t, :], out_offset=None, in_=yrows[:, :],
                                                in_offset=bass.IndirectOffsetOnAxis(ap=pos_g[:, 0, k, t:t + 1], axis=0)).then_inc(y_ld.sem, 16)

            gather(0)

            def iteration(g, p, prev, this, nxt, more):
                def subtract(g, s):
                    hold(pool, c_mx, g, s + 1)
                    c = s % 2
                    pool.tensor_tensor(Sc[:, c, :, :], Sc[:, c, :, :], bc(mx[:, c, :], S), ALU.subtract).then_inc(c_sub.sem, 1)

                if nxt:
                    for s in range(GT):
                        xt = X[:, bass.ds((g + 1) * GT + s, 1), :].rearrange("p o (w h e) -> p (o w) h e", h=2, e=2)
                        sw = big[:, 0, s * D:(s + 1) * D].rearrange("p (w h e) -> p w h e", h=2, e=2)
                        s4 = S4[:, bass.ds((g + 1) * GT + s, 1), :].broadcast_to([P, D // 4, 4]).rearrange("p w (h e) -> p w h e", h=2)
                        if s == 0:
                            hold(pool, r_x, g + 1, 0)
                            hold(pool, y_add, g + 1)
                        for e in range(2):
                            ins = pool.tensor_tensor(sw[:, :, :, e], xt[:, :, :, 1 - e], s4[:, :, :, e], ALU.mult)
                        ins.then_inc(r_swp.sem, 1)
                if prev:
                    hold(pool, d_st, g - 1)
                    pool.tensor_tensor(rstd2[:, :], ve2[:, :], half[:, 0:GT], ALU.pow).then_inc(d_rstd.sem, 1)
                if this:
                    subtract(g, 1)
                if more:
                    gather(g + 2)
                if prev:
                    pool.tensor_tensor(x2b[:, :, :], x2[:, :, :], rows[:, 1:2, :].broadcast_to([P, GT, D]), ALU.add).then_inc(d_x2b.sem, 1)
                if this:
                    subtract(g, 2)
                if nxt:
                    hold(pool, c_st, g + 1)
                    pool.tensor_tensor(rstd[:, :], ve[:, :], half[:, 0:GT], ALU.pow).then_inc(c_rstd.sem, 1)
                    hold(pool, c_xmul, g + 1)
                    pool.tensor_tensor(xmT[:, 1 - p, :].rearrange("d (b s) -> d b s", s=S), big[:, 1, :].rearrange("d (b s) -> d b s", s=S),
                                       bc(shiftT[:, bass.ds((g + 1) * GB, GB)], S), ALU.add).then_inc(c_xm.sem, 1)
                if this:
                    subtract(g, 3)
                if prev:
                    hold(pool, f_u, g - 1, 0)
                    pool.tensor_copy(ohx[:, :, :].rearrange("e t (b s) -> e (t b) s", s=S),
                                     bc(ohC[:, bass.ds((g - 1) * GB, GB)], S)).then_inc(f_oh.sem, 1)
                if nxt:
                    subtract(g + 1, 0)
                if prev:
                    hold(pool, o_st, g - 1)
                    pool.tensor_tensor(rstd3[:, :], ve3[:, :], half[:, 0:GT], ALU.pow).then_inc(o_rstd.sem, 1)
                    hold(pool, o_g, g - 1)
                    pool.wait_ge(out_done[1 - p], (g - 1 - (1 - p)) * 8 + 16)
                    pool.tensor_tensor(ot[:, 1 - p, :, :], z[:, :, :], rows[:, 3:4, :].broadcast_to([P, GT, D]), ALU.add).then_inc(o_b.sem, 1)

            pipeline(pool, iteration)

        @block.scalar
        def _(act):
            n = [0]

            def step(ins):
                n[0] += 1
                ins.then_inc(act_set, 1)

            for sig in (a_row, e_in, e_relu):
                sig.open(act)
            act.wait_ge(ld_small, 16 * N_SMALL)
            act.wait_ge(dve_set, D_ANG)
            step(act.activation(sB[:, :], sA[:, :], ACT.Sin))
            step(act.activation(trk[:, :, :], tr[:, :, :], ACT.Sin))
            act.wait_ge(act_set, 2)
            step(act.activation(sC[:, :], sB[:, :], ACT.Tanh, scale=0.5))
            act.wait_ge(pe_set, E_HYP1)
            step(act.activation(gammaT[:, :], W[0][:, 0:B], ACT.Relu, bias=hb[:, 0:1]))
            act.wait_ge(pe_set, E_HYP2)
            step(act.activation(betaT[:, :], W[1][:, 0:B], ACT.Identity, bias=hb[:, 1:2]))
            act.wait_ge(pe_set, E_STY1)
            step(act.activation(idf[0:SQ, :], W[0][0:SQ, 0:B], ACT.Relu, bias=hb[0:SQ, 2:3]))
            act.wait_ge(pe_set, E_STY2)
            step(act.activation(betaT[:, :], W[2][:, 0:B], ACT.Identity, bias=hb[:, 4:5]))
            step(act.activation(gammaT[:, :], W[1][:, 0:B], ACT.Identity, bias=hb[:, 3:4]))
            act.wait_ge(act_set, 8)
            step(act.activation(sD[:, :], gammaT[:, :], ACT.Abs))
            act.wait_ge(act_set, 9)
            step(act.activation(sD[:, :], sD[:, :], ACT.Exp, scale=-1.0))
            act.wait_ge(act_set, 10)
            step(act.activation(sD[:, :], sD[:, :], ACT.Ln, bias=1.0))
            assert n[0] == A_SET, n[0]
            def normalised(g):
                hold(act, a_st, g)
                act.activation(rstd[:, :], ve[:, :], ACT.Sqrt).then_inc(a_sqrt.sem, 1)
                hold(act, a_T, g)
                act.activation(hA[:, :], W[3][:, :], ACT.Identity, bias=ln_gb[:, 1:2], scale=ln_gb[:, 0:1]).then_inc(a_h.sem, 1)

            def over_time(g):
                hold(act, a_dve, g, 2)
                act.activation(big[:, 0, :], hA[:, :], ACT.Square).then_inc(a_sq.sem, 1)
                hold(act, a_dve, g, 4)
                act.activation(vs[:, 2, :], vs[:, 1, :], ACT.Sqrt).then_inc(a_rv.sem, 1)

            def copy_rows(g, c):
                hold(act, a_rT, g)
                hold(act, slot_free, g - 2)
                act.activation(hrow[:, c, :, :].rearrange("p t d -> p (t d)"), W[c][:, :], ACT.Copy).then_inc(a_row.sem, 1)

            normalised(0)
            over_time(0)
            normalised(1)
            with act.Fori(0, (NG - 2) // 2) as i:
                for c in range(2):
                    copy_rows(i * 2 + c, c)
                    over_time(i * 2 + c + 1)
                    normalised(i * 2 + c + 2)
            copy_rows(NG - 2, (NG - 2) % 2)
            over_time(NG - 1)
            copy_rows(NG - 1, (NG - 1) % 2)
            act.wait_ge(gate_dve, 1)
            act.activation(g2[:, :], m2[:, :], ACT.Exp).then_inc(gate_act, 1)

            def step(place, ahead, first, middle, last):
                if ahead:
                    hold(act, e_T, place.at(1))
                    hold(act, e_h, place.at(-1))
                    act.activation(tile_inT[:, place.slot(1) % 2, :], PS[:, 2 + place.slot(1) % 2, 0:P], ACT.Copy).then_inc(e_in.sem, 1)
                if middle:
                    hold(act, e_add, place.at(-1))
                    hd = hid[:, 0, 2 + place.slot(-1) % 2, :]
                    act.activation(hd, hd, ACT.Relu).then_inc(e_relu.sem, 1)
            tile_pipeline(act, step)
            act.wait_ge(vb_ones, 2)

            def iteration(g, p, prev, this, nxt, more):
                def copy_pT(s):
                    hold(act, c_pT, g, s + 1)
                    read(act.activation(PT[:, :, :].rearrange("p j q -> p (j q)"), bank(f"P{s}")[:, :], ACT.Copy), f"P{s}")

                def copy_v(g, s):
                    hold(act, c_v, g, s + 1)
                    read(act.activation(VB[:, s % 2, :, :, 0:HP * HD], bank(f"V{s}")[:, :].rearrange("p (b j v) -> p b j v", b=BT, j=HJ), ACT.Copy), f"V{s}")

                def exps(g, s):
                    hold(act, c_sub, g, s + 1)
                    act.activation(Sc[:, s % 2, :, :], Sc[:, s % 2, :, :], ACT.Exp).then_inc(c_exp.sem, 1)

                def gelu(c):
                    hold(act, d_f, g - 1, c + 1)
                    read(act.activation(hid[:, 0, c, :], bank(f"F{c}")[:, :], ACT.Gelu_apprx_sigmoid, bias=b1[:, c:c + 1]), f"F{c}")

                if prev:
                    hold(act, d_cT, g - 1)
                    read(act.activation(ctxT[:, :], bank("CT")[:, :], ACT.Identity, bias=cols[:, 2:3]), "CT")
                if this:
                    copy_pT(0)
                    copy_v(g, 1)
                    exps(g, 1)
                    copy_pT(1)
                    copy_v(g, 2)
                if prev:
                    hold(act, t2, g - 1)
                    read(act.activation(h2T[:, :], bank("T2")[:, :], ACT.Identity, bias=cols[:, 4:5], scale=cols[:, 3:4]), "T2")
                if this:
                    exps(g, 2)
                if prev:
                    for c in range(FC):
                        gelu(c)
                if this:
                    copy_pT(2)
                    copy_v(g, 3)
                    exps(g, 3)
                if nxt:
                    hold(act, qp, g + 1)
                    read(act.activation(QT[:, :], bank("Q")[:, :], ACT.Identity, bias=bqs[:, :], scale=HD ** -0.5), "Q")
                    hold(act, kp, g + 1)
                    for h in range(HP):
                        ins = act.activation(KM[:, :, h, :], bank("K")[:, :].rearrange("d (b s) -> d b s", s=S), ACT.Identity,
                                             bias=bkm[:, h:h + 1], scale=hm4[:, h:h + 1])
                    read(ins, "K")
                if this:
                    copy_pT(3)
                if prev:
                    hold(act, t3, g - 1)
                    read(act.activation(X3T[:, :], bank("T3")[:, :], ACT.Copy), "T3")
                    hold(act, dp, g - 1)
                    for b in range(BT):
                        ins = act.activation(hBD[S * b:S * b + S, 0, :, S * b:S * b + S],
                                             bank("D")[S * b:S * b + S, :].rearrange("p (t q) -> p t q", q=P)[:, :, S * b:S * b + S],
                                             ACT.Gelu, bias=cols[S * b:S * b + S, 5:6])
                    read(ins, "D")
                if nxt:
                    copy_v(g + 1, 0)
                    exps(g + 1, 0)

            pipeline(act, iteration)

        @block.vector
        def _(dve):
            n = [0]

            def step(ins):
                n[0] += 1
                ins.then_inc(dve_set, 1)
                dve.wait_ge(dve_set, n[0])

            def wrap(ap, k, extra):
                step(dve.tensor_scalar(k, ap, 1 / (2 * PI), extra, ALU.mult, ALU.add))
                step(dve.tensor_scalar(k, k, ROUND, -ROUND, ALU.add, ALU.add))
                step(dve.scalar_tensor_tensor(out=ap, in0=k, scalar=-TWO_PI_HI, in1=ap, op0=ALU.mult, op1=ALU.add))
                step(dve.scalar_tensor_tensor(out=ap, in0=k, scalar=-TWO_PI_LO, in1=ap, op0=ALU.mult, op1=ALU.add))

            for sig in (placed, e_hc, e_add, e_yc, r_x, c_sc):
                sig.open(dve)
            for done in tile_st:
                dve.sem_inc(done, 16)
            dve.wait_ge(ld_small, 16 * N_SMALL)
            dve.wait_ge(pool_set, P_SET)
            step(dve.tensor_copy(iof[:, :], iot[:, :]))
            step(dve.tensor_copy(acf[:, :], acol[:, :]))
            step(dve.tensor_copy(dsf[:, :], desc[:, :]))
            step(dve.tensor_copy(seq[:, :], seqi[:, :]))
            step(dve.tensor_copy(regf[:, :], regi[:, :]))
            step(dve.tensor_copy(base[:, :], regi[:, :]))
            step(dve.tensor_copy(idf[0:NS, :], ids[0:NS, :]))
            step(dve.tensor_scalar(onehot[:, :], idf[0:NS, :], iof[0:NS, :], None, ALU.is_equal))
            assert n[0] == D_ONEHOT, n[0]
            step(dve.tensor_copy(sB[:, :], ids2[:, :]))
            step(dve.tensor_scalar(sB[:, :], sB[:, :], 0.01, 4000.0, ALU.mult, ALU.mult))
            step(dve.tensor_scalar(sA[:, :], sB[:, :], fq[:, :], None, ALU.mult))
            wrap(sA[:, :], sB[:, :], ph[:, 0:1])
            step(dve.tensor_scalar(sA[:, :], sA[:, :], ph[:, 1:2], PI, ALU.add, ALU.min))
            step(dve.tensor_scalar(sA[:, :], sA[:, :], -PI, None, ALU.max))
            for k in range(4):
                step(dve.tensor_copy(tr[:, k, :], ang[:, k // 2, :]))
                wrap(tr[:, k, :], trk[:, k, :], 0.25 * (k % 2))
                step(dve.tensor_scalar(tr[:, k, :], tr[:, k, :], PI / 2 * (k % 2), PI, ALU.add, ALU.min))
                step(dve.tensor_scalar(tr[:, k, :], tr[:, k, :], -PI, None, ALU.max))
            assert n[0] == D_ANG, n[0]
            step(dve.tensor_reduce(out=hm4[:, :], in_=hm16[:, :].rearrange("p (j h) -> p h j", h=HP), axis=AX.X, op=ALU.add))
            step(dve.tensor_scalar(bkm[:, :], hm4[:, :], cols[:, 1:2], None, ALU.mult))
            step(dve.tensor_scalar(bqs[:, :], cols[:, 0:1], HD ** -0.5, None, ALU.mult))
            step(dve.tensor_tensor(vecs[:, 0:NX], vecs[:, 0:NX], emt[:, :], ALU.add))
            step(dve.tensor_copy(vecs[:, NX:NX + 1], emt[:, 0:1]))
            step(dve.tensor_copy(vecs[:, NX + 1:NX + 2], emt[:, NX - 1:NX]))
            step(dve.tensor_copy(dom4f[:, :], dom4[:, :]))
            step(dve.memset(wv4[:, :, :, :, :], 0.0))
            for h in range(HP):
                step(dve.tensor_copy(wv4[:, h, :, h, :], wv[:, :].rearrange("d (j h v) -> d j h v", j=HJ, h=HP)[:, :, h, :]))
            assert n[0] == D_TAB, n[0]
            dve.wait_ge(pe_set, E_SE)
            step(dve.tensor_copy(sD[0:SE, :], W[3][0:SE, 0:B]))
            dve.wait_ge(pe_set, E_DT)
            step(dve.tensor_copy(dwT[:, :, :], PS[:, 0:1, 0:A].broadcast_to([P, 4, A])))
            step(dve.tensor_copy(upT[:, :], PS[0:A, 1, 0:D]))
            assert n[0] == D_UPT, n[0]
            dve.wait_ge(act_set, 3)
            step(dve.scalar_tensor_tensor(out=sC[:, :], in0=sC[:, :], scalar=1.0, in1=sB[:, :], op0=ALU.add, op1=ALU.mult))
            step(dve.tensor_scalar(sC[:, :], sC[:, :], 0.5, None, ALU.mult))
            assert n[0] == D_SILU, n[0]
            dve.wait_ge(pe_set, E_ADA)
            step(dve.tensor_scalar(scaleT[:, :], PS[:, 2, 0:B], bada[:, 0:1], 1.0, ALU.add, ALU.add))
            step(dve.tensor_scalar(shiftT[:, :], PS[:, 3, 0:B], bada[:, 1:2], None, ALU.add))
            dve.wait_ge(pe_set, E_WU)
            step(dve.tensor_copy(wus[:, :, :].rearrange("p c d -> p (c d)"), PS[:, 0, :]))
            assert n[0] == D_WUS, n[0]
            dve.wait_ge(pe_set, E_CT)
            step(dve.tensor_tensor(CT[:, :], PS[0:NX + 2, 1, 0:D], upb[:, :], ALU.add))
            dve.wait_ge(pe_set, E_ROT)
            rot = PS[:, 2, 0:5 * NT].rearrange("p (k t) -> p k t", k=5)
            for k, (dst, src, sign) in enumerate(((S4, 0, 1), (S4, 0, -1), (S4, 2, 1), (S4, 2, -1), (C4, 1, 1), (C4, 1, 1), (C4, 3, 1), (C4, 3, 1))):
                step(dve.tensor_scalar(dst[:, :, k % 4], rot[:, src, :], float(sign), None, ALU.mult))
            step(dve.tensor_copy(domx[:, :], rot[:, 4, :]))
            step(dve.tensor_scalar(domy[:, :], domx[:, :], 0.0, None, ALU.is_ge))
            step(dve.scalar_tensor_tensor(out=domy[:, :], in0=domx[:, :], scalar=float(NX), in1=domy[:, :], op0=ALU.is_lt, op1=ALU.mult))
            step(dve.scalar_tensor_tensor(out=domx[:, :], in0=domx[:, :], scalar=-float(NX), in1=domy[:, :], op0=ALU.add, op1=ALU.mult))
            step(dve.tensor_scalar(domx[:, :], domx[:, :], float(NX), float(A), ALU.add, ALU.mult))
            step(dve.tensor_scalar(widx[:, :], domx[:, :], acf[:, :], None, ALU.add))
            assert n[0] == D_WIDX, n[0]
            step(dve.tensor_copy(sB[0:NX + 2, :], ids3[:, :]))
            step(dve.tensor_scalar(sA[0:NX + 2, :], sB[0:NX + 2, :], 0.0, float(NX + 1), ALU.is_lt, ALU.mult))
            step(dve.scalar_tensor_tensor(out=sA[0:NX + 2, :], in0=sB[0:NX + 2, :], scalar=float(NX) - 0.5, in1=sA[0:NX + 2, :], op0=ALU.is_gt, op1=ALU.add))
            step(dve.tensor_scalar(sB[0:NX + 2, :], sB[0:NX + 2, :], -1.0, float(NX), ALU.max, ALU.min))
            step(dve.tensor_tensor(sA[0:NX + 2, :], sA[0:NX + 2, :], sB[0:NX + 2, :], ALU.add))
            step(dve.tensor_scalar(ohC[:, :], sA[0:NX + 2, :], iof[0:NX + 2, :], None, ALU.is_equal))
            dve.wait_ge(act_set, A_SET)
            step(dve.scalar_tensor_tensor(out=gammaT[:, :], in0=gammaT[:, :], scalar=0.0, in1=sD[:, :], op0=ALU.max, op1=ALU.add))
            step(dve.tensor_scalar(gammaT[:, :], gammaT[:, :], 1e-8, None, ALU.add))
            assert n[0] == D_SET, n[0]

            def stats(src, sig, g, st=st, mv=mv, ve=ve):
                for s in range(GT):
                    dve.bn_stats(st[:, s, :], src(s)).then_inc(sig.sem, 1)
                hold_apart(dve, sig, g, GT)
                for s in range(GT):
                    dve.bn_aggr(mv[:, s, :], st[:, s, :]).then_inc(sig.sem, 1)
                hold_apart(dve, sig, g, 2 * GT)
                dve.tensor_scalar(ve[:, :], mv[:, :, 1], 1e-5, None, ALU.add).then_inc(sig.sem, 1)

            def normalise(dst, src, sig, g, mv=mv, rstd=rstd):
                for s in range(GT):
                    dve.tensor_scalar(dst(s), src(s), mv[:, s, 0:1], rstd[:, s:s + 1], ALU.subtract, ALU.mult).then_inc(sig.sem, 1)

            def tile_of(g, s):
                return X[:, bass.ds(g * GT + s, 1), :].rearrange("p o d -> p (o d)")

            dve.wait_ge(ld_x, 16)
            def normalised(g):
                stats(lambda s: tile_of(g, s), a_st, g)
                hold(dve, a_sqrt, g)
                dve.reciprocal(rstd[:, :], rstd[:, :]).then_inc(a_rstd.sem, 1)
                hold(dve, a_rstd, g)
                hold(dve, a_T, g - 1)
                normalise(lambda s: xn[:, s, :], lambda s: tile_of(g, s), a_xn, g)

            seg = hA[:, :].rearrange("d (b s) -> d b s", s=S)

            def centre(g):
                hold(dve, a_h, g)
                dve.tensor_reduce(out=vs[:, 0, :], in_=seg, axis=AX.X, op=ALU.add).then_inc(a_dve.sem, 1)
                hold(dve, a_dve, g, 1)
                dve.scalar_tensor_tensor(out=seg, in0=bc(vs[:, 0, :], S), scalar=-1.0 / S, in1=seg, op0=ALU.mult, op1=ALU.add).then_inc(a_dve.sem, 1)

            def variance(g):
                hold(dve, a_sq, g)
                dve.tensor_reduce(out=vs[:, 1, :], in_=big[:, 0, :].rearrange("d (b s) -> d b s", s=S), axis=AX.X, op=ALU.add).then_inc(a_dve.sem, 1)
                hold(dve, a_dve, g, 3)
                dve.tensor_scalar(vs[:, 1, :], vs[:, 1, :], 1.0 / S, 1e-8, ALU.mult, ALU.add).then_inc(a_dve.sem, 1)

            def styled(g):
                hold(dve, a_rv, g)
                dve.reciprocal(vs[:, 3, :], vs[:, 2, :]).then_inc(a_dve.sem, 1)
                hold(dve, a_dve, g, 5)
                dve.tensor_tensor(vs[:, 3, :], vs[:, 3, :], gammaT[:, bass.ds(g * GB, GB)], ALU.mult).then_inc(a_dve.sem, 1)
                hold(dve, a_dve, g, 6)
                dve.tensor_tensor(seg, seg, bc(vs[:, 3, :], S), ALU.mult).then_inc(a_dve.sem, 1)
                hold(dve, a_dve, g, 7)
                hold(dve, a_rT, g - 1)
                dve.tensor_tensor(hTw[:, 0, :].rearrange("d (b s) -> d b s", s=S), seg, bc(betaT[:, bass.ds(g * GB, GB)], S), ALU.add).then_inc(a_dve.sem, 1)

            def pick(g, k, ins):
                ins.then_inc(best.sem, 1)
                dve.wait_ge(best.sem, best.upto(g, k))

            def choose(g, k, m, which):
                mval = m[:, bass.ds(g * GT, GT)]
                pick(g, k, dve.tensor_reduce(out=mval, in_=Lg, axis=AX.X, op=ALU.max))
                pick(g, k + 1, dve.tensor_tensor(ta, Lg, bc(mval, NE), ALU.is_equal))
                pick(g, k + 2, dve.tensor_tensor(ta, ta, dsf[:, :].unsqueeze(1).broadcast_to([P, GT, NE]), ALU.mult))
                pick(g, k + 3, dve.tensor_reduce(out=mw[:, :], in_=ta, axis=AX.X, op=ALU.max))
                pick(g, k + 4, dve.tensor_tensor(sel[:, which, bass.ds(g * GT, GT), :], ta, bc(mw[:, :], NE), ALU.is_equal))

            def best_two(g):
                hold(dve, a_lg, g)
                pick(g, 1, dve.tensor_copy(Lg.rearrange("p t e -> p (t e)"), W[2][:, bass.ds(g * GT * NE, GT * NE)]))
                choose(g, 2, m1, 0)
                pick(g, 7, dve.scalar_tensor_tensor(out=Lg, in0=sel[:, 0, bass.ds(g * GT, GT), :], scalar=MASKED, in1=Lg, op0=ALU.mult, op1=ALU.add))
                choose(g, 8, m2, 1)
                pick(g, 13, dve.tensor_tensor(both[:, 0:GT, :], sel[:, 0, bass.ds(g * GT, GT), :], sel[:, 1, bass.ds(g * GT, GT), :], ALU.add))

            def place_rows(g, c):
                hold(dve, a_pos, g)
                dve.tensor_tensor(pf, PS[:, 0, 0:GT * NE].rearrange("p (t e) -> p t e", e=NE), base[:, :].unsqueeze(1).broadcast_to([P, GT, NE]), ALU.add).then_inc(placed.sem, 1)
                dve.wait_ge(placed.sem, placed.upto(g, 1))
                dve.tensor_tensor(picked, sel[:, :, bass.ds(g * GT, GT), :], pf.unsqueeze(1).broadcast_to([P, 2, GT, NE]), ALU.mult).then_inc(placed.sem, 1)
                dve.tensor_tensor(base[:, :], PS[:, 0, GT * NE:(GT + 1) * NE], base[:, :], ALU.add).then_inc(placed.sem, 1)
                dve.wait_ge(placed.sem, placed.upto(g, 3))
                dve.tensor_reduce(out=posf[:, :, bass.ds(g * GT, GT)], in_=picked, axis=AX.X, op=ALU.add).then_inc(placed.sem, 1)
                dve.wait_ge(placed.sem, placed.upto(g, 4))
                hold(dve, slot_free, g - 2)
                dve.sem_inc(passed["DVE"])
                dve.tensor_copy(pos_g[:, c, :, :], posf[:, :, bass.ds(g * GT, GT)]).then_inc(idx_ready.sem, 1)

            normalised(0)
            centre(0)
            variance(0)
            styled(0)
            normalised(1)
            with dve.Fori(0, (NG - 2) // 2) as i:
                for c in range(2):
                    g = i * 2 + c
                    centre(g + 1)
                    best_two(g)
                    variance(g + 1)
                    place_rows(g, c)
                    styled(g + 1)
                    normalised(g + 2)
            centre(NG - 1)
            best_two(NG - 2)
            variance(NG - 1)
            place_rows(NG - 2, 0)
            styled(NG - 1)
            best_two(NG - 1)
            place_rows(NG - 1, 1)

            k = [0]

            def then(ins):
                k[0] += 1
                ins.then_inc(listed_dve, 1)
                dve.wait_ge(listed_dve, k[0])

            dve.tensor_copy(pads[:, :], base[:, :]).then_inc(pads_ready, 1)
            then(dve.tensor_tensor(tiles[:, :], base[:, :], regf[:, :], ALU.subtract))
            then(dve.tensor_scalar(tiles[:, :], tiles[:, :], 1.0 / P, (P - 1) / (2.0 * P), ALU.mult, ALU.add))
            then(dve.tensor_scalar(tiles[:, :], tiles[:, :], ROUND, -ROUND, ALU.add, ALU.add))
            then(dve.tensor_copy(ends[:, 0:1], tiles[:, 0:1]))
            for e in range(1, NE):
                then(dve.tensor_tensor(ends[:, e:e + 1], ends[:, e - 1:e], tiles[:, e:e + 1], ALU.add))
            then(dve.tensor_scalar(jump[:, :], tiles[:, :], -float(P), float(REGION), ALU.mult, ALU.add))
            then(dve.tensor_tensor(passed_end, bc(seq[:, :], NE), ends[:, :].unsqueeze(1).broadcast_to([P, LIST, NE]), ALU.is_ge))
            then(dve.tensor_reduce(out=listf, in_=passed_end, axis=AX.X, op=ALU.add))
            then(dve.tensor_scalar(listf, listf, float(NE - 1), None, ALU.min))
            then(dve.tensor_copy(expert_at[:, :], listf))
            then(dve.memset(pairf, 0.0))
            then(dve.tensor_scalar(pairf[:, 0:LIST], listf, float(NE), None, ALU.mult))
            then(dve.tensor_tensor(pairf[:, 3:LIST + 3], pairf[:, 3:LIST + 3], listf, ALU.add))
            then(dve.tensor_copy(pair_at[:, :], pairf))
            quad = pairf[:, 3:LIST].rearrange("p (j q) -> p j q", q=4)
            for q in range(1, 4):
                then(dve.scalar_tensor_tensor(out=quad[:, :, 0], in0=quad[:, :, q], scalar=float(NE ** (2 * q)), in1=quad[:, :, 0], op0=ALU.mult, op1=ALU.add))
            then(dve.tensor_copy(eight_at[:, :], quad[:, :, 0]))
            then(dve.tensor_tensor(passed_end, passed_end, jump[:, :].unsqueeze(1).broadcast_to([P, LIST, NE]), ALU.mult))
            then(dve.tensor_reduce(out=listf, in_=passed_end, axis=AX.X, op=ALU.add))
            then(dve.scalar_tensor_tensor(out=listf, in0=seq[:, :], scalar=float(P), in1=listf, op0=ALU.mult, op1=ALU.add))
            dve.tensor_copy(row_at[:, :], listf).then_inc(listed, 1)
            then(dve.tensor_tensor(ends[:, :], ends[:, :], tiles[:, :], ALU.subtract))
            then(dve.scalar_tensor_tensor(out=ends[:, :], in0=ends[:, :], scalar=float(P), in1=regf[:, :], op0=ALU.mult, op1=ALU.subtract))
            then(dve.tensor_tensor(moves, sel, ends[:, :].unsqueeze(1).unsqueeze(1).broadcast_to([P, 2, NT, NE]), ALU.mult))
            then(dve.tensor_reduce(out=moved[:, :, :], in_=moves, axis=AX.X, op=ALU.add))
            then(dve.tensor_tensor(moved[:, :, :], moved[:, :, :], posf[:, :, :], ALU.add))
            then(dve.tensor_copy(pos[:, :, :], moved[:, :, :]))
            then(dve.tensor_tensor(m2[:, :], m2[:, :], m1[:, :], ALU.subtract))
            dve.sem_inc(gate_dve, 1)
            dve.wait_ge(gate_act, 1)
            then(dve.tensor_scalar(g1[:, :], g2[:, :], 1.0, None, ALU.add))
            then(dve.reciprocal(g1[:, :], g1[:, :]))
            then(dve.tensor_tensor(g2[:, :], g2[:, :], g1[:, :], ALU.mult))
            dve.wait_ge(ld_b2, 16)

            def step(place, ahead, first, middle, last):
                if first:
                    c = place.slot(0) % 2
                    hold(dve, e_h, place.at(0))
                    hold(dve, e_hT, place.at(-2))
                    dve.tensor_copy(hid[:, 0, c, :], W[c][:, :]).then_inc(e_hc.sem, 1)
                if middle:
                    c = place.slot(-1) % 2
                    expert = dve.value_load(expert_at[0:1, bass.ds(place.at(-1), 1)], min_val=0, max_val=NE - 1)
                    hold(dve, e_hT, place.at(-1))
                    hold_apart(dve, e_y, place.at(-3))
                    dve.tensor_tensor(hid[:, 0, 2 + c, :].rearrange("p (c n) -> p c n", c=FC), PS[:, c, :].rearrange("p (c n) -> p c n", c=FC),
                                      bc(B1E[:, bass.ds(expert, 1), :].rearrange("p o c -> p (o c)"), P), ALU.add).then_inc(e_add.sem, 1)
                if last:
                    c = place.slot(-2)
                    expert = dve.value_load(expert_at[0:1, bass.ds(place.at(-2), 1)], min_val=0, max_val=NE - 1)
                    hold(dve, e_y, place.at(-2))
                    dve.wait_ge(tile_st[c], place.round(-2) * 16 + 16)
                    dve.sem_inc(passed["DVE"])
                    dve.tensor_tensor(tile_out[:, c, :], W[2 + c % 2][:, 0:P], B2E[:, bass.ds(expert, 1), :].rearrange("p o d -> p (o d)"), ALU.add).then_inc(e_yc.sem, 1)

            tile_pipeline(dve, step)
            hold(dve, e_y, LIST - 1)

            def add_experts(g):
                hold(dve, y_ld, g)
                for k, gate in enumerate((g1, g2)):
                    if k:
                        hold(dve, y_add, g, 1)
                    for s in range(GT):
                        ins = dve.scalar_tensor_tensor(out=tile_of(g, s), in0=Y[:, k, s, :], scalar=gate[:, bass.ds(g * GT + s, 1)], in1=tile_of(g, s),
                                                       op0=ALU.mult, op1=ALU.add)
                    ins.then_inc(y_add.sem, 1)

            def next_rows(g):
                dve.tensor_copy(pos_g[:, 0, :, :], pos[:, :, bass.ds(g * GT, GT)]).then_inc(y_idx.sem, 1)

            next_rows(0)
            add_experts(0)
            hold(dve, y_add, 0)
            dve.sem_inc(passed["DVE"])
            next_rows(1)
            hold(dve, bias_masked, NG - 1)

            def iteration(g, p, prev, this, nxt, more):
                def scores(g, s):
                    hold(dve, c_qk, g, s + 1)
                    sc = Sc[:, s % 2, :, :]
                    dve.tensor_tensor(sc.rearrange("p (j h) k -> p j (h k)", j=HJ), PS[:, :, 0:P],
                                      BIAS[:, bass.ds(g * GT + s, 1), :, :].rearrange("p o (j h) k -> p (o j) (h k)", j=HJ), ALU.add).then_inc(c_sc.sem, 1)
                    hold(dve, c_sc, g, s + 1)
                    dve.tensor_reduce(out=mx[:, s % 2, :], in_=sc, axis=AX.X, op=ALU.max).then_inc(c_mx.sem, 1)

                def context(s):
                    hold(dve, c_pv, g, s + 1)
                    cv = bank(f"C{s}")[:, 0:HJ * GV].rearrange("p (j v) -> p j v", j=HJ)
                    dve.reciprocal(rs[:, :, :], cv[:, :, HP * HD:GV]).then_inc(c_rs.sem, 1)
                    hold(dve, c_rs, g, s + 1)
                    read(dve.tensor_tensor(Cn[:, s, :].rearrange("p (j h v) -> p j h v", j=HJ, h=HP),
                                           cv[:, :, 0:HP * HD].rearrange("p j (h v) -> p j h v", h=HP), bc(rs[:, :, :], HD), ALU.mult), f"C{s}")

                if prev:
                    hold(dve, d_o, g - 1)
                    read(dve.tensor_tensor(x2[:, :, :], bank("O")[:, :].rearrange("p (t d) -> p t d", d=D), rows[:, 0:1, :].broadcast_to([P, GT, D]), ALU.add), "O")
                    was_read(dve, "O", g)
                    stats(lambda s: x2[:, s, :], d_st, g - 1, st2, mv2, ve2)
                if this:
                    scores(g, 1)
                if prev:
                    hold(dve, d_rstd, g - 1)
                    normalise(lambda s: xn2[:, s, :], lambda s: x2[:, s, :], d_xn, g - 1, mv2, rstd2)
                if this:
                    context(0)
                if nxt:
                    for s in range(GT):
                        hold(dve, r_swp, g + 1, s + 1)
                        xt = X[:, bass.ds((g + 1) * GT + s, 1), :].rearrange("p o (w f) -> p (o w) f", f=4)
                        dve.tensor_tensor(xt, xt, C4[:, bass.ds((g + 1) * GT + s, 1), :].broadcast_to([P, D // 4, 4]), ALU.mult).then_inc(r_mul.sem, 1)
                    for s in range(GT):
                        hold(dve, r_mul, g + 1, s + 1)
                        dve.tensor_tensor(tile_of(g + 1, s), tile_of(g + 1, s), big[:, 0, s * D:(s + 1) * D], ALU.add).then_inc(r_x.sem, 1)
                if this:
                    scores(g, 2)
                if nxt:
                    hold_apart(dve, r_x, g + 1)
                    stats(lambda s: tile_of(g + 1, s), c_st, g + 1)
                if this:
                    context(1)
                if nxt:
                    hold(dve, c_rstd, g + 1)
                    normalise(lambda s: xn[:, s, :], lambda s: tile_of(g + 1, s), c_xn, g + 1)
                    hold(dve, t1, g + 1)
                    read(dve.tensor_tensor(big[:, 1, :].rearrange("d (b s) -> d b s", s=S), bank("T1")[:, :].rearrange("d (b s) -> d b s", s=S),
                                           bc(scaleT[:, bass.ds((g + 1) * GB, GB)], S), ALU.mult), "T1")
                    was_read(dve, "T1", g)
                    dve.sem_inc(c_xmul.sem)
                if this:
                    scores(g, 3)
                    context(2)
                if prev:
                    hold(dve, d_y, g - 1)
                    hold(dve, d_x2b, g - 1)
                    read(dve.tensor_tensor(X3[:, :, :].rearrange("p t d -> p (t d)"), bank("Y")[:, :], x2b[:, :, :].rearrange("p t d -> p (t d)"), ALU.add), "Y")
                if this:
                    context(3)
                if nxt:
                    scores(g + 1, 0)
                if more:
                    add_experts(g + 2)
                    if not (isinstance(g, int) and g == NG - 3):
                        hold(dve, y_add, g + 2)
                        dve.sem_inc(passed["DVE"])
                        next_rows(g + 3)
                if prev:
                    hold(dve, f_u, g - 1)
                    was_read(dve, "Y", g)
                    hold(dve, o_b, g - 1, 0)
                    read(dve.tensor_tensor(z[:, :, :].rearrange("p t d -> p (t d)"), bank("U")[:, :], X3[:, :, :].rearrange("p t d -> p (t d)"), ALU.add), "U")
                    was_read(dve, "U", g)
                    stats(lambda s: z[:, s, :], o_st, g - 1, st3, mv3, ve3)
                    hold(dve, o_rstd, g - 1)
                    normalise(lambda s: z[:, s, :], lambda s: z[:, s, :], o_zn, g - 1, mv3, rstd3)
                    hold(dve, o_zn, g - 1)
                    dve.tensor_tensor(z[:, :, :], z[:, :, :], rows[:, 2:3, :].broadcast_to([P, GT, D]), ALU.mult).then_inc(o_g.sem, 1)

            pipeline(dve, iteration)

        @block.tensor
        def _(pe):
            n = [0]

            def mark(ins, at):
                n[0] += 1
                ins.then_inc(pe_set, 1)
                assert n[0] == at, (n[0], at)

            for sig in (a_T, a_lg, a_rT, e_T, e_h, e_hT, e_y, f_u):
                sig.open(pe)
            pe.wait_ge(ld_small, 16 * N_SMALL)
            pe.wait_ge(pool_set, P_SET)
            pe.wait_ge(dve_set, D_ONEHOT)
            mark(pe.matmul(W[3][0:SE, 0:B], embw[:, :], onehot[:, :], start=True, stop=True), E_SE)
            pe.transpose(PS[:, 0, 0:A], doww[:, :], ident[0:A, 0:A])
            mark(pe.transpose(PS[0:A, 1, 0:D], upw[:, :], ident[:, :]), E_DT)
            pe.wait_ge(dve_set, D_TAB + 1)
            mark(pe.matmul(W[0][:, 0:B], hypw1[:, :], sD[0:SE, :], start=True, stop=True), E_HYP1)
            pe.wait_ge(act_set, 4)
            mark(pe.matmul(W[1][:, 0:B], hypw2[:, :], gammaT[:, :], start=True, stop=True), E_HYP2)
            pe.wait_ge(act_set, 5)
            mark(pe.matmul(W[0][0:SQ, 0:B], styw1[:, :], betaT[:, :], start=True, stop=True), E_STY1)
            pe.wait_ge(act_set, 6)
            pe.matmul(W[1][:, 0:B], styw2[:, 0:D], idf[0:SQ, :], start=True, stop=True)
            mark(pe.matmul(W[2][:, 0:B], styw2[:, D:2 * D], idf[0:SQ, :], start=True, stop=True), E_STY2)
            pe.wait_ge(dve_set, D_SILU)
            pe.matmul(PS[:, 2, 0:B], wada[:, 0:D], sC[:, :], start=True, stop=True)
            mark(pe.matmul(PS[:, 3, 0:B], wada[:, D:2 * D], sC[:, :], start=True, stop=True), E_ADA)
            for c in range(NX // 4):
                ins = pe.matmul(PS[:, 0, c * D:(c + 1) * D], exw[:, 4 * c:4 * c + 4, :].rearrange("o e a -> o (e a)"), upT[:, :], start=True, stop=True)
            mark(ins, E_WU)
            mark(pe.matmul(PS[0:NX + 2, 1, 0:D], vecs[:, :], upT[:, :], start=True, stop=True), E_CT)
            pe.wait_ge(dve_set, D_WUS)
            pe.matmul(PS[:, 2, 0:4 * NT], e4[:, :], trk[:, :, :].rearrange("b k t -> b (k t)"), start=True, stop=True)
            mark(pe.matmul(PS[:, 2, 4 * NT:5 * NT], e4[:, :], dom4f[:, :], start=True, stop=True), E_ROT)
            pe.wait_ge(act_set, A_SET)
            def normalised(g):
                for s in range(GT):
                    hold(pe, a_xn, g, s + 1)
                    ins = pe.transpose(W[3][:, s * P:(s + 1) * P], xn[:, s, :], ident[:, :])
                ins.then_inc(a_T.sem, 1)

            def styled(g, c):
                hold(pe, a_dve, g)
                for s in range(GT):
                    ins = pe.matmul(W[2][:, bass.ds((g * GT + s) * NE, NE)], hTw[:, 0, s * P:(s + 1) * P], rw[:, :], start=True, stop=True)
                ins.then_inc(a_lg.sem, 1)
                hold(pe, a_row, g - 2)
                for s in range(GT):
                    ins = pe.transpose(W[c][:, s * P:(s + 1) * P], hTw[:, 0, s * P:(s + 1) * P], ident[:, :])
                ins.then_inc(a_rT.sem, 1)

            def count(g):
                hold(pe, best, g)
                hold(pe, placed, g, 0)
                pe.sem_inc(passed["PE"])
                counts = PS[:, 0, 0:(GT + 1) * NE].rearrange("p (t e) -> p t e", e=NE)
                pe.matmul(counts, upper[:, :], both[:, :, :], start=True, stop=False)
                for r in range(GT):
                    ins = pe.matmul(counts[:, r + 1:GT + 1, :], ones[:, :], both[:, r:r + 1, :].broadcast_to([P, GT - r, NE]), start=False, stop=(r == GT - 1))
                ins.then_inc(a_pos.sem, 1)

            normalised(0)
            styled(0, 0)
            normalised(1)
            with pe.Fori(0, (NG - 2) // 2) as i:
                for c in range(2):
                    g = i * 2 + c
                    count(g)
                    styled(g + 1, 1 - c)
                    normalised(g + 2)
            count(NG - 2)
            styled(NG - 1, 1)
            count(NG - 1)
            hold(pe, a_row, NG - 1)
            pe.wait_ge(ld_exp, 32)
            eight = [None]

            def step(place, ahead, first, middle, last):
                if isinstance(place.j, int):
                    two = pe.value_load(pair_at[0:1, place.at(1):place.at(2)], min_val=0, max_val=NE * NE - 1)
                else:
                    if place.q == 0:
                        eight[0] = pe.value_load(eight_at[0:1, bass.ds(place.j, 1)], min_val=0, max_val=NE ** 8 - 1)
                    two = eight[0] // NE ** (2 * place.q) % (NE * NE)
                first_expert, last_expert = two // NE, two % NE
                if ahead:
                    c = place.slot(1)
                    pe.wait_ge(tile_ld[c], place.round(1) * 16 + 16)
                    hold(pe, e_in, place.at(-1))
                    pe.transpose(PS[:, 2 + c % 2, 0:P], tile_in[:, c, :], ident[:, :]).then_inc(e_T.sem, 1)
                if middle:
                    c = place.slot(-1) % 2
                    hold(pe, e_add, place.at(-3))
                    hold(pe, e_hc, place.at(-1))
                    for k in range(FC):
                        ins = pe.transpose(PS[:, c, k * P:(k + 1) * P], hid[:, 0, c, k * P:(k + 1) * P], ident[:, :])
                    ins.then_inc(e_hT.sem, 1)
                if last:
                    c = place.slot(-2) % 2
                    hold(pe, e_yc, place.at(-4))
                    hold(pe, e_relu, place.at(-2))
                    pe.sem_inc(passed["PE"])
                    for k in range(FC):
                        ins = pe.matmul(W[2 + c][:, 0:P], hid[:, 0, 2 + c, k * P:(k + 1) * P], W2E[:, bass.ds(last_expert, 1), k, :].rearrange("p o d -> p (o d)"),
                                        start=(k == 0), stop=(k == FC - 1))
                    ins.then_inc(e_y.sem, 1)
                if ahead:
                    c = place.slot(1) % 2
                    hold(pe, e_hc, place.at(-1))
                    hold(pe, e_in, place.at(1))
                    pe.sem_inc(passed["PE"])
                    pe.matmul(W[c][:, :], tile_inT[:, c, :], W1E[:, bass.ds(first_expert, 1), :].rearrange("p o f -> p (o f)"), start=True, stop=True).then_inc(e_h.sem, 1)

            pe.wait_ge(listed, 1)
            tile_pipeline(pe, step)
            hold(pe, e_yc, LIST - 1)
            pe.wait_ge(ld_wsel, 16 * NT)
            pe.wait_ge(dve_set, D_SET)

            def iteration(g, p, prev, this, nxt, more):
                def transposed(name, src, ready, g_of, sig):
                    free(name, g)
                    for s in range(GT):
                        if ready is not None:
                            hold(pe, ready, g_of, s + 1)
                        ins = pe.transpose(bank(name)[:, s * P:(s + 1) * P], src[:, s, :], ident[:, :])
                    ins.then_inc(sig.sem, 1)

                def scores(g, s, par):
                    hold_apart(pe, c_sc, g, s)
                    for b in range(BT):
                        for j in range(HJ):
                            lo = s * P + b * S
                            ins = pe.matmul(PS[S * b:S * b + S, j, 0:P], QT[32 * j:32 * j + 32, lo:lo + S],
                                            KM[32 * j:32 * j + 32, s * BT + b, :, :].rearrange("d h k -> d (h k)"), start=True, stop=True)
                    ins.then_inc(c_qk.sem, 1)

                def values(it, g, s, par):
                    free(f"V{s}", it)
                    for b in range(BT):
                        lo = s * P + b * S
                        for h in range(HP):
                            ins = pe.matmul(bank(f"V{s}")[S * h:S * h + S, b * D:(b + 1) * D], xmT[:, par, lo:lo + S],
                                            wv4[:, h, :, :, :].rearrange("d j h v -> d (j h v)"), start=True, stop=True)
                    ins.then_inc(c_v.sem, 1)

                def transposed_probs(s):
                    hold(pe, c_exp, g, s + 1)
                    free(f"P{s}", g)
                    for j in range(HJ):
                        ins = pe.transpose(bank(f"P{s}")[:, j * P:(j + 1) * P], Sc[:, s % 2, j * HP:(j + 1) * HP, :].rearrange("p h k -> p (h k)"), ident[:, :])
                    ins.then_inc(c_pT.sem, 1)

                def context(s):
                    was_read(pe, f"P{s}", g)
                    free(f"C{s}", g)
                    for b in range(BT):
                        for j in range(HJ):
                            ins = pe.matmul(bank(f"C{s}")[S * b:S * b + S, j * GV:(j + 1) * GV], PT[:, j, b * S:b * S + S], VB[:, s % 2, b, j, :],
                                            start=True, stop=True)
                    ins.then_inc(c_pv.sem, 1)

                def up(c):
                    free(f"F{c}", g)
                    pe.matmul(bank(f"F{c}")[:, :], w1[:, c * P:(c + 1) * P], h2T[:, :], start=True, stop=True).then_inc(d_f.sem, 1)

                if prev:
                    was_read(pe, "C3", g - 1)
                    transposed("CT", Cn, None, None, d_cT)
                if this:
                    transposed_probs(0)
                if prev:
                    was_read(pe, "CT", g)
                    free("O", g)
                    for s in range(GT):
                        pe.matmul(bank("O")[:, s * D:(s + 1) * D], ctxT[:, s * P:(s + 1) * P], wo[:, :], start=True, stop=False)
                        ins = pe.matmul(bank("O")[:, s * D:(s + 1) * D], xmT[:, 1 - p, s * P:(s + 1) * P], ident[:, :], start=False, stop=True)
                    ins.then_inc(d_o.sem, 1)
                if this:
                    scores(g, 1, p)
                    values(g, g, 1, p)
                    context(0)
                    transposed_probs(1)
                    scores(g, 2, p)
                    values(g, g, 2, p)
                if prev:
                    transposed("T2", xn2, d_xn, g - 1, t2)
                if this:
                    context(1)
                if prev:
                    was_read(pe, "T2", g)
                    for c in range(FC - 1):
                        up(c)
                if nxt:
                    transposed("T1", xn, c_xn, g + 1, t1)
                if prev:
                    up(FC - 1)
                if this:
                    transposed_probs(2)
                    scores(g, 3, p)
                    values(g, g, 3, p)
                    context(2)
                if nxt:
                    hold(pe, c_xm, g + 1)
                    free("Q", g)
                    pe.matmul(bank("Q")[:, :], wq[:, :], xmT[:, 1 - p, :], start=True, stop=True).then_inc(qp.sem, 1)
                    free("K", g)
                    pe.matmul(bank("K")[:, :], wk[:, :], xmT[:, 1 - p, :], start=True, stop=True).then_inc(kp.sem, 1)
                if prev:
                    for c in range(FC):
                        was_read(pe, f"F{c}", g)
                    free("Y", g)
                    for s in range(GT):
                        for c in range(FC):
                            ins = pe.matmul(bank("Y")[:, s * D:(s + 1) * D], hid[:, 0, c, s * P:(s + 1) * P], w2[:, c, :], start=(c == 0), stop=(c == FC - 1))
                    ins.then_inc(d_y.sem, 1)
                if this:
                    transposed_probs(3)
                if prev:
                    was_read(pe, "Y", g)
                    transposed("T3", X3, None, None, t3)
                if this:
                    context(3)
                if prev:
                    was_read(pe, "T3", g)
                    free("D", g)
                    pe.matmul(bank("D")[:, :], dwT[:, :, :].rearrange("d r a -> d (r a)"), X3T[:, :], start=True, stop=True).then_inc(dp.sem, 1)
                if nxt:
                    was_read(pe, "Q", g)
                    was_read(pe, "K", g)
                    pe.sem_inc(passed["PE"])
                    scores(g + 1, 0, 1 - p)
                    values(g, g + 1, 0, 1 - p)
                if prev:
                    was_read(pe, "D", g)
                    hold(pe, f_oh, g - 1)
                    free("U", g)
                    for s in range(GT):
                        pe.matmul(bank("U")[:, s * D:(s + 1) * D], hBD[:, 0, s, :], WSEL[:, bass.ds((g - 1) * GT + s, 1), :].rearrange("p o d -> p (o d)"), start=True, stop=False)
                        ins = pe.matmul(bank("U")[:, s * D:(s + 1) * D], ohx[:, s, :], CT[:, :], start=False, stop=True)
                    ins.then_inc(f_u.sem, 1)

            pipeline(pe, iteration)


N_SMALL = 49
P_SET = 24
A_SET = 11
E_SE, E_DT, E_HYP1, E_HYP2, E_STY1, E_STY2, E_ADA, E_WU, E_CT, E_ROT = range(1, 11)
D_ONEHOT = 8
D_ANG = 45
D_TAB = 57
D_UPT = 60
D_SILU = 62
D_WUS = 65
D_WIDX = 80
D_SET = 88
T_D = 13


def kernel(**inputs):
    import numpy as np
    import concourse.bacc as bacc
    from concourse.bass_utils import run_bass_kernel_spmd

    nc = bacc.Bacc("TRN2", target_bir_lowering=False, num_devices=1)
    arrays = {name: np.ascontiguousarray(v) for name, v in inputs.items()}
    half = 64
    f = np.exp(np.arange(half, dtype=np.float32) * np.float32(-np.log(10000.0) / (half - 1))).astype(np.float32)
    freqs = np.zeros((128, 3), np.float32)
    freqs[:, 0] = np.concatenate([f, f])
    freqs[half:, 1] = 0.25
    freqs[half:, 2] = np.pi / 2
    arrays["freqs"] = freqs
    aps = {}
    for name, v in arrays.items():
        aps[name] = nc.dram_tensor(name + "_dram", v.shape, mybir.dt.from_np(v.dtype), kind="ExternalInput").ap()
    shape = inputs["x"].shape
    out = nc.dram_tensor("out_dram", shape, F32, kind="ExternalOutput").ap()
    build(nc, aps, out)
    r = run_bass_kernel_spmd(nc, [{k + "_dram": v for k, v in arrays.items()}], core_ids=[0])
    return r.results[0]["out_dram"]
```

```python
from contextlib import ExitStack

import concourse.bass as bass
from concourse import mybir

F32 = mybir.dt.float32
BF16 = mybir.dt.bfloat16
I32 = mybir.dt.int32
U32 = mybir.dt.uint32
U8 = mybir.dt.uint8
ALU = mybir.AluOpType
ACT = mybir.ActivationFunctionType
AX = mybir.AxisListType

P = 128
PI = 3.14159265358979
TWO_PI_HI = 6.28125
TWO_PI_LO = 2 * PI - TWO_PI_HI
ROUND = 12582912.0
MASKED = -1.0e30


class Signal:

    def __init__(self, sem, per, lead):
        self.sem, self.per, self.lead = sem, per, lead

    def open(self, eng):
        eng.sem_inc(self.sem, self.lead)

    def upto(self, g, k=None):
        return g * self.per + (self.per if k is None else k) + self.lead


def build(nc, a, out):
    B, S, D = a["x"].shape
    NT = B * S // P
    BT = P // S
    GT = 4
    NG = NT // GT
    GB = GT * BT
    GN = GT * P
    H = 16
    HD = D // H
    NE, _, FF = a["L0_cond_exp_w1"].shape
    FC = FF // P
    HJ = 4
    HP = H // HJ
    GV = HP * HD + HP
    NX, A, _ = a["L3_cond_expert_W"].shape
    NS, SE = a["L0_cond_subj_emb"].shape
    SQ = a["L0_cond_sty_w1"].shape[1]

    LIST = 2 * NT + NE - 1
    REGION = B * S + P
    SPARE = 8
    assert (LIST - 3) % 4 == (LIST - 7) % 4 == 0 and LIST - 2 * NT < SPARE

    wud = nc.dram_tensor("expert_up_rows", [(NX + 1) * A, D], F32, kind="Internal").ap()
    hrows = nc.dram_tensor("expert_in_rows", [NE * REGION + SPARE * P, D], F32, kind="Internal").ap()
    yrows = nc.dram_tensor("expert_out_rows", [LIST * P, D], F32, kind="Internal").ap()

    with ExitStack() as ctx:
        def sb(name, shape, dt=F32):
            return ctx.enter_context(nc.sbuf_tensor(name, shape, dt))

        def sem(name):
            return ctx.enter_context(nc.semaphore(name))

        def signal(name, per=1, lead=0):
            return Signal(sem(name), per, lead)

        X = sb("X", [P, NT, D])
        ROOM = sb("ROOM", [P, NT * P])
        BIAS = sb("BIAS", [P, NT, H, S])
        EXP = sb("EXP", [P, 2 * NE * FF])
        W1E = EXP[:, 0:NE * FF].rearrange("p (e f) -> p e f", e=NE)
        W2E = EXP[:, NE * FF:2 * NE * FF].rearrange("p (e c d) -> p e c d", e=NE, c=FC)
        hid = sb("hid", [P, 2, FC, GN])
        lent = [0]

        def setup(shape, dt=F32):
            n = 1
            for d in shape[1:]:
                n *= d
            lent[0] += n
            assert lent[0] <= FC * GN
            ap = hid[0:shape[0], 1, :, :].rearrange("p c n -> p (c n)")[:, lent[0] - n:lent[0]]
            return ap if dt is F32 else ap.bitcast(dt)

        used = [0]

        def part(n):
            lo = used[0] if used[0] + n <= 2 * NE * FF or used[0] >= 2 * NE * FF else 2 * NE * FF
            used[0] = lo + n
            if lo < 2 * NE * FF:
                return EXP[:, lo:lo + n]
            lo -= 2 * NE * FF
            assert lo + n <= 3 * NT * P // 4
            return ROOM[:, lo:lo + n]

        big = sb("big", [P, 2, GN]); hTw = sb("hTw", [P, 1, GN])
        hA = (ROOM[:, 3 * GN:4 * GN], big[:, 1, :])
        hrow = ROOM[:, 0:2 * GT * (P + NE)].rearrange("p (c t n) -> p c t n", c=2, t=GT)
        tile_in = ROOM[:, 0:GN].rearrange("p (c d) -> p c d", d=D)
        tile_out = ROOM[:, GN:2 * GN].rearrange("p (c d) -> p c d", d=D)
        tile_inT = ROOM[:, 3 * GN:3 * GN + 2 * P].rearrange("p (c n) -> p c n", c=2)
        Y = ROOM[:, 3 * NT * P // 4:NT * P].rearrange("p (k t d) -> p k t d", k=2, d=D)

        B1E = sb("B1E", [P, NE, FC])
        ident_rw = sb("ident_rw", [P, P + NE])
        ident = ident_rw[:, 0:P]; rw = ident_rw[:, P:P + NE]
        ln_gb = sb("ln_gb", [P, 2])
        ids = setup([P, B], I32); ids2 = setup([P, B], I32); ids3 = setup([NX + 2, B], I32)
        idf = setup([P, B])
        embw = setup([NS, SE])
        hypw1 = setup([SE, P]); hypw2 = setup([P, P])
        styw1 = setup([P, SQ]); styw2 = setup([SQ, 2 * D])
        hb = sb("hb", [P, 5])
        wada = setup([P, 2 * D]); bada = sb("bada", [P, 2])
        B2E = sb("B2E", [P, NE, D])
        fq = sb("fq", [P, 1]); ph = sb("ph", [P, 2])
        wq = sb("wq", [P, D]); wk = sb("wk", [P, D]); wv = sb("wv", [P, D]); wo = sb("wo", [P, D])
        w1 = sb("w1", [P, FF]); w2 = sb("w2", [P, FC, D]); b1 = sb("b1", [P, FC])
        cols = sb("cols", [P, 6])
        bqs = sb("bqs", [P, 1]); bkm = sb("bkm", [P, HP])
        rows = sb("rows", [P, 4, D])
        maskb = sb("maskb", [P, NT, S], U8); ot = sb("ot", [P, 2, GT, D])
        maskn = ot[:, :, :, :].rearrange("p a t d -> p (a t d)").rearrange("p (t k) -> p t k", k=S)
        hm16 = sb("hm16", [P, H]); hm4 = sb("hm4", [P, HP]); vm = sb("vm", [P, BT, HJ, HP])
        e4 = sb("e4", [BT, P]); ang = sb("ang", [BT, 2, NT]); tr = sb("tr", [BT, 4, NT]); trk = sb("trk", [BT, 4, NT])
        C4 = sb("C4", [P, NT, 4]); S4 = sb("S4", [P, NT, 4])
        iot = sb("iot", [P, 1], I32); iof = sb("iof", [P, 1]); acol = sb("acol", [P, 1], I32); acf = sb("acf", [P, 1])
        half = sb("half", [P, GB])
        desc = sb("desc", [P, NE], I32); dsf = sb("dsf", [P, NE])
        onehot = setup([NS, B])
        ohx1, ohx2, ohx3 = (ROOM[0:NX + 2, 6 * GN + k * B:6 * GN + (k + 1) * B] for k in range(3))
        sA = setup([P, B]); sB = setup([P, B]); sC = setup([P, B]); sD = setup([P, B])
        gammaT = sb("gammaT", [P, B]); betaT = sb("betaT", [P, B])
        scaleT = sb("scaleT", [P, B]); shiftT = sb("shiftT", [P, B])
        doww = sb("doww", [A, D]); dwT = sb("dwT", [P, 4, A]); upw = sb("upw", [P, A]); upT = sb("upT", [A, D])
        exw = ROOM[0:A, 4 * GN:5 * GN].rearrange("o (e a) -> o e a", e=NX); wus = ROOM[:, 5 * GN:6 * GN].rearrange("p (c d) -> p c d", d=D)
        vecs = sb("vecs", [A, NX + 2]); emt = sb("emt", [A, NX])
        upb = sb("upb", [NX + 2, D]); CT = sb("CT", [NX + 2, D]); ohC = sb("ohC", [NX + 2, B])
        dom4 = sb("dom4", [BT, NT], I32); dom4f = sb("dom4f", [BT, NT]); domx = sb("domx", [P, NT]); domy = sb("domy", [P, NT])
        widx = sb("widx", [P, NT], U32)
        WSEL = sb("WSEL", [P, NT, D])
        hBD = sb("hBD", [P, 1, GT, P])
        g1 = sb("g1", [P, NT]); g2 = sb("g2", [P, NT]); m1 = sb("m1", [P, NT]); m2 = sb("m2", [P, NT]); mw = sb("mw", [P, GT])
        upper = sb("upper", [P, P], BF16); ones = sb("ones", [P, P], BF16); both = sb("both", [P, GT + 1, NE], BF16)
        posf = sb("posf", [P, 2, NT]); moved = sb("moved", [P, 2, NT]); pos = sb("pos", [P, 2, NT], U32)
        pos_g = sb("pos_g", [P, 2, 2, GT], U32)
        base = sb("base", [P, NE]); regi = sb("regi", [P, NE], I32); regf = sb("regf", [P, NE])
        pads = sb("pads", [P, NE], I32); tiles = sb("tiles", [P, NE]); ends = sb("ends", [P, NE]); jump = sb("jump", [P, NE])
        seqi = sb("seqi", [P, LIST], I32); seq = sb("seq", [P, LIST])
        row_at = sb("row_at", [P, LIST], I32); expert_at = sb("expert_at", [P, LIST], I32); pair_at = sb("pair_at", [P, LIST + 3], I32); eight_at = sb("eight_at", [P, (LIST - 3) // 4], I32)
        st = sb("st", [P, GT, 6]); mv = sb("mv", [P, GT, 2]); ve = sb("ve", [P, GT]); rstd = sb("rstd", [P, GT])
        xn = sb("xn", [P, GT, D]); xn2 = part(GT * D).rearrange("p (t d) -> p t d", d=D)
        st2, st3 = (sb(f"st{k}", [P, GT, 6]) for k in (2, 3))
        mv2, mv3 = (sb(f"mv{k}", [P, GT, 2]) for k in (2, 3))
        ve2, ve3, rstd2, rstd3 = (sb(f"{n}", [P, GT]) for n in ("ve2", "ve3", "rstd2", "rstd3"))
        vs = sb("vs", [P, 4, GB])
        sel = hid[:, 0, 0, 0:2 * NT * NE].rearrange("p (k t e) -> p k t e", k=2, e=NE)
        Lg, ta, pf = (hid[:, 0, 1, k * GT * NE:(k + 1) * GT * NE].rearrange("p (t e) -> p t e", e=NE) for k in range(3))
        picked = hid[:, 0, 2, 0:2 * GT * NE].rearrange("p (k t e) -> p k t e", k=2, e=NE)
        moves = hid[:, 0, 1, :].rearrange("p (k t e) -> p k t e", k=2, e=NE)
        passed_end = hid[:, 0, 2:4, :].rearrange("p c n -> p (c n)")[:, 0:LIST * NE].rearrange("p (i e) -> p i e", e=NE)
        pairf = hid[:, 0, 1, GN // 2 + P:GN // 2 + P + LIST + 3]
        rowf = hid[:, 0, 3, GN - P:GN - P + LIST]
        listf = hid[:, 0, 1, GN // 2:GN // 2 + LIST]
        xmT = part(2 * GN).rearrange("p (c n) -> p c n", c=2); QT = part(GN); KM = part(GB * HP * S).rearrange("p (b h k) -> p b h k", h=HP, k=S)
        Sc = part(2 * H * S).rearrange("p (c h k) -> p c h k", c=2, h=H)
        PT = part(HJ * P).rearrange("p (j q) -> p j q", j=HJ)
        VB = part(2 * BT * HJ * GV).rearrange("p (c b j v) -> p c b j v", c=2, b=BT, j=HJ)
        wv4 = sb("wv4", [P, HP, HJ, HP, HD])
        Cn = part(GT * D).rearrange("p (t d) -> p t d", d=D)
        mx = sb("mx", [P, 2, H]); rs = sb("rs", [P, HJ, HP])
        ctxT = part(GN)
        x2, x2b, X3, z = (part(GT * D).rearrange("p (t d) -> p t d", d=D) for _ in range(4))
        h2T = part(GN); X3T = part(GN)
        ohx = sb("ohx", [NX + 2, GT, P])

        PS = ctx.enter_context(nc.psum_tensor("PS", [P, 4, 512], F32))
        rows_lg = PS[:, 1:3, 0:2 * (P + NE)].rearrange("p b (t n) -> p b t n", t=2)
        W = [ctx.enter_context(nc.psum_tensor(f"W{i}", [P, 512], F32)) for i in range(4)]

        ld_first = sem("ld_first"); ld_angles = sem("ld_angles"); ld_rest = sem("ld_rest"); ld_exp_b = sem("ld_exp_b"); ld_x = sem("ld_x"); ld_exp = sem("ld_exp"); ld_bias = sem("ld_bias"); ld_mask = sem("ld_mask")
        st_wu = sem("st_wu"); ld_wsel = sem("ld_wsel"); out_done = [sem(f"out_done{i}") for i in range(2)]
        pool_set = sem("pool_set"); dve_set = sem("dve_set"); act_set = sem("act_set"); pe_set = sem("pe_set")
        zeroed = sem("zeroed")
        bias_masked = signal("bias_masked", GT)
        a_st = signal("a_st", 2 * GT + 1); a_sqrt = signal("a_sqrt"); a_rstd = signal("a_rstd"); a_xn = signal("a_xn", GT)
        a_T = signal("a_T", lead=1); a_h = signal("a_h"); a_dve = signal("a_dve", 8); a_sq = signal("a_sq"); a_rv = signal("a_rv")
        a_rT = signal("a_rT", lead=1); a_row = signal("a_row", lead=2)
        best = signal("best", 13); a_pos = signal("a_pos"); placed = signal("placed", 4, lead=1)
        idx_ready = signal("idx_ready"); slot_free = signal("slot_free", lead=2); scattered = [sem(f"scattered{c}") for c in range(2)]
        listed = sem("listed"); paired = sem("paired"); pads_ready = sem("pads_ready"); pads_done = sem("pads_done"); spare_done = sem("spare_done")
        gate_act = sem("gate_act"); gate_dve = sem("gate_dve")
        tile_ld = [sem(f"tile_ld{c}") for c in range(4)]; tile_st = [sem(f"tile_st{c}") for c in range(4)]
        e_T, e_in, e_h, e_hc, e_hT, e_add, e_relu, e_y, e_yc = (
            signal(n, lead=2) for n in ("e_T", "e_in", "e_h", "e_hc", "e_hT", "e_add", "e_relu", "e_y", "e_yc"))
        y_idx = signal("y_idx"); y_ld = [signal(f"y_ld{k}", 16 * GT) for k in range(2)]; y_add = signal("y_add", 2)
        r_mul = signal("r_mul", GT); r_swp = signal("r_swp", GT); r_x = signal("r_x", GT, lead=1)
        c_st = signal("c_st", 2 * GT + 1); c_rstd = signal("c_rstd"); c_xn = signal("c_xn", GT)
        c_xm = signal("c_xm"); c_qk = signal("c_qk", GT); c_sc = signal("c_sc", GT, lead=1); c_mx = signal("c_mx", GT)
        c_sub = signal("c_sub", GT); c_exp = signal("c_exp", GT); c_rs = signal("c_rs", GT)
        c_pv = signal("c_pv", GT); c_v = signal("c_v", GT); c_pT = signal("c_pT", GT)
        d_cT = signal("d_cT"); d_o = signal("d_o"); d_x2b = signal("d_x2b")
        d_st = signal("d_st", 2 * GT + 1); d_rstd = signal("d_rstd"); d_xn = signal("d_xn", GT); d_f = signal("d_f", FC)
        d_y = signal("d_y"); f_oh = signal("f_oh"); f_u = signal("f_u", lead=1)
        t1 = signal("t1"); t2 = signal("t2"); t3 = signal("t3"); qp = signal("qp"); kp = signal("kp"); dp = signal("dp")
        o_st = signal("o_st", 2 * GT + 1); o_rstd = signal("o_rstd"); o_zn = signal("o_zn", GT)
        o_b = signal("o_b")
        vb_ones = sem("vb_ones"); listed_dve = sem("listed_dve")

        bank_read = [sem(f"bank_read{b}") for b in range(4)]
        NEXT, PREV = ("T1", "Q", "K", "V0"), ("CT", "O", "T2", "F0", "F1", "F2", "F3", "Y", "T3", "D", "U")
        TURNS = ("CT", "P0", "O", "V1", "C0",
                 "V2", "P1", "T2", "C1", "F0", "F1", "F2",
                 "V3", "T1", "F3", "P2", "C2", "Q", "K", "Y",
                 "P3", "T3", "C3", "D", "V0", "U")
        BANK = {name: k % 4 for k, name in enumerate(TURNS)}

        def turns(name, g):
            mine = [t for t in TURNS if BANK[t] == BANK[name]]
            k = mine.index(name)
            start = sum(t in NEXT for t in mine)
            if isinstance(g, int) and g == -1:
                return sum(t in NEXT for t in mine[:k])
            if isinstance(g, int) and g == 0:
                return start + sum(t not in PREV for t in mine[:k])
            if isinstance(g, int) and g >= NG - 1:
                last = start + sum(t not in PREV for t in mine) + (NG - 2) * len(mine)
                if g == NG - 1:
                    return last + sum(t not in NEXT for t in mine[:k])
                return last + sum(t not in NEXT for t in mine) + sum(t in PREV for t in mine[:k])
            return (g - 1) * len(mine) + start + sum(t not in PREV for t in mine) + k

        def free(name, g):
            n = turns(name, g)
            if not (isinstance(n, int) and n == 0):
                nc.tensor.wait_ge(bank_read[BANK[name]], n)

        def was_read(eng, name, g):
            eng.wait_ge(bank_read[BANK[name]], turns(name, g) + 1)

        def read(ins, name):
            ins.then_inc(bank_read[BANK[name]], 1)

        def bank(name):
            return W[BANK[name]]

        class Place:

            def __init__(self, j, q):
                self.j, self.q = j, q

            def at(self, d):
                return self.j * 4 + (self.q + 2 + d)

            def slot(self, d):
                return (self.q + 2 + d) % 4

            def round(self, d):
                return self.j + (self.q + 2 + d) // 4

        def tile_pipeline(eng, step):
            step(Place(-1, 1), True, False, False, False)
            step(Place(-1, 2), True, True, False, False)
            step(Place(-1, 3), True, True, True, False)
            with eng.Fori(0, (LIST - 3) // 4) as j:
                for q in range(4):
                    step(Place(j, q), True, True, True, True)
            j = (LIST - 3) // 4
            step(Place(j, 0), False, True, True, True)
            step(Place(j, 1), False, False, True, True)
            step(Place(j, 2), False, False, False, True)

        def pipeline(eng, iteration):
            iteration(-1, 1, False, False, True, True)
            iteration(0, 0, False, True, True, True)
            with eng.Fori(0, (NG - 4) // 2) as i:
                for p in range(2):
                    iteration(i * 2 + p + 1, (p + 1) % 2, True, True, True, True)
            iteration(NG - 3, (NG - 3) % 2, True, True, True, True)
            iteration(NG - 2, (NG - 2) % 2, True, True, True, False)
            iteration(NG - 1, (NG - 1) % 2, True, True, False, False)
            iteration(NG, NG % 2, True, False, False, False)

        block = ctx.enter_context(nc.Block())

        passed = {e.engine.name: sem(f"passed_{e.engine.name}") for e in (nc.vector, nc.scalar, nc.tensor, nc.gpsimd)}

        def hold(eng, sig, g, k=None):
            eng.wait_ge(sig.sem, sig.upto(g, k))

        def hold_apart(eng, sig, g, k=None):
            eng.wait_ge(sig.sem, sig.upto(g, k))
            eng.sem_inc(passed[eng.engine.name])

        def bc(ap, n):
            return ap.unsqueeze(len(ap.shape)).broadcast_to(list(ap.shape) + [n])

        def col(ap):
            return ap.rearrange("(p o) -> p o", o=1)

        def on_all(ap, n=P):
            return ap.rearrange("(o d) -> o d", o=1).broadcast_to([n, ap.shape[0]])

        x_view = a["x"].rearrange("(t b) s d -> (b s) t d", b=BT)
        out_view = out.rearrange("(t b) s d -> (b s) t d", b=BT)
        bias_view = a["fside_Bx16xSxS_0"].rearrange("b h q k -> b q h k")

        @block.sync
        def _(sp):
            first = (
                (ids[0:NS, :], on_all(a["itok_B_6_14"], NS)), (embw[:, :], a["L0_cond_subj_emb"]),
                (hypw1[:, :], a["L0_cond_hyp_w1"]), (hypw2[:, :], a["L0_cond_hyp_w2"]),
                (styw1[:, :], a["L0_cond_sty_w1"]), (styw2[:, :], a["L0_cond_sty_w2"]),
                (hb[:, 0:1], col(a["L0_cond_hyp_b1"])), (hb[:, 1:2], col(a["L0_cond_hyp_b2"])),
                (hb[0:SQ, 2:3], col(a["L0_cond_sty_b1"])),
                (hb[:, 3:5], a["L0_cond_sty_b2"].rearrange("(c p) -> p c", p=P)),
                (ln_gb[:, 0:1], col(a["L0_cond_ln_g"])), (ln_gb[:, 1:2], col(a["L0_cond_ln_b"])),
                (rw[:, :], a["L0_cond_router_w"]),
            )
            rest = (
                (ids2[:, :], on_all(a["itok_B_34_63"])), (fq[:, :], a["freqs"][:, 0:1]), (ph[:, :], a["freqs"][:, 1:3]),
                (ang[:, 0, :], a["condB_theta"].rearrange("(t b) -> b t", b=BT)),
                (ang[:, 1, :], a["condB_phi"].rearrange("(t b) -> b t", b=BT)),
                (ids3[:, :], on_all(a["itok_B_0_15"], NX + 2)),
                (dom4[:, :], a["itok_B_0_15"].rearrange("(t b) -> b t", b=BT)),
                (wada[:, :], a["L2_cond_W_ada"]), (bada[:, :], a["L2_cond_b_ada"].rearrange("(c p) -> p c", p=P)),
                (doww[:, :], a["L3_cond_down_W"]), (upw[:, :], a["L3_cond_up_W"]),
                (exw[:, :, :], a["L3_cond_expert_W"].rearrange("e o a -> o e a")),
                (vecs[:, 0:NX], a["L3_cond_expert_b"].rearrange("e o -> o e")),
                (emt[:, :], a["L3_cond_domain_emb"].rearrange("e o -> o e")),
                (upb[:, :], on_all(a["L3_cond_up_b"], NX + 2)),
                (wq[:, :], a["L2_cond_Wq"]), (wk[:, :], a["L2_cond_Wk"]), (wv[:, :], a["L2_cond_Wv"]), (wo[:, :], a["L2_cond_Wo"]),
                (w1[:, :], a["L2_cond_W1"]), (w2[:, :, :], a["L2_cond_W2"].rearrange("(c p) d -> p c d", p=P)),
                (b1[:, :], a["L2_cond_b1"].rearrange("(c p) -> p c", p=P)),
                (cols[:, 0:1], col(a["L2_cond_bq"])), (cols[:, 1:2], col(a["L2_cond_bk"])), (cols[:, 2:3], col(a["L2_cond_bv"])),
                (cols[:, 3:4], col(a["L2_cond_g2"])), (cols[:, 4:5], col(a["L2_cond_beta2"])),
                (rows[:, 0, :], on_all(a["L2_cond_bo"])), (rows[:, 1, :], on_all(a["L2_cond_b2"])),
                (rows[:, 2, :], on_all(a["L3_cond_ln_gamma"])), (rows[:, 3, :], on_all(a["L3_cond_ln_beta"])),
            ) + tuple((cols[A * r:A * r + A, 5:6], col(a["L3_cond_down_b"])) for r in range(4))
            assert (len(first), len(rest)) == (N_FIRST, N_REST), (len(first), len(rest))
            for k, (dst, src) in enumerate(first):
                sp.dma_start(dst, src, allow_slow_non_contiguous=True).then_inc(ld_first, 16)
                if k == 5:
                    sp.dma_start(X[:, :, :], x_view).then_inc(ld_x, 16)
            for k, (dst, src) in enumerate(rest):
                sp.dma_start(dst, src, allow_slow_non_contiguous=True).then_inc(ld_angles if k < N_ANGLES else ld_rest, 16)
            sp.dma_start(W1E[:, :, :], a["L0_cond_exp_w1"].rearrange("e d f -> d e f")).then_inc(ld_exp, 16)
            sp.dma_start(W2E[:, :, :, :], a["L0_cond_exp_w2"].rearrange("e (c p) d -> p e c d", p=P)).then_inc(ld_exp, 16)
            for dst, src in ((B1E[:, :, :], a["L0_cond_exp_b1"].rearrange("e (c p) -> p e c", p=P)),
                             (B2E[:, :, :].rearrange("p e d -> p (e d)"), on_all(a["L0_cond_exp_b2"].rearrange("e d -> (e d)")))):
                sp.dma_start(dst, src, allow_slow_non_contiguous=True).then_inc(ld_exp_b, 16)
            sp.wait_ge(zeroed, 1)
            for c in range(SPARE // GT):
                lo = NE * REGION + c * GN
                sp.dma_start(hrows[lo:lo + GN, :].rearrange("(t p) d -> p t d", p=P), hBD[:, 0, :, :]).then_inc(spare_done, 16)
            sp.dma_start(maskb[:, :, :], a["mask_Bx1xSxS_bk0"].rearrange("(t b) o q k -> (b o q) t k", b=BT)).then_inc(ld_mask, 16)
            with sp.Fori(0, NT) as t:
                for b in range(BT):
                    sp.dma_start(BIAS[S * b:S * b + S, bass.ds(t, 1), :, :].rearrange("p o h k -> p (o h) k"),
                                 bias_view[bass.ds(t * BT + b, 1), :, :, :].rearrange("o q h k -> (o q) h k")).then_inc(ld_bias, 16)
            sp.wait_ge(pads_ready, 1)
            for e in range(NE):
                row = sp.value_load(pads[0:1, e:e + 1], min_val=0, max_val=NE * REGION)
                sp.dma_start(hrows[bass.ds(row, P), :], hBD[:, 0, 0, :]).then_inc(pads_done, 16)
            sp.wait_ge(listed, 1)
            first_rows = [sp.value_load(row_at[0:1, c:c + 1], min_val=0, max_val=NE * REGION + (SPARE - 1) * P) for c in range(4)]
            for c in range(2):
                sp.wait_ge(scattered[c], NG // 2 * 16 * 2 * GT)
            sp.wait_ge(pads_done, 16 * NE)
            sp.wait_ge(spare_done, 16 * 2)

            def load(place, d):
                row = sp.value_load(row_at[0:1, bass.ds(place.at(d), 1)], min_val=0, max_val=NE * REGION + (SPARE - 1) * P)
                hold(sp, e_T, place.at(d - 4))
                sp.dma_start(tile_in[:, place.slot(d), :], hrows[bass.ds(row, P), :]).then_inc(tile_ld[place.slot(d)], 16)

            def store(place):
                hold(sp, e_yc, place.at(0))
                sp.dma_start(yrows[bass.ds(place.at(0) * P, P), :], tile_out[:, place.slot(0), :]).then_inc(tile_st[place.slot(0)], 16)

            for c, row in enumerate(first_rows):
                sp.dma_start(tile_in[:, c, :], hrows[bass.ds(row, P), :]).then_inc(tile_ld[c], 16)
            for i in range(3):
                load(Place(0, i - 2), 4)
            with sp.Fori(0, (LIST - 7) // 4) as j:
                for q in range(4):
                    load(Place(j, q + 1), 4)
                    store(Place(j, q - 2))
            for i in range((LIST - 7) // 4 * 4, LIST):
                store(Place(i // 4, i % 4 - 2))
            with sp.Fori(0, NG // 2) as i:
                for p in range(2):
                    g = i * 2 + p
                    hold(sp, o_b, g)
                    sp.dma_start(out_view[:, bass.ds(g * GT, GT), :], ot[:, p, :, :]).then_inc(out_done[p], 16)
            for p in range(2):
                sp.wait_ge(out_done[p], 16 * (NG // 2) + 16)

        @block.gpsimd
        def _(pool):
            n = [0]

            def step(ins):
                n[0] += 1
                ins.then_inc(pool_set, 1)
                pool.wait_ge(pool_set, n[0])

            def band(ap, base, pattern, cm):
                step(pool.affine_select(out=ap, in_=ap, compare_op=ALU.is_ge, fill=0.0, base=base,
                                        pattern=pattern, channel_multiplier=cm))

            slot_free.open(pool)
            for done in out_done:
                pool.sem_inc(done, 16)
            step(pool.memset(ident[:, :], 0.0))
            step(pool.affine_select(out=ident[:, :], in_=ident[:, :], compare_op=ALU.not_equal, fill=1.0,
                                    base=0, pattern=[[-1, P]], channel_multiplier=1))
            step(pool.iota(iot[:, :], [[0, 1]], base=0, channel_multiplier=1))
            for q in range(4):
                step(pool.iota(acol[A * q:A * q + A, :], [[0, 1]], base=0, channel_multiplier=1))
            step(pool.iota(desc[:, :], [[-1, NE]], base=NE, channel_multiplier=0))
            step(pool.memset(half[:, :], -0.5))
            step(pool.memset(ones[:, :], 1.0))
            step(pool.memset(both[:, :, :], 0.0))
            step(pool.memset(upper[:, :], 1.0))
            band(upper[:, :], -1, [[1, P]], -1)
            step(pool.iota(seqi[:, :], [[1, LIST]], base=0, channel_multiplier=0))
            step(pool.iota(regi[:, :], [[REGION, NE]], base=0, channel_multiplier=0))
            step(pool.memset(hm16[:, :], 1.0))
            band(hm16[:, :], 0, [[-HD, H]], 1)
            band(hm16[:, :], HD - 1, [[HD, H]], -1)
            step(pool.memset(vm[:, :, :, :], 1.0))
            band(vm[:, :, :, :], 0, [[0, BT], [0, HJ], [-S, HP]], 1)
            band(vm[:, :, :, :], S - 1, [[0, BT], [0, HJ], [S, HP]], -1)
            step(pool.memset(e4[:, :], 1.0))
            band(e4[:, :], 0, [[1, P]], -S)
            band(e4[:, :], S - 1, [[-1, P]], S)
            step(pool.tensor_copy(iof[:, :], iot[:, :]))
            assert n[0] == P_SET, n[0]
            pool.memset(hBD[:, :, :, :], 0.0).then_inc(zeroed, 1)

            def wrap(ap, k, turns_of, extra):
                step(pool.tensor_scalar(k, ap, 1 / (2 * PI), extra, ALU.mult, ALU.add))
                step(pool.tensor_scalar(k, k, ROUND, -ROUND, ALU.add, ALU.add))
                for turn in (TWO_PI_HI, TWO_PI_LO):
                    step(pool.tensor_scalar(turns_of, k, turn, None, ALU.mult))
                    step(pool.tensor_tensor(ap, ap, turns_of, ALU.subtract))

            pool.wait_ge(ld_angles, 16 * N_ANGLES)
            step(pool.tensor_copy(sB[:, :], ids2[:, :]))
            step(pool.tensor_scalar(sB[:, :], sB[:, :], 0.01, 4000.0, ALU.mult, ALU.mult))
            step(pool.tensor_scalar(sA[:, :], sB[:, :], fq[:, :], None, ALU.mult))
            wrap(sA[:, :], sB[:, :], sC[:, :], ph[:, 0:1])
            step(pool.tensor_scalar(sA[:, :], sA[:, :], ph[:, 1:2], PI, ALU.add, ALU.min))
            step(pool.tensor_scalar(sA[:, :], sA[:, :], -PI, None, ALU.max))
            for k in range(4):
                step(pool.tensor_copy(tr[:, k, :], ang[:, k // 2, :]))
                wrap(tr[:, k, :], trk[:, k, :], sC[0:BT, 0:NT], 0.25 * (k % 2))
                step(pool.tensor_scalar(tr[:, k, :], tr[:, k, :], PI / 2 * (k % 2), PI, ALU.add, ALU.min))
                step(pool.tensor_scalar(tr[:, k, :], tr[:, k, :], -PI, None, ALU.max))
            assert n[0] == P_ANG, n[0]
            pool.wait_ge(ld_rest, 16 * (N_REST - N_ANGLES))
            step(pool.tensor_tensor(hm4[:, :], hm16[:, 0:HP], hm16[:, HP:2 * HP], ALU.add))
            for j in range(2, HJ):
                step(pool.tensor_tensor(hm4[:, :], hm4[:, :], hm16[:, j * HP:(j + 1) * HP], ALU.add))
            step(pool.tensor_scalar(bkm[:, :], hm4[:, :], cols[:, 1:2], None, ALU.mult))
            step(pool.tensor_scalar(bqs[:, :], cols[:, 0:1], HD ** -0.5, None, ALU.mult))
            step(pool.tensor_tensor(vecs[:, 0:NX], vecs[:, 0:NX], emt[:, :], ALU.add))
            step(pool.tensor_copy(vecs[:, NX:NX + 1], emt[:, 0:1]))
            step(pool.tensor_copy(vecs[:, NX + 1:NX + 2], emt[:, NX - 1:NX]))
            step(pool.tensor_copy(dom4f[:, :], dom4[:, :]))
            step(pool.memset(wv4[:, :, :, :, :], 0.0))
            for h in range(HP):
                step(pool.tensor_copy(wv4[:, h, :, h, :], wv[:, :].rearrange("d (j h v) -> d j h v", j=HJ, h=HP)[:, :, h, :]))
            step(pool.tensor_copy(ohx1[:, :], ids3[:, :]))
            step(pool.tensor_scalar(ohx2[:, :], ohx1[:, :], 0.0, float(NX + 1), ALU.is_lt, ALU.mult))
            step(pool.tensor_scalar(ohx3[:, :], ohx1[:, :], float(NX) - 0.5, None, ALU.is_gt))
            step(pool.tensor_tensor(ohx2[:, :], ohx2[:, :], ohx3[:, :], ALU.add))
            step(pool.tensor_scalar(ohx1[:, :], ohx1[:, :], -1.0, float(NX), ALU.max, ALU.min))
            step(pool.tensor_tensor(ohx2[:, :], ohx2[:, :], ohx1[:, :], ALU.add))
            step(pool.tensor_scalar(ohC[:, :], ohx2[:, :], iof[0:NX + 2, :], None, ALU.is_equal))
            step(pool.tensor_copy(acf[:, :], acol[:, :]))
            assert n[0] == P_TAB, n[0]

            def scatter(g, c):
                hold(pool, a_row, g)
                hold_apart(pool, idx_ready, g)
                for t in range(GT):
                    for k in range(2):
                        pool.indirect_dma_start(out=hrows[:, :], out_offset=bass.IndirectOffsetOnAxis(ap=pos_g[:, c, k, t:t + 1], axis=0),
                                                in_=hrow[:, c, t, 0:D], in_offset=None).then_inc(scattered[c], 16)

            for c in range(2):
                scatter(c, c)
            with pool.Fori(0, (NG - 2) // 2) as i:
                for c in range(2):
                    pool.wait_ge(scattered[c], (i + 1) * (16 * 2 * GT))
                    pool.sem_inc(slot_free.sem)
                    scatter(i * 2 + c + 2, c)
            pool.wait_ge(ld_mask, 16)
            step(pool.tensor_copy(maskn[:, :, :], maskb[:, :, :]))
            step(pool.tensor_scalar(maskn[:, :, :], maskn[:, :, :], MASKED, 0.0, ALU.mult, ALU.add))
            pool.wait_ge(dve_set, D_WIDX)
            pool.dma_start(wud[0:NX * A, :].rearrange("(c p) d -> p c d", p=P), wus[:, :, :]).then_inc(st_wu, 16)
            pool.dma_start(wud[NX * A:(NX + 1) * A, :], upT[:, :]).then_inc(st_wu, 16)
            pool.wait_ge(st_wu, 32)
            for t in range(NT):
                pool.indirect_dma_start(out=WSEL[:, t, :], out_offset=None, in_=wud[:, :],
                                        in_offset=bass.IndirectOffsetOnAxis(ap=widx[:, t:t + 1], axis=0)).then_inc(ld_wsel, 16)
            pool.wait_ge(ld_bias, 16 * B)
            with pool.Fori(0, NG) as g:
                for s in range(GT):
                    bt = BIAS[:, bass.ds(g * GT + s, 1), :, :].rearrange("p o h k -> p (o h) k")
                    mk = maskn[:, bass.ds(g * GT + s, 1), :].broadcast_to([P, H, S])
                    pool.tensor_tensor(bt, bt, mk, ALU.add).then_inc(bias_masked.sem, 1)
            hold(pool, e_y, LIST - 1)
            for c in range(2):
                pool.tensor_copy(VB[:, c, :, :, HP * HD:GV], vm[:, :, :, :]).then_inc(vb_ones, 1)
            for c in range(4):
                pool.wait_ge(tile_st[c], 16 * ((LIST - 1 - c) // 4 + 1) + 16)

            def gather(g, first, last):
                if first == 0:
                    hold_apart(pool, y_idx, g)
                for r in range(first, last):
                    k, t = r // GT, r % GT
                    pool.indirect_dma_start(out=Y[:, k, t, :], out_offset=None, in_=yrows[:, :],
                                            in_offset=bass.IndirectOffsetOnAxis(ap=pos_g[:, 0, k, t:t + 1], axis=0)).then_inc(y_ld[k].sem, 16)

            gather(0, 0, 2 * GT)

            def iteration(g, p, prev, this, nxt, more):
                def subtract(g, s):
                    hold(pool, c_mx, g, s + 1)
                    c = s % 2
                    pool.tensor_tensor(Sc[:, c, :, :], Sc[:, c, :, :], bc(mx[:, c, :], S), ALU.subtract).then_inc(c_sub.sem, 1)

                if this:
                    subtract(g, 1)
                if prev:
                    hold(pool, d_st, g - 1)
                    pool.tensor_tensor(rstd2[:, :], ve2[:, :], half[:, 0:GT], ALU.pow).then_inc(d_rstd.sem, 1)
                if nxt:
                    for s in range(GT):
                        xt = X[:, bass.ds((g + 1) * GT + s, 1), :].rearrange("p o (w h e) -> p (o w) h e", h=2, e=2)
                        sw = big[:, 0, s * D:(s + 1) * D].rearrange("p (w h e) -> p w h e", h=2, e=2)
                        s4 = S4[:, bass.ds((g + 1) * GT + s, 1), :].broadcast_to([P, D // 4, 4]).rearrange("p w (h e) -> p w h e", h=2)
                        if s == 0:
                            hold(pool, r_x, g + 1, 0)
                            hold(pool, y_add, g + 1)
                        for e in range(2):
                            ins = pool.tensor_tensor(sw[:, :, :, e], xt[:, :, :, 1 - e], s4[:, :, :, e], ALU.mult)
                        ins.then_inc(r_swp.sem, 1)
                if this and more:
                    gather(g + 2, 0, 2)
                if prev:
                    pool.tensor_tensor(x2b[:, :, :], x2[:, :, :], rows[:, 1:2, :].broadcast_to([P, GT, D]), ALU.add).then_inc(d_x2b.sem, 1)
                if this:
                    subtract(g, 2)
                if nxt:
                    hold(pool, c_st, g + 1)
                    pool.tensor_tensor(rstd[:, :], ve[:, :], half[:, 0:GT], ALU.pow).then_inc(c_rstd.sem, 1)
                    if this and more:
                        gather(g + 2, 2, 6)
                if more:
                    gather(g + 2, 6 if this else 0, 2 * GT)
                if this:
                    subtract(g, 3)
                if prev:
                    hold(pool, f_u, g - 1, 0)
                    pool.tensor_copy(ohx[:, :, :].rearrange("e t (b s) -> e (t b) s", s=S),
                                     bc(ohC[:, bass.ds((g - 1) * GB, GB)], S)).then_inc(f_oh.sem, 1)
                if nxt:
                    subtract(g + 1, 0)
                if prev:
                    hold(pool, o_st, g - 1)
                    pool.tensor_tensor(rstd3[:, :], ve3[:, :], half[:, 0:GT], ALU.pow).then_inc(o_rstd.sem, 1)

            pipeline(pool, iteration)

        @block.scalar
        def _(act):
            n = [0]

            def step(ins):
                n[0] += 1
                ins.then_inc(act_set, 1)

            for sig in (a_row, e_in, e_relu):
                sig.open(act)
            act.wait_ge(ld_first, 16 * N_FIRST)
            def deviation(g):
                hold(act, a_st, g)
                act.activation(rstd[:, :], ve[:, :], ACT.Sqrt).then_inc(a_sqrt.sem, 1)

            def affine(g, c):
                hold(act, a_T, g)
                act.activation(hA[c], W[3][:, :], ACT.Identity, bias=ln_gb[:, 1:2], scale=ln_gb[:, 0:1]).then_inc(a_h.sem, 1)

            def squares(g, c):
                hold(act, a_dve, g, 2)
                act.activation(big[:, 0, :], hA[c], ACT.Square).then_inc(a_sq.sem, 1)

            def deviation_over_time(g):
                hold(act, a_dve, g, 4)
                act.activation(vs[:, 2, :], vs[:, 1, :], ACT.Sqrt).then_inc(a_rv.sem, 1)

            def copy_rows(g, c):
                hold(act, a_rT, g)
                hold(act, slot_free, g - 2)
                act.activation(hrow[:, c, :, :].rearrange("p (b t) n -> p b t n", b=2), rows_lg[:, :, :, :], ACT.Copy).then_inc(a_row.sem, 1)

            act.wait_ge(pe_set, E_HYP1)
            step(act.activation(gammaT[:, :], W[0][:, 0:B], ACT.Relu, bias=hb[:, 0:1]))
            deviation(0)
            act.wait_ge(pe_set, E_HYP2)
            step(act.activation(betaT[:, :], W[1][:, 0:B], ACT.Identity, bias=hb[:, 1:2]))
            act.wait_ge(pe_set, E_STY1)
            step(act.activation(idf[0:SQ, :], W[0][0:SQ, 0:B], ACT.Relu, bias=hb[0:SQ, 2:3]))
            act.wait_ge(pe_set, E_STY2)
            step(act.activation(betaT[:, :], W[2][:, 0:B], ACT.Identity, bias=hb[:, 4:5]))
            step(act.activation(gammaT[:, :], W[1][:, 0:B], ACT.Identity, bias=hb[:, 3:4]))
            act.wait_ge(act_set, 5)
            step(act.activation(sD[:, :], gammaT[:, :], ACT.Abs))
            affine(0, 0)
            squares(0, 0)
            act.wait_ge(act_set, 6)
            step(act.activation(sD[:, :], sD[:, :], ACT.Exp, scale=-1.0))
            act.wait_ge(act_set, 7)
            step(act.activation(sD[:, :], sD[:, :], ACT.Ln, bias=1.0))
            assert n[0] == A_SET, n[0]
            deviation(1)
            deviation_over_time(0)
            affine(1, 1)
            with act.Fori(0, (NG - 2) // 2) as i:
                for c in range(2):
                    g = i * 2 + c
                    squares(g + 1, 1 - c)
                    copy_rows(g, c)
                    deviation(g + 2)
                    deviation_over_time(g + 1)
                    affine(g + 2, c)
            squares(NG - 1, (NG - 1) % 2)
            copy_rows(NG - 2, (NG - 2) % 2)
            deviation_over_time(NG - 1)
            act.wait_ge(pool_set, P_TAB)
            step(act.activation(sB[:, :], sA[:, :], ACT.Sin))
            step(act.activation(trk[:, :, :], tr[:, :, :], ACT.Sin))
            act.wait_ge(act_set, A_SET + 2)
            step(act.activation(sC[:, :], sB[:, :], ACT.Tanh, scale=0.5))
            copy_rows(NG - 1, (NG - 1) % 2)
            act.wait_ge(gate_dve, 1)
            act.activation(g2[:, :], m2[:, :], ACT.Exp).then_inc(gate_act, 1)

            def step(place, ahead, first, middle, last):
                if ahead:
                    hold(act, e_T, place.at(1))
                    hold(act, e_h, place.at(-1))
                    act.activation(tile_inT[:, place.slot(1) % 2, :], PS[:, 2 + place.slot(1) % 2, 0:P], ACT.Copy).then_inc(e_in.sem, 1)
                if middle:
                    hold(act, e_add, place.at(-1))
                    hd = hid[:, 0, 2 + place.slot(-1) % 2, :]
                    act.activation(hd, hd, ACT.Relu).then_inc(e_relu.sem, 1)
            tile_pipeline(act, step)
            act.wait_ge(vb_ones, 2)

            def iteration(g, p, prev, this, nxt, more):
                def copy_pT(s):
                    hold(act, c_pT, g, s + 1)
                    read(act.activation(PT[:, :, :].rearrange("p j q -> p (j q)"), bank(f"P{s}")[:, :], ACT.Copy), f"P{s}")

                def copy_v(g, s):
                    hold(act, c_v, g, s + 1)
                    read(act.activation(VB[:, s % 2, :, :, 0:HP * HD], bank(f"V{s}")[:, :].rearrange("p (b j v) -> p b j v", b=BT, j=HJ), ACT.Copy), f"V{s}")

                def exps(g, s):
                    hold(act, c_sub, g, s + 1)
                    act.activation(Sc[:, s % 2, :, :], Sc[:, s % 2, :, :], ACT.Exp).then_inc(c_exp.sem, 1)

                def gelu(c):
                    hold(act, d_f, g - 1, c + 1)
                    read(act.activation(hid[:, 0, c, :], bank(f"F{c}")[:, :], ACT.Gelu_apprx_sigmoid, bias=b1[:, c:c + 1]), f"F{c}")

                if prev:
                    hold(act, d_cT, g - 1)
                    read(act.activation(ctxT[:, :], bank("CT")[:, :], ACT.Identity, bias=cols[:, 2:3]), "CT")
                if this:
                    copy_pT(0)
                    copy_v(g, 1)
                    exps(g, 1)
                    copy_pT(1)
                    copy_v(g, 2)
                if prev:
                    hold(act, t2, g - 1)
                    read(act.activation(h2T[:, :], bank("T2")[:, :], ACT.Identity, bias=cols[:, 4:5], scale=cols[:, 3:4]), "T2")
                if this:
                    exps(g, 2)
                if prev:
                    for c in range(FC):
                        gelu(c)
                if this:
                    copy_pT(2)
                    copy_v(g, 3)
                    exps(g, 3)
                if nxt:
                    hold(act, qp, g + 1)
                    read(act.activation(QT[:, :], bank("Q")[:, :], ACT.Identity, bias=bqs[:, :], scale=HD ** -0.5), "Q")
                    hold(act, kp, g + 1)
                    for h in range(HP):
                        ins = act.activation(KM[:, :, h, :], bank("K")[:, :].rearrange("d (b s) -> d b s", s=S), ACT.Identity,
                                             bias=bkm[:, h:h + 1], scale=hm4[:, h:h + 1])
                    read(ins, "K")
                if this:
                    copy_pT(3)
                if prev:
                    hold(act, t3, g - 1)
                    read(act.activation(X3T[:, :], bank("T3")[:, :], ACT.Copy), "T3")
                    hold(act, dp, g - 1)
                    for b in range(BT):
                        ins = act.activation(hBD[S * b:S * b + S, 0, :, S * b:S * b + S],
                                             bank("D")[S * b:S * b + S, :].rearrange("p (t q) -> p t q", q=P)[:, :, S * b:S * b + S],
                                             ACT.Gelu, bias=cols[S * b:S * b + S, 5:6])
                    read(ins, "D")
                if nxt:
                    copy_v(g + 1, 0)
                    exps(g + 1, 0)

            pipeline(act, iteration)

        @block.vector
        def _(dve):
            n = [0]

            def step(ins):
                n[0] += 1
                ins.then_inc(dve_set, 1)
                dve.wait_ge(dve_set, n[0])

            for sig in (placed, e_hc, e_add, e_yc, r_x, c_sc):
                sig.open(dve)
            for done in tile_st:
                dve.sem_inc(done, 16)
            dve.wait_ge(ld_first, 16 * N_FIRST)
            dve.wait_ge(pool_set, P_SET)
            step(dve.tensor_copy(dsf[:, :], desc[:, :]))
            step(dve.tensor_copy(seq[:, :], seqi[:, :]))
            step(dve.tensor_copy(regf[:, :], regi[:, :]))
            step(dve.tensor_copy(base[:, :], regi[:, :]))
            step(dve.tensor_copy(idf[0:NS, :], ids[0:NS, :]))
            step(dve.tensor_scalar(onehot[:, :], idf[0:NS, :], iof[0:NS, :], None, ALU.is_equal))
            assert n[0] == D_ONEHOT, n[0]
            dve.wait_ge(pe_set, E_SE)
            step(dve.tensor_copy(sD[0:SE, :], W[3][0:SE, 0:B]))
            def stats(src, sig, g, st=st, mv=mv, ve=ve):
                for s in range(GT):
                    dve.bn_stats(st[:, s, :], src(s)).then_inc(sig.sem, 1)
                hold_apart(dve, sig, g, GT)
                for s in range(GT):
                    dve.bn_aggr(mv[:, s, :], st[:, s, :]).then_inc(sig.sem, 1)
                hold_apart(dve, sig, g, 2 * GT)
                dve.tensor_scalar(ve[:, :], mv[:, :, 1], 1e-5, None, ALU.add).then_inc(sig.sem, 1)

            def normalise(dst, src, sig, g, mv=mv, rstd=rstd):
                for s in range(GT):
                    dve.tensor_scalar(dst(s), src(s), mv[:, s, 0:1], rstd[:, s:s + 1], ALU.subtract, ALU.mult).then_inc(sig.sem, 1)

            def tile_of(g, s):
                return X[:, bass.ds(g * GT + s, 1), :].rearrange("p o d -> p (o d)")

            dve.wait_ge(ld_x, 16)
            def measured(g):
                stats(lambda s: tile_of(g, s), a_st, g)

            def normalised(g):
                hold(dve, a_sqrt, g)
                dve.reciprocal(rstd[:, :], rstd[:, :]).then_inc(a_rstd.sem, 1)
                hold(dve, a_rstd, g)
                hold(dve, a_T, g - 1)
                normalise(lambda s: xn[:, s, :], lambda s: tile_of(g, s), a_xn, g)

            seg = [h.rearrange("d (b s) -> d b s", s=S) for h in hA]

            def centre(g, c):
                hold(dve, a_h, g)
                dve.tensor_reduce(out=vs[:, 0, :], in_=seg[c], axis=AX.X, op=ALU.add).then_inc(a_dve.sem, 1)
                hold(dve, a_dve, g, 1)
                dve.scalar_tensor_tensor(out=seg[c], in0=bc(vs[:, 0, :], S), scalar=-1.0 / S, in1=seg[c], op0=ALU.mult, op1=ALU.add).then_inc(a_dve.sem, 1)

            def variance(g):
                hold(dve, a_sq, g)
                dve.tensor_reduce(out=vs[:, 1, :], in_=big[:, 0, :].rearrange("d (b s) -> d b s", s=S), axis=AX.X, op=ALU.add).then_inc(a_dve.sem, 1)
                hold(dve, a_dve, g, 3)
                dve.tensor_scalar(vs[:, 1, :], vs[:, 1, :], 1.0 / S, 1e-8, ALU.mult, ALU.add).then_inc(a_dve.sem, 1)

            def styled(g, c):
                hold(dve, a_rv, g)
                dve.reciprocal(vs[:, 3, :], vs[:, 2, :]).then_inc(a_dve.sem, 1)
                hold(dve, a_dve, g, 5)
                dve.tensor_tensor(vs[:, 3, :], vs[:, 3, :], gammaT[:, bass.ds(g * GB, GB)], ALU.mult).then_inc(a_dve.sem, 1)
                hold(dve, a_dve, g, 6)
                dve.tensor_tensor(seg[c], seg[c], bc(vs[:, 3, :], S), ALU.mult).then_inc(a_dve.sem, 1)
                hold(dve, a_dve, g, 7)
                hold(dve, a_rT, g - 1)
                dve.tensor_tensor(hTw[:, 0, :].rearrange("d (b s) -> d b s", s=S), seg[c], bc(betaT[:, bass.ds(g * GB, GB)], S), ALU.add).then_inc(a_dve.sem, 1)

            def pick(g, k, ins):
                ins.then_inc(best.sem, 1)
                dve.wait_ge(best.sem, best.upto(g, k))

            def choose(g, k, m, which):
                mval = m[:, bass.ds(g * GT, GT)]
                pick(g, k, dve.tensor_reduce(out=mval, in_=Lg, axis=AX.X, op=ALU.max))
                pick(g, k + 1, dve.tensor_tensor(ta, Lg, bc(mval, NE), ALU.is_equal))
                pick(g, k + 2, dve.tensor_tensor(ta, ta, dsf[:, :].unsqueeze(1).broadcast_to([P, GT, NE]), ALU.mult))
                pick(g, k + 3, dve.tensor_reduce(out=mw[:, :], in_=ta, axis=AX.X, op=ALU.max))
                pick(g, k + 4, dve.tensor_tensor(sel[:, which, bass.ds(g * GT, GT), :], ta, bc(mw[:, :], NE), ALU.is_equal))

            def best_two(g, c):
                hold(dve, a_row, g)
                pick(g, 1, dve.tensor_copy(Lg, hrow[:, c, :, P:P + NE]))
                choose(g, 2, m1, 0)
                pick(g, 7, dve.scalar_tensor_tensor(out=Lg, in0=sel[:, 0, bass.ds(g * GT, GT), :], scalar=MASKED, in1=Lg, op0=ALU.mult, op1=ALU.add))
                choose(g, 8, m2, 1)
                pick(g, 13, dve.tensor_tensor(both[:, 0:GT, :], sel[:, 0, bass.ds(g * GT, GT), :], sel[:, 1, bass.ds(g * GT, GT), :], ALU.add))

            def place_rows(g, c):
                hold(dve, a_pos, g)
                dve.tensor_tensor(pf, PS[:, 0, 0:GT * NE].rearrange("p (t e) -> p t e", e=NE), base[:, :].unsqueeze(1).broadcast_to([P, GT, NE]), ALU.add).then_inc(placed.sem, 1)
                dve.wait_ge(placed.sem, placed.upto(g, 1))
                dve.tensor_tensor(picked, sel[:, :, bass.ds(g * GT, GT), :], pf.unsqueeze(1).broadcast_to([P, 2, GT, NE]), ALU.mult).then_inc(placed.sem, 1)
                dve.tensor_tensor(base[:, :], PS[:, 0, GT * NE:(GT + 1) * NE], base[:, :], ALU.add).then_inc(placed.sem, 1)
                dve.wait_ge(placed.sem, placed.upto(g, 3))
                dve.tensor_reduce(out=posf[:, :, bass.ds(g * GT, GT)], in_=picked, axis=AX.X, op=ALU.add).then_inc(placed.sem, 1)
                dve.wait_ge(placed.sem, placed.upto(g, 4))
                hold(dve, slot_free, g - 2)
                dve.sem_inc(passed["DVE"])
                dve.tensor_copy(pos_g[:, c, :, :], posf[:, :, bass.ds(g * GT, GT)]).then_inc(idx_ready.sem, 1)

            measured(0)
            normalised(0)
            centre(0, 0)
            measured(1)
            variance(0)
            dve.wait_ge(act_set, A_SET)
            step(dve.scalar_tensor_tensor(out=gammaT[:, :], in0=gammaT[:, :], scalar=0.0, in1=sD[:, :], op0=ALU.max, op1=ALU.add))
            step(dve.tensor_scalar(gammaT[:, :], gammaT[:, :], 1e-8, None, ALU.add))
            assert n[0] == D_STYLE, n[0]
            normalised(1)
            styled(0, 0)
            with dve.Fori(0, (NG - 2) // 2) as i:
                for c in range(2):
                    g = i * 2 + c
                    centre(g + 1, 1 - c)
                    measured(g + 2)
                    best_two(g, c)
                    variance(g + 1)
                    normalised(g + 2)
                    place_rows(g, c)
                    styled(g + 1, 1 - c)
            centre(NG - 1, 1)
            best_two(NG - 2, 0)
            variance(NG - 1)
            place_rows(NG - 2, 0)
            dve.wait_ge(pe_set, E_DT)
            step(dve.tensor_copy(dwT[:, :, :], W[0][:, 0:A].unsqueeze(1).broadcast_to([P, 4, A])))
            step(dve.tensor_copy(upT[:, :], W[1][0:A, 0:D]))
            assert n[0] == D_UPT, n[0]
            styled(NG - 1, 1)
            best_two(NG - 1, 1)
            place_rows(NG - 1, 1)

            k = [0]

            def then(ins):
                k[0] += 1
                ins.then_inc(listed_dve, 1)
                dve.wait_ge(listed_dve, k[0])

            dve.tensor_copy(pads[:, :], base[:, :]).then_inc(pads_ready, 1)
            then(dve.tensor_tensor(tiles[:, :], base[:, :], regf[:, :], ALU.subtract))
            then(dve.tensor_scalar(tiles[:, :], tiles[:, :], 1.0 / P, (P - 1) / (2.0 * P), ALU.mult, ALU.add))
            then(dve.tensor_scalar(tiles[:, :], tiles[:, :], ROUND, -ROUND, ALU.add, ALU.add))
            then(dve.tensor_copy(ends[:, 0:1], tiles[:, 0:1]))
            for e in range(1, NE):
                then(dve.tensor_tensor(ends[:, e:e + 1], ends[:, e - 1:e], tiles[:, e:e + 1], ALU.add))
            then(dve.tensor_scalar(jump[:, :], tiles[:, :], -float(P), float(REGION), ALU.mult, ALU.add))
            then(dve.tensor_tensor(passed_end, bc(seq[:, :], NE), ends[:, :].unsqueeze(1).broadcast_to([P, LIST, NE]), ALU.is_ge))
            then(dve.tensor_reduce(out=listf, in_=passed_end, axis=AX.X, op=ALU.add))
            then(dve.tensor_tensor(passed_end, passed_end, jump[:, :].unsqueeze(1).broadcast_to([P, LIST, NE]), ALU.mult))
            then(dve.tensor_reduce(out=rowf, in_=passed_end, axis=AX.X, op=ALU.add))
            then(dve.scalar_tensor_tensor(out=rowf, in0=seq[:, :], scalar=float(P), in1=rowf, op0=ALU.mult, op1=ALU.add))
            dve.tensor_copy(row_at[:, :], rowf).then_inc(listed, 1)
            dve.wait_ge(act_set, A_SET + 3)
            step(dve.scalar_tensor_tensor(out=sC[:, :], in0=sC[:, :], scalar=1.0, in1=sB[:, :], op0=ALU.add, op1=ALU.mult))
            step(dve.tensor_scalar(sC[:, :], sC[:, :], 0.5, None, ALU.mult))
            assert n[0] == D_SILU, n[0]
            then(dve.tensor_tensor(m2[:, :], m2[:, :], m1[:, :], ALU.subtract))
            dve.sem_inc(gate_dve, 1)
            dve.wait_ge(pe_set, E_WU)
            step(dve.tensor_copy(wus[:, :, :].rearrange("p c d -> p (c d)"), W[0][:, :]))
            dve.wait_ge(pe_set, E_CT)
            step(dve.tensor_tensor(CT[:, :], W[1][0:NX + 2, 0:D], upb[:, :], ALU.add))
            assert n[0] == D_WUS, n[0]
            then(dve.tensor_scalar(listf, listf, float(NE - 1), None, ALU.min))
            then(dve.tensor_copy(expert_at[:, :], listf))
            then(dve.memset(pairf, 0.0))
            then(dve.tensor_scalar(pairf[:, 0:LIST], listf, float(NE), None, ALU.mult))
            then(dve.tensor_tensor(pairf[:, 3:LIST + 3], pairf[:, 3:LIST + 3], listf, ALU.add))
            then(dve.tensor_copy(pair_at[:, :], pairf))
            quad = pairf[:, 3:LIST].rearrange("p (j q) -> p j q", q=4)
            for q in range(1, 4):
                then(dve.scalar_tensor_tensor(out=quad[:, :, 0], in0=quad[:, :, q], scalar=float(NE ** (2 * q)), in1=quad[:, :, 0], op0=ALU.mult, op1=ALU.add))
            dve.tensor_copy(eight_at[:, :], quad[:, :, 0]).then_inc(paired, 1)
            then(dve.tensor_tensor(ends[:, :], ends[:, :], tiles[:, :], ALU.subtract))
            then(dve.scalar_tensor_tensor(out=ends[:, :], in0=ends[:, :], scalar=float(P), in1=regf[:, :], op0=ALU.mult, op1=ALU.subtract))
            then(dve.tensor_tensor(moves, sel, ends[:, :].unsqueeze(1).unsqueeze(1).broadcast_to([P, 2, NT, NE]), ALU.mult))
            then(dve.tensor_reduce(out=moved[:, :, :], in_=moves, axis=AX.X, op=ALU.add))
            then(dve.tensor_tensor(moved[:, :, :], moved[:, :, :], posf[:, :, :], ALU.add))
            then(dve.tensor_copy(pos[:, :, :], moved[:, :, :]))
            dve.wait_ge(gate_act, 1)
            then(dve.tensor_scalar(g1[:, :], g2[:, :], 1.0, None, ALU.add))
            then(dve.reciprocal(g1[:, :], g1[:, :]))
            then(dve.tensor_tensor(g2[:, :], g2[:, :], g1[:, :], ALU.mult))
            dve.wait_ge(pool_set, P_TAB)
            dve.wait_ge(pe_set, E_ADA)
            step(dve.tensor_scalar(scaleT[:, :], W[2][:, 0:B], bada[:, 0:1], 1.0, ALU.add, ALU.add))
            step(dve.tensor_scalar(shiftT[:, :], W[2][:, B:2 * B], bada[:, 1:2], None, ALU.add))
            dve.wait_ge(pe_set, E_ROT)
            rot = W[3][:, 0:5 * NT].rearrange("p (k t) -> p k t", k=5)
            for k, (dst, src, sign) in enumerate(((S4, 0, 1), (S4, 0, -1), (S4, 2, 1), (S4, 2, -1), (C4, 1, 1), (C4, 1, 1), (C4, 3, 1), (C4, 3, 1))):
                step(dve.tensor_scalar(dst[:, :, k % 4], rot[:, src, :], float(sign), None, ALU.mult))
            step(dve.tensor_copy(domx[:, :], rot[:, 4, :]))
            step(dve.tensor_scalar(domy[:, :], domx[:, :], 0.0, None, ALU.is_ge))
            step(dve.scalar_tensor_tensor(out=domy[:, :], in0=domx[:, :], scalar=float(NX), in1=domy[:, :], op0=ALU.is_lt, op1=ALU.mult))
            step(dve.scalar_tensor_tensor(out=domx[:, :], in0=domx[:, :], scalar=-float(NX), in1=domy[:, :], op0=ALU.add, op1=ALU.mult))
            step(dve.tensor_scalar(domx[:, :], domx[:, :], float(NX), float(A), ALU.add, ALU.mult))
            step(dve.tensor_scalar(widx[:, :], domx[:, :], acf[:, :], None, ALU.add))
            assert n[0] == D_WIDX, n[0]
            dve.wait_ge(ld_exp_b, 32)

            def step(place, ahead, first, middle, last):
                if first:
                    c = place.slot(0) % 2
                    hold(dve, e_h, place.at(0))
                    hold(dve, e_hT, place.at(-2))
                    dve.tensor_copy(hid[:, 0, c, :], W[c][:, :]).then_inc(e_hc.sem, 1)
                if middle:
                    c = place.slot(-1) % 2
                    expert = dve.value_load(expert_at[0:1, bass.ds(place.at(-1), 1)], min_val=0, max_val=NE - 1)
                    hold(dve, e_hT, place.at(-1))
                    hold_apart(dve, e_y, place.at(-3))
                    dve.tensor_tensor(hid[:, 0, 2 + c, :].rearrange("p (c n) -> p c n", c=FC), PS[:, c, :].rearrange("p (c n) -> p c n", c=FC),
                                      bc(B1E[:, bass.ds(expert, 1), :].rearrange("p o c -> p (o c)"), P), ALU.add).then_inc(e_add.sem, 1)
                if last:
                    c = place.slot(-2)
                    expert = dve.value_load(expert_at[0:1, bass.ds(place.at(-2), 1)], min_val=0, max_val=NE - 1)
                    hold(dve, e_y, place.at(-2))
                    dve.wait_ge(tile_st[c], place.round(-2) * 16 + 16)
                    dve.sem_inc(passed["DVE"])
                    dve.tensor_tensor(tile_out[:, c, :], W[2 + c % 2][:, 0:P], B2E[:, bass.ds(expert, 1), :].rearrange("p o d -> p (o d)"), ALU.add).then_inc(e_yc.sem, 1)

            tile_pipeline(dve, step)
            hold(dve, e_y, LIST - 1)

            def add_expert(g, k):
                hold(dve, y_ld[k], g)
                if k:
                    hold(dve, y_add, g, 1)
                for s in range(GT):
                    ins = dve.scalar_tensor_tensor(out=tile_of(g, s), in0=Y[:, k, s, :], scalar=(g1, g2)[k][:, bass.ds(g * GT + s, 1)],
                                                   in1=tile_of(g, s), op0=ALU.mult, op1=ALU.add)
                ins.then_inc(y_add.sem, 1)

            def next_rows(g):
                dve.tensor_copy(pos_g[:, 0, :, :], pos[:, :, bass.ds(g * GT, GT)]).then_inc(y_idx.sem, 1)

            def experts_of_next(g):
                for k in range(2):
                    add_expert(g + 2, k)

            def rows_of_next(g):
                if not (isinstance(g, int) and g == NG - 3):
                    hold(dve, y_add, g + 2)
                    dve.sem_inc(passed["DVE"])
                    next_rows(g + 3)

            next_rows(0)
            for k in range(2):
                add_expert(0, k)
            hold(dve, y_add, 0)
            dve.sem_inc(passed["DVE"])
            next_rows(1)
            hold(dve, bias_masked, NG - 1)

            def iteration(g, p, prev, this, nxt, more):
                def scores(g, s):
                    hold(dve, c_qk, g, s + 1)
                    sc = Sc[:, s % 2, :, :]
                    dve.tensor_tensor(sc.rearrange("p (j h) k -> p j (h k)", j=HJ), PS[:, :, 0:P],
                                      BIAS[:, bass.ds(g * GT + s, 1), :, :].rearrange("p o (j h) k -> p (o j) (h k)", j=HJ), ALU.add).then_inc(c_sc.sem, 1)
                    hold(dve, c_sc, g, s + 1)
                    dve.tensor_reduce(out=mx[:, s % 2, :], in_=sc, axis=AX.X, op=ALU.max).then_inc(c_mx.sem, 1)

                def context(s):
                    hold(dve, c_pv, g, s + 1)
                    cv = bank(f"C{s}")[:, 0:HJ * GV].rearrange("p (j v) -> p j v", j=HJ)
                    dve.reciprocal(rs[:, :, :], cv[:, :, HP * HD:GV]).then_inc(c_rs.sem, 1)
                    hold(dve, c_rs, g, s + 1)
                    read(dve.tensor_tensor(Cn[:, s, :].rearrange("p (j h v) -> p j h v", j=HJ, h=HP),
                                           cv[:, :, 0:HP * HD].rearrange("p j (h v) -> p j h v", h=HP), bc(rs[:, :, :], HD), ALU.mult), f"C{s}")

                if this:
                    scores(g, 1)
                if prev:
                    hold(dve, d_o, g - 1)
                    read(dve.tensor_tensor(x2[:, :, :], bank("O")[:, :].rearrange("p (t d) -> p t d", d=D), rows[:, 0:1, :].broadcast_to([P, GT, D]), ALU.add), "O")
                    was_read(dve, "O", g)
                    stats(lambda s: x2[:, s, :], d_st, g - 1, st2, mv2, ve2)
                if prev:
                    hold(dve, d_rstd, g - 1)
                    normalise(lambda s: xn2[:, s, :], lambda s: x2[:, s, :], d_xn, g - 1, mv2, rstd2)
                if this:
                    context(0)
                if nxt:
                    for s in range(GT):
                        hold(dve, r_swp, g + 1, s + 1)
                        xt = X[:, bass.ds((g + 1) * GT + s, 1), :].rearrange("p o (w f) -> p (o w) f", f=4)
                        dve.tensor_tensor(xt, xt, C4[:, bass.ds((g + 1) * GT + s, 1), :].broadcast_to([P, D // 4, 4]), ALU.mult).then_inc(r_mul.sem, 1)
                    for s in range(GT):
                        hold(dve, r_mul, g + 1, s + 1)
                        dve.tensor_tensor(tile_of(g + 1, s), tile_of(g + 1, s), big[:, 0, s * D:(s + 1) * D], ALU.add).then_inc(r_x.sem, 1)
                if this:
                    scores(g, 2)
                if nxt:
                    hold_apart(dve, r_x, g + 1)
                    stats(lambda s: tile_of(g + 1, s), c_st, g + 1)
                if this:
                    context(1)
                if nxt:
                    hold(dve, c_rstd, g + 1)
                    normalise(lambda s: xn[:, s, :], lambda s: tile_of(g + 1, s), c_xn, g + 1)
                    hold(dve, t1, g + 1)
                    read(dve.tensor_tensor(big[:, 1, :].rearrange("d (b s) -> d b s", s=S), bank("T1")[:, :].rearrange("d (b s) -> d b s", s=S),
                                           bc(scaleT[:, bass.ds((g + 1) * GB, GB)], S), ALU.mult), "T1")
                    was_read(dve, "T1", g)
                    dve.tensor_tensor(xmT[:, 1 - p, :].rearrange("d (b s) -> d b s", s=S), big[:, 1, :].rearrange("d (b s) -> d b s", s=S),
                                      bc(shiftT[:, bass.ds((g + 1) * GB, GB)], S), ALU.add).then_inc(c_xm.sem, 1)
                if this:
                    scores(g, 3)
                    context(2)
                if this and more:
                    experts_of_next(g)
                if prev:
                    hold(dve, d_y, g - 1)
                    hold(dve, d_x2b, g - 1)
                    read(dve.tensor_tensor(X3[:, :, :].rearrange("p t d -> p (t d)"), bank("Y")[:, :], x2b[:, :, :].rearrange("p t d -> p (t d)"), ALU.add), "Y")
                if this and more:
                    rows_of_next(g)
                if this:
                    context(3)
                if nxt:
                    scores(g + 1, 0)
                if more and not this:
                    experts_of_next(g)
                    rows_of_next(g)
                if prev:
                    hold(dve, f_u, g - 1)
                    was_read(dve, "Y", g)
                    read(dve.tensor_tensor(z[:, :, :].rearrange("p t d -> p (t d)"), bank("U")[:, :], X3[:, :, :].rearrange("p t d -> p (t d)"), ALU.add), "U")
                    was_read(dve, "U", g)
                    stats(lambda s: z[:, s, :], o_st, g - 1, st3, mv3, ve3)
                    for s in range(GT):
                        dve.scalar_tensor_tensor(out=z[:, s, :], in0=z[:, s, :], scalar=mv3[:, s, 0:1], in1=rows[:, 2, :],
                                                 op0=ALU.subtract, op1=ALU.mult).then_inc(o_zn.sem, 1)
                    hold(dve, o_rstd, g - 1)
                    dve.wait_ge(out_done[1 - p], (g - 1 - (1 - p)) * 8 + 16)
                    for s in range(GT):
                        hold(dve, o_zn, g - 1, s + 1)
                        ins = dve.scalar_tensor_tensor(out=ot[:, 1 - p, s, :], in0=z[:, s, :], scalar=rstd3[:, s:s + 1], in1=rows[:, 3, :],
                                                       op0=ALU.mult, op1=ALU.add)
                    ins.then_inc(o_b.sem, 1)

            pipeline(dve, iteration)

        @block.tensor
        def _(pe):
            n = [0]

            def mark(ins, at):
                n[0] += 1
                ins.then_inc(pe_set, 1)
                assert n[0] == at, (n[0], at)

            for sig in (a_T, a_rT, e_T, e_h, e_hT, e_y, f_u):
                sig.open(pe)
            pe.wait_ge(ld_first, 16 * N_FIRST)
            pe.wait_ge(pool_set, P_SET)
            pe.wait_ge(dve_set, D_ONEHOT)
            mark(pe.matmul(W[3][0:SE, 0:B], embw[:, :], onehot[:, :], start=True, stop=True), E_SE)
            pe.wait_ge(dve_set, D_ONEHOT + 1)
            mark(pe.matmul(W[0][:, 0:B], hypw1[:, :], sD[0:SE, :], start=True, stop=True), E_HYP1)
            pe.wait_ge(act_set, 1)
            mark(pe.matmul(W[1][:, 0:B], hypw2[:, :], gammaT[:, :], start=True, stop=True), E_HYP2)
            pe.wait_ge(act_set, 2)
            mark(pe.matmul(W[0][0:SQ, 0:B], styw1[:, :], betaT[:, :], start=True, stop=True), E_STY1)
            pe.wait_ge(act_set, 3)
            pe.matmul(W[1][:, 0:B], styw2[:, 0:D], idf[0:SQ, :], start=True, stop=True)
            mark(pe.matmul(W[2][:, 0:B], styw2[:, D:2 * D], idf[0:SQ, :], start=True, stop=True), E_STY2)
            def normalised(g):
                for s in range(GT):
                    hold(pe, a_xn, g, s + 1)
                    ins = pe.transpose(W[3][:, s * P:(s + 1) * P], xn[:, s, :], ident[:, :])
                ins.then_inc(a_T.sem, 1)

            def styled(g):
                hold(pe, a_dve, g)
                hold(pe, a_row, g - 1)
                for s in range(GT):
                    ins = pe.matmul(rows_lg[:, s // 2, s % 2, :], hTw[:, 0, s * P:(s + 1) * P], ident_rw[:, :], start=True, stop=True)
                ins.then_inc(a_rT.sem, 1)

            def count(g):
                hold(pe, best, g)
                hold(pe, placed, g, 0)
                pe.sem_inc(passed["PE"])
                counts = PS[:, 0, 0:(GT + 1) * NE].rearrange("p (t e) -> p t e", e=NE)
                pe.matmul(counts, upper[:, :], both[:, :, :], start=True, stop=False)
                for r in range(GT):
                    ins = pe.matmul(counts[:, r + 1:GT + 1, :], ones[:, :], both[:, r:r + 1, :].broadcast_to([P, GT - r, NE]), start=False, stop=(r == GT - 1))
                ins.then_inc(a_pos.sem, 1)

            normalised(0)
            normalised(1)
            pe.wait_ge(act_set, A_SET)
            styled(0)
            with pe.Fori(0, (NG - 2) // 2) as i:
                for c in range(2):
                    g = i * 2 + c
                    count(g)
                    normalised(g + 2)
                    styled(g + 1)
            count(NG - 2)
            pe.wait_ge(ld_rest, 16 * (N_REST - N_ANGLES))
            pe.wait_ge(pool_set, P_TAB)
            pe.transpose(W[0][:, 0:A], doww[:, :], ident[0:A, 0:A])
            mark(pe.transpose(W[1][0:A, 0:D], upw[:, :], ident[:, :]), E_DT)
            styled(NG - 1)
            pe.wait_ge(dve_set, D_UPT)
            for c in range(NX // 4):
                ins = pe.matmul(W[0][:, c * D:(c + 1) * D], exw[:, 4 * c:4 * c + 4, :].rearrange("o e a -> o (e a)"), upT[:, :], start=True, stop=True)
            mark(ins, E_WU)
            mark(pe.matmul(W[1][0:NX + 2, 0:D], vecs[:, :], upT[:, :], start=True, stop=True), E_CT)
            pe.wait_ge(act_set, A_SET + 2)
            pe.matmul(W[3][:, 0:4 * NT], e4[:, :], trk[:, :, :].rearrange("b k t -> b (k t)"), start=True, stop=True)
            mark(pe.matmul(W[3][:, 4 * NT:5 * NT], e4[:, :], dom4f[:, :], start=True, stop=True), E_ROT)
            count(NG - 1)
            pe.wait_ge(dve_set, D_SILU)
            pe.matmul(W[2][:, 0:B], wada[:, 0:D], sC[:, :], start=True, stop=True)
            mark(pe.matmul(W[2][:, B:2 * B], wada[:, D:2 * D], sC[:, :], start=True, stop=True), E_ADA)
            pe.wait_ge(dve_set, D_WUS)
            hold(pe, a_row, NG - 1)
            hold(pe, placed, NG - 1, 3)
            pe.wait_ge(ld_exp, 32)
            eight = [None]

            def step(place, ahead, first, middle, last):
                if isinstance(place.j, int):
                    two = pe.value_load(pair_at[0:1, place.at(1):place.at(2)], min_val=0, max_val=NE * NE - 1)
                else:
                    if place.q == 0:
                        eight[0] = pe.value_load(eight_at[0:1, bass.ds(place.j, 1)], min_val=0, max_val=NE ** 8 - 1)
                    two = eight[0] // NE ** (2 * place.q) % (NE * NE)
                first_expert, last_expert = two // NE, two % NE
                if ahead:
                    c = place.slot(1)
                    pe.wait_ge(tile_ld[c], place.round(1) * 16 + 16)
                    hold(pe, e_in, place.at(-1))
                    pe.transpose(PS[:, 2 + c % 2, 0:P], tile_in[:, c, :], ident[:, :]).then_inc(e_T.sem, 1)
                if middle:
                    c = place.slot(-1) % 2
                    hold(pe, e_add, place.at(-3))
                    hold(pe, e_hc, place.at(-1))
                    for k in range(FC):
                        ins = pe.transpose(PS[:, c, k * P:(k + 1) * P], hid[:, 0, c, k * P:(k + 1) * P], ident[:, :])
                    ins.then_inc(e_hT.sem, 1)
                if last:
                    c = place.slot(-2) % 2
                    hold(pe, e_yc, place.at(-4))
                    hold(pe, e_relu, place.at(-2))
                    pe.sem_inc(passed["PE"])
                    for k in range(FC):
                        ins = pe.matmul(W[2 + c][:, 0:P], hid[:, 0, 2 + c, k * P:(k + 1) * P], W2E[:, bass.ds(last_expert, 1), k, :].rearrange("p o d -> p (o d)"),
                                        start=(k == 0), stop=(k == FC - 1))
                    ins.then_inc(e_y.sem, 1)
                if ahead:
                    c = place.slot(1) % 2
                    hold(pe, e_hc, place.at(-1))
                    hold(pe, e_in, place.at(1))
                    pe.sem_inc(passed["PE"])
                    pe.matmul(W[c][:, :], tile_inT[:, c, :], W1E[:, bass.ds(first_expert, 1), :].rearrange("p o f -> p (o f)"), start=True, stop=True).then_inc(e_h.sem, 1)

            pe.wait_ge(paired, 1)
            tile_pipeline(pe, step)
            hold(pe, e_yc, LIST - 1)
            pe.wait_ge(ld_wsel, 16 * NT)
            pe.wait_ge(dve_set, D_WIDX)

            def iteration(g, p, prev, this, nxt, more):
                def transposed(name, src, ready, g_of, sig):
                    free(name, g)
                    for s in range(GT):
                        if ready is not None:
                            hold(pe, ready, g_of, s + 1)
                        ins = pe.transpose(bank(name)[:, s * P:(s + 1) * P], src[:, s, :], ident[:, :])
                    ins.then_inc(sig.sem, 1)

                def scores(g, s, par):
                    hold_apart(pe, c_sc, g, s)
                    for b in range(BT):
                        for j in range(HJ):
                            lo = s * P + b * S
                            ins = pe.matmul(PS[S * b:S * b + S, j, 0:P], QT[32 * j:32 * j + 32, lo:lo + S],
                                            KM[32 * j:32 * j + 32, s * BT + b, :, :].rearrange("d h k -> d (h k)"), start=True, stop=True)
                    ins.then_inc(c_qk.sem, 1)

                def values(it, g, s, par):
                    free(f"V{s}", it)
                    for b in range(BT):
                        lo = s * P + b * S
                        for h in range(HP):
                            ins = pe.matmul(bank(f"V{s}")[S * h:S * h + S, b * D:(b + 1) * D], xmT[:, par, lo:lo + S],
                                            wv4[:, h, :, :, :].rearrange("d j h v -> d (j h v)"), start=True, stop=True)
                    ins.then_inc(c_v.sem, 1)

                def transposed_probs(s):
                    hold(pe, c_exp, g, s + 1)
                    free(f"P{s}", g)
                    for j in range(HJ):
                        ins = pe.transpose(bank(f"P{s}")[:, j * P:(j + 1) * P], Sc[:, s % 2, j * HP:(j + 1) * HP, :].rearrange("p h k -> p (h k)"), ident[:, :])
                    ins.then_inc(c_pT.sem, 1)

                def context(s):
                    was_read(pe, f"P{s}", g)
                    free(f"C{s}", g)
                    for b in range(BT):
                        for j in range(HJ):
                            ins = pe.matmul(bank(f"C{s}")[S * b:S * b + S, j * GV:(j + 1) * GV], PT[:, j, b * S:b * S + S], VB[:, s % 2, b, j, :],
                                            start=True, stop=True)
                    ins.then_inc(c_pv.sem, 1)

                def up(c):
                    free(f"F{c}", g)
                    pe.matmul(bank(f"F{c}")[:, :], w1[:, c * P:(c + 1) * P], h2T[:, :], start=True, stop=True).then_inc(d_f.sem, 1)

                if prev:
                    was_read(pe, "C3", g - 1)
                    transposed("CT", Cn, None, None, d_cT)
                if this:
                    transposed_probs(0)
                if prev:
                    was_read(pe, "CT", g)
                    free("O", g)
                    for s in range(GT):
                        pe.matmul(bank("O")[:, s * D:(s + 1) * D], ctxT[:, s * P:(s + 1) * P], wo[:, :], start=True, stop=False)
                        ins = pe.matmul(bank("O")[:, s * D:(s + 1) * D], xmT[:, 1 - p, s * P:(s + 1) * P], ident[:, :], start=False, stop=True)
                    ins.then_inc(d_o.sem, 1)
                if this:
                    scores(g, 1, p)
                    values(g, g, 1, p)
                    context(0)
                    values(g, g, 2, p)
                    transposed_probs(1)
                    scores(g, 2, p)
                if prev:
                    transposed("T2", xn2, d_xn, g - 1, t2)
                if this:
                    context(1)
                if prev:
                    was_read(pe, "T2", g)
                    for c in range(FC - 1):
                        up(c)
                if this:
                    values(g, g, 3, p)
                if nxt:
                    transposed("T1", xn, c_xn, g + 1, t1)
                if prev:
                    up(FC - 1)
                if this:
                    transposed_probs(2)
                    scores(g, 3, p)
                    context(2)
                if nxt:
                    hold(pe, c_xm, g + 1)
                    free("Q", g)
                    pe.matmul(bank("Q")[:, :], wq[:, :], xmT[:, 1 - p, :], start=True, stop=True).then_inc(qp.sem, 1)
                    free("K", g)
                    pe.matmul(bank("K")[:, :], wk[:, :], xmT[:, 1 - p, :], start=True, stop=True).then_inc(kp.sem, 1)
                if prev:
                    for c in range(FC):
                        was_read(pe, f"F{c}", g)
                    free("Y", g)
                    for s in range(GT):
                        for c in range(FC):
                            ins = pe.matmul(bank("Y")[:, s * D:(s + 1) * D], hid[:, 0, c, s * P:(s + 1) * P], w2[:, c, :], start=(c == 0), stop=(c == FC - 1))
                    ins.then_inc(d_y.sem, 1)
                if this:
                    transposed_probs(3)
                if prev:
                    was_read(pe, "Y", g)
                    transposed("T3", X3, None, None, t3)
                if this:
                    context(3)
                if prev:
                    was_read(pe, "T3", g)
                    free("D", g)
                    pe.matmul(bank("D")[:, :], dwT[:, :, :].rearrange("d r a -> d (r a)"), X3T[:, :], start=True, stop=True).then_inc(dp.sem, 1)
                if nxt:
                    was_read(pe, "Q", g)
                    was_read(pe, "K", g)
                    pe.sem_inc(passed["PE"])
                    scores(g + 1, 0, 1 - p)
                    values(g, g + 1, 0, 1 - p)
                if prev:
                    was_read(pe, "D", g)
                    hold(pe, f_oh, g - 1)
                    free("U", g)
                    for s in range(GT):
                        pe.matmul(bank("U")[:, s * D:(s + 1) * D], hBD[:, 0, s, :], WSEL[:, bass.ds((g - 1) * GT + s, 1), :].rearrange("p o d -> p (o d)"), start=True, stop=False)
                        ins = pe.matmul(bank("U")[:, s * D:(s + 1) * D], ohx[:, s, :], CT[:, :], start=False, stop=True)
                    ins.then_inc(f_u.sem, 1)

            pipeline(pe, iteration)


N_FIRST = 13
N_REST = 35
N_ANGLES = 7
P_SET = 25
P_ANG = 72
P_TAB = 94
A_SET = 8
E_SE, E_HYP1, E_HYP2, E_STY1, E_STY2, E_DT, E_WU, E_CT, E_ROT, E_ADA = range(1, 11)
D_ONEHOT = 6
D_STYLE = 9
D_UPT = 11
D_SILU = 13
D_WUS = 15
D_WIDX = 31


def kernel(**inputs):
    import numpy as np
    import concourse.bacc as bacc
    from concourse.bass_utils import run_bass_kernel_spmd

    nc = bacc.Bacc("TRN2", target_bir_lowering=False, num_devices=1)
    arrays = {name: np.ascontiguousarray(v) for name, v in inputs.items()}
    half = 64
    f = np.exp(np.arange(half, dtype=np.float32) * np.float32(-np.log(10000.0) / (half - 1))).astype(np.float32)
    freqs = np.zeros((128, 3), np.float32)
    freqs[:, 0] = np.concatenate([f, f])
    freqs[half:, 1] = 0.25
    freqs[half:, 2] = np.pi / 2
    arrays["freqs"] = freqs
    aps = {}
    for name, v in arrays.items():
        aps[name] = nc.dram_tensor(name + "_dram", v.shape, mybir.dt.from_np(v.dtype), kind="ExternalInput").ap()
    shape = inputs["x"].shape
    out = nc.dram_tensor("out_dram", shape, F32, kind="ExternalOutput").ap()
    build(nc, aps, out)
    r = run_bass_kernel_spmd(nc, [{k + "_dram": v for k, v in arrays.items()}], core_ids=[0])
    return r.results[0]["out_dram"]
```
